# Optimizing a Trainium2 kernel written in Bass

```python
import numpy as np
import jax
import jax.numpy as jnp

def _softmax(x, axis=-1):
    return jax.nn.softmax(x, axis=axis)

def _gelu(x):
    return jax.nn.gelu(x, approximate=True)

def _silu(x):
    return jax.nn.silu(x)

def _sigmoid(x):
    return jax.nn.sigmoid(x)

def _layernorm(x, axis=-1, eps=1e-05):
    m = jnp.mean(x, axis=axis, keepdims=True)
    v = jnp.var(x, axis=axis, keepdims=True)
    return (x - m) / jnp.sqrt(v + eps)

def _scatter_add(tgt, idx, src, axis=0):
    return tgt.at[idx].add(src)

def _segment_sum(src, seg, n):
    return jax.ops.segment_sum(src, seg, n)
kernel_name = 'mk_xattn_ffn_d4_seqx_r8_9af2fc'

def setup_inputs(seed: int=0):
    np.random.seed(seed)
    _w = jnp.asarray

    def _rec_inputs():
        import jax
        import jax.numpy as jnp
        _rk = jax.random.key(seed)
        x = -0.0002928 + 1 * jax.random.normal(jax.random.fold_in(_rk, 1), (16, 256, 128), jnp.float32)
        _lenS = 256 - jax.random.randint(jax.random.fold_in(_rk, 7), (16,), 0, max(1, 256 // 4) + 1, jnp.int32)
        _lenS2 = 1601 - jax.random.randint(jax.random.fold_in(_rk, 8), (16,), 0, max(1, 1601 // 4) + 1, jnp.int32)
        _ctx_512P = jax.random.normal(jax.random.fold_in(_rk, 11), (16, 16, 64), jnp.float32)
        _ctx_512c = jax.random.dirichlet(jax.random.fold_in(_rk, 511), 0.3 * jnp.ones((16,), jnp.float32), (16, 1601))
        _ctx_512t = jnp.einsum('bsk,bkd->bsd', _ctx_512c, _ctx_512P)
        _ctx_512t = _ctx_512t * jax.lax.rsqrt(jnp.mean(jnp.square(_ctx_512t)) + 1e-12) * 0.953939
        ctx_512 = 0.00222621 + 0.99962 * (_ctx_512t + 0.3 * jax.random.normal(jax.random.fold_in(_rk, 611), (16, 1601, 64), jnp.float32))
        return (x, ctx_512)
    x, ctx_512 = _rec_inputs()

    def _L0_xattn_setup():
        import jax, jax.numpy as jnp
        import numpy as np
        B, T, TC, C, CC, H = (2, 256, 64, 128, 64, 16)
        D = C // H

        def _heads(t):
            b, l, _ = t.shape
            return t.reshape(b, l, H, D).transpose(0, 2, 1, 3)
        key = jax.random.key(seed)
        ks = jax.random.split(key, 18)
        w = lambda k, i, o: jax.random.normal(k, (i, o), jnp.float32) / np.sqrt(i).astype(np.float32)
        return {'x': jax.random.normal(ks[0], (B, T, C), jnp.float32), 'cross_input': jax.random.normal(ks[1], (B, TC, CC), jnp.float32), 'Wk': w(ks[2], C, C), 'bk': jnp.zeros((C,), jnp.float32), 'Wq': w(ks[3], C, C), 'bq': jnp.zeros((C,), jnp.float32), 'Wv': w(ks[4], C, C), 'bv': jnp.zeros((C,), jnp.float32), 'Wck': w(ks[5], CC, C), 'bck': jnp.zeros((C,), jnp.float32), 'Wcq': w(ks[6], C, C), 'bcq': jnp.zeros((C,), jnp.float32), 'Wcv': w(ks[7], CC, C), 'bcv': jnp.zeros((C,), jnp.float32), 'Wp': w(ks[8], C, C), 'bp': jnp.zeros((C,), jnp.float32)}
    _L0_xattn_all = _L0_xattn_setup()
    _L0_xattn_in = {k: v for k, v in _L0_xattn_all.items() if k in ('Wk', 'bk', 'Wq', 'bq', 'Wv', 'bv', 'Wck', 'bck', 'Wcq', 'bcq', 'Wcv', 'bcv', 'Wp', 'bp')}
    del _L0_xattn_all

    def _L0_ffn_setup():
        import jax, jax.numpy as jnp
        import numpy as np
        TOP_K = 4
        key = jax.random.key(seed)
        ks = jax.random.split(key, 5)
        B, T, D = (2, 128, 128)
        P, PD = (32, 32)
        return {'x': jax.random.normal(ks[0], (B, T, D), dtype=jnp.float32), 'hasher_w': jax.random.normal(ks[1], (PD, D), dtype=jnp.float32) * 0.03, 'keys': jax.random.normal(ks[2], (P, PD), dtype=jnp.float32) * 0.1, 'values_down': jax.random.normal(ks[3], (P, D, PD), dtype=jnp.float32) * 0.01, 'values_up': jax.random.normal(ks[4], (P, PD, D), dtype=jnp.float32) * 0.01, 'scale': jnp.full((1,), 0.1, dtype=jnp.float32)}
    _L0_ffn_all = _L0_ffn_setup()
    _L0_ffn_in = {k: v for k, v in _L0_ffn_all.items() if k in ('hasher_w', 'keys', 'values_down', 'values_up', 'scale')}
    del _L0_ffn_all

    def _L1_xattn_setup():
        import jax, jax.numpy as jnp
        import numpy as np
        DIM = 128
        LATENT_DIM = 64
        NUM_HEADS = 16
        HEAD_DIM = DIM // NUM_HEADS
        SCALE = HEAD_DIM ** (-0.5)
        key = jax.random.key(seed)
        k1, k2, k3, k4, k5 = jax.random.split(key, 5)
        B, xN, zN = (2, 256, 256)
        x = jax.random.normal(k1, (B, xN, DIM), dtype=jnp.float32)
        z = jax.random.normal(k2, (B, zN, LATENT_DIM), dtype=jnp.float32)
        Wq = jax.random.normal(k3, (DIM, DIM), dtype=jnp.float32) * DIM ** (-0.5)
        Wkv = jax.random.normal(k4, (2 * DIM, LATENT_DIM), dtype=jnp.float32) * LATENT_DIM ** (-0.5)
        Wo = jax.random.normal(k5, (DIM, DIM), dtype=jnp.float32) * DIM ** (-0.5)
        return {'x': x, 'z': z, 'Wq': Wq, 'Wkv': Wkv, 'Wo': Wo}
    _L1_xattn_all = _L1_xattn_setup()
    _L1_xattn_in = {k: v for k, v in _L1_xattn_all.items() if k in ('Wq', 'Wkv', 'Wo')}
    del _L1_xattn_all

    def _L1_ffn_setup():
        import jax, jax.numpy as jnp
        import numpy as np
        B, S, D_MODEL, D_HIDDEN = (4, 256, 128, 512)

        def act_quant(x):
            scale = 127.0 / jnp.clip(jnp.max(jnp.abs(x), axis=-1, keepdims=True), 1e-05)
            return jnp.clip(jnp.round(x * scale), -128, 127) / scale

        def weight_quant(w):
            scale = 1.0 / jnp.clip(jnp.mean(jnp.abs(w)), 1e-05)
            return jnp.clip(jnp.round(w * scale), -1, 1) / scale

        def bit_linear(x, w):
            xq = x + jax.lax.stop_gradient(act_quant(x) - x)
            wq = w + jax.lax.stop_gradient(weight_quant(w) - w)
            return jnp.einsum('bsd,hd->bsh', xq, wq)

        def depthwise_conv1d(x_bcl, w, b):
            y = jax.lax.conv_general_dilated(x_bcl, w, window_strides=(1,), padding=[(1, 1)], dimension_numbers=('NCH', 'OIH', 'NCH'), feature_group_count=x_bcl.shape[1])
            return y + b[None, :, None]
        key = jax.random.key(seed)
        ks = jax.random.split(key, 5)
        lim1 = 1.0 / np.sqrt(D_MODEL)
        lim2 = 1.0 / np.sqrt(D_HIDDEN)
        limc = 1.0 / np.sqrt(3.0)
        return {'x': jax.random.normal(ks[0], (B, S, D_MODEL), dtype=jnp.float32), 'w1': jax.random.uniform(ks[1], (D_HIDDEN, D_MODEL), jnp.float32, -lim1, lim1), 'conv_w': jax.random.uniform(ks[2], (D_HIDDEN, 1, 3), jnp.float32, -limc, limc), 'conv_b': jax.random.uniform(ks[3], (D_HIDDEN,), jnp.float32, -limc, limc), 'w2': jax.random.uniform(ks[4], (D_MODEL, D_HIDDEN), jnp.float32, -lim2, lim2)}
    _L1_ffn_all = _L1_ffn_setup()
    _L1_ffn_in = {k: v for k, v in _L1_ffn_all.items() if k in ('w1', 'conv_w', 'conv_b', 'w2')}
    del _L1_ffn_all

    def _L2_xattn_setup():
        import jax, jax.numpy as jnp
        import numpy as np
        H, D, C1, C2, S, M, B, W = (16, 32, 128, 64, 256, 64, 2, 4)

        def _ln(x, g, b):
            m = jnp.mean(x, -1, keepdims=True)
            v = jnp.var(x, -1, keepdims=True)
            return (x - m) * jax.lax.rsqrt(v + 1e-05) * g + b

        def _mha(x, y, wq, wk, wv, li1_w, li1_b, lnx_g, lnx_b, lny_g, lny_b, ln3_g, ln3_b, li2_w, li2_b, li3_w, li3_b, causal):
            xn = _ln(x, lnx_g, lnx_b)
            yn = _ln(y, lny_g, lny_b)
            q = jnp.einsum('bsc,hcd->bhsd', xn, wq)
            k = jnp.einsum('btc,hcd->bhtd', yn, wk)
            v = jnp.einsum('btc,hcd->bhtd', yn, wv)
            a = jax.nn.softmax(jnp.einsum('bhsd,bhtd->bhst', q, k) * D ** (-0.5), axis=-1)
            if causal:
                s, t = (a.shape[-2], a.shape[-1])
                mask = (jnp.arange(t)[None, :] > jnp.arange(s)[:, None]).astype(a.dtype)
                a = a * mask
            o = jnp.einsum('bhst,bhtd->bhsd', a, v)
            o = o.transpose(0, 2, 1, 3).reshape(x.shape[0], x.shape[1], H * D)
            x_out = x + o @ li1_w + li1_b
            h = jax.nn.gelu(_ln(x_out, ln3_g, ln3_b) @ li2_w + li2_b, approximate=False)
            return x_out + h @ li3_w + li3_b
        key = jax.random.key(seed)
        ks = iter(jax.random.split(key, 64))

        def w(shape, scale=0.02):
            return jax.random.normal(next(ks), shape, jnp.float32) * scale
        inp = {'xx': jax.random.normal(next(ks), (B, S, C1), jnp.float32), 'ee': jax.random.normal(next(ks), (B, M, C2), jnp.float32), 'ln1_g': jnp.ones(C1, jnp.float32), 'ln1_b': jnp.zeros(C1, jnp.float32), 'ln2_g': jnp.ones(C1, jnp.float32), 'ln2_b': jnp.zeros(C1, jnp.float32)}
        for pfx, cy in (('a1', C1), ('a2', C2)):
            inp[pfx + '_wq'] = w((H, C1, D))
            inp[pfx + '_wk'] = w((H, cy, D))
            inp[pfx + '_wv'] = w((H, cy, D))
            inp[pfx + '_li1_w'] = w((H * D, C1))
            inp[pfx + '_li1_b'] = jnp.zeros(C1, jnp.float32)
            inp[pfx + '_lnx_g'] = jnp.ones(C1, jnp.float32)
            inp[pfx + '_lnx_b'] = jnp.zeros(C1, jnp.float32)
            inp[pfx + '_lny_g'] = jnp.ones(cy, jnp.float32)
            inp[pfx + '_lny_b'] = jnp.zeros(cy, jnp.float32)
            inp[pfx + '_ln3_g'] = jnp.ones(C1, jnp.float32)
            inp[pfx + '_ln3_b'] = jnp.zeros(C1, jnp.float32)
            inp[pfx + '_li2_w'] = w((C1, C1 * W))
            inp[pfx + '_li2_b'] = jnp.zeros(C1 * W, jnp.float32)
            inp[pfx + '_li3_w'] = w((C1 * W, C1))
            inp[pfx + '_li3_b'] = jnp.zeros(C1, jnp.float32)
        inp['training'] = 0
        return inp
    _L2_xattn_all = _L2_xattn_setup()
    _L2_xattn_in = {k: v for k, v in _L2_xattn_all.items() if k in ('ln1_g', 'ln1_b', 'ln2_g', 'ln2_b', 'a1_wq', 'a1_wk', 'a1_wv', 'a1_li1_w', 'a1_li1_b', 'a1_lnx_g', 'a1_lnx_b', 'a1_lny_g', 'a1_lny_b', 'a1_ln3_g', 'a1_ln3_b', 'a1_li2_w', 'a1_li2_b', 'a1_li3_w', 'a1_li3_b', 'a2_wq', 'a2_wk', 'a2_wv', 'a2_li1_w', 'a2_li1_b', 'a2_lnx_g', 'a2_lnx_b', 'a2_lny_g', 'a2_lny_b', 'a2_ln3_g', 'a2_ln3_b', 'a2_li2_w', 'a2_li2_b', 'a2_li3_w', 'a2_li3_b')}
    del _L2_xattn_all

    def _L2_ffn_setup():
        import jax, jax.numpy as jnp
        import numpy as np
        B, T, D, E, H = (8, 256, 128, 8, 32)
        LN_EPS = 1e-05
        key = jax.random.key(seed)
        ks = jax.random.split(key, 4)
        return {'x': jax.random.normal(ks[0], (B, T, D), dtype=jnp.float32), 'Wg': jax.random.normal(ks[1], (E, D), dtype=jnp.float32) * 0.02, 'ln_scale': jnp.ones((E, D), dtype=jnp.float32), 'ln_bias': jnp.zeros((E, D), dtype=jnp.float32), 'W1': jax.random.normal(ks[2], (E, D, H), dtype=jnp.float32) * 0.02, 'b1': jnp.zeros((E, H), dtype=jnp.float32), 'W2': jax.random.normal(ks[3], (E, H, D), dtype=jnp.float32) * 0.02, 'b2': jnp.zeros((E, D), dtype=jnp.float32)}
    _L2_ffn_all = _L2_ffn_setup()
    _L2_ffn_in = {k: v for k, v in _L2_ffn_all.items() if k in ('Wg', 'ln_scale', 'ln_bias', 'W1', 'b1', 'W2', 'b2')}
    del _L2_ffn_all

    def _L3_xattn_setup():
        import jax, jax.numpy as jnp
        import numpy as np
        HEADS = 16
        D_MODEL = 128
        IMG_MODEL = 64
        D_K = D_MODEL // HEADS
        key = jax.random.key(seed)
        ks = jax.random.split(key, 12)
        B, LQ, LKV = (8, 256, 128)
        s_dm = 1.0 / np.sqrt(D_MODEL)
        s_im = 1.0 / np.sqrt(IMG_MODEL)
        return {'q': jax.random.normal(ks[0], (B, LQ, D_MODEL), jnp.float32), 'k': jax.random.normal(ks[1], (B, LKV, IMG_MODEL), jnp.float32), 'v': jax.random.normal(ks[2], (B, LKV, IMG_MODEL), jnp.float32), 'Wq': jax.random.normal(ks[3], (D_MODEL, D_MODEL), jnp.float32) * s_dm, 'bq': jnp.zeros((D_MODEL,), jnp.float32), 'Wk': jax.random.normal(ks[4], (IMG_MODEL, D_MODEL), jnp.float32) * s_im, 'bk': jnp.zeros((D_MODEL,), jnp.float32), 'Wv': jax.random.normal(ks[5], (IMG_MODEL, D_MODEL), jnp.float32) * s_im, 'bv': jnp.zeros((D_MODEL,), jnp.float32), 'Wo': jax.random.normal(ks[6], (D_MODEL, D_MODEL), jnp.float32) * s_dm, 'bo': jnp.zeros((D_MODEL,), jnp.float32)}
    _L3_xattn_all = _L3_xattn_setup()
    _L3_xattn_in = {k: v for k, v in _L3_xattn_all.items() if k in ('Wq', 'bq', 'Wk', 'bk', 'Wv', 'bv', 'Wo', 'bo')}
    del _L3_xattn_all

    def _L3_ffn_setup():
        import jax, jax.numpy as jnp
        import numpy as np
        DIM = 128
        MOE_HID = 64
        SHARED_HID = 256
        N_EXPERTS = 16
        TOP_K = 2
        NORM_TOPK_PROB = True
        key = jax.random.key(seed)
        ks = jax.random.split(key, 9)
        s = 0.02
        x = jax.random.normal(ks[0], (2, 128, DIM), dtype=jnp.float32)
        Wg = jax.random.normal(ks[1], (N_EXPERTS, DIM), dtype=jnp.float32) * s
        We_gate = jax.random.normal(ks[2], (N_EXPERTS, MOE_HID, DIM), dtype=jnp.float32) * s
        We_up = jax.random.normal(ks[3], (N_EXPERTS, MOE_HID, DIM), dtype=jnp.float32) * s
        We_down = jax.random.normal(ks[4], (N_EXPERTS, DIM, MOE_HID), dtype=jnp.float32) * s
        Ws_gate = jax.random.normal(ks[5], (SHARED_HID, DIM), dtype=jnp.float32) * s
        Ws_up = jax.random.normal(ks[6], (SHARED_HID, DIM), dtype=jnp.float32) * s
        Ws_down = jax.random.normal(ks[7], (DIM, SHARED_HID), dtype=jnp.float32) * s
        Wsg = jax.random.normal(ks[8], (1, DIM), dtype=jnp.float32) * s
        return {'x': x, 'Wg': Wg, 'We_gate': We_gate, 'We_up': We_up, 'We_down': We_down, 'Ws_gate': Ws_gate, 'Ws_up': Ws_up, 'Ws_down': Ws_down, 'Wsg': Wsg}
    _L3_ffn_all = _L3_ffn_setup()
    _L3_ffn_in = {k: v for k, v in _L3_ffn_all.items() if k in ('Wg', 'We_gate', 'We_up', 'We_down', 'Ws_gate', 'Ws_up', 'Ws_down', 'Wsg')}
    del _L3_ffn_all
    return {'x': x, 'ctx_512': ctx_512, 'L0_xattn_Wk': _L0_xattn_in['Wk'], 'L0_xattn_bk': _L0_xattn_in['bk'], 'L0_xattn_Wq': _L0_xattn_in['Wq'], 'L0_xattn_bq': _L0_xattn_in['bq'], 'L0_xattn_Wv': _L0_xattn_in['Wv'], 'L0_xattn_bv': _L0_xattn_in['bv'], 'L0_xattn_Wck': _L0_xattn_in['Wck'], 'L0_xattn_bck': _L0_xattn_in['bck'], 'L0_xattn_Wcq': _L0_xattn_in['Wcq'], 'L0_xattn_bcq': _L0_xattn_in['bcq'], 'L0_xattn_Wcv': _L0_xattn_in['Wcv'], 'L0_xattn_bcv': _L0_xattn_in['bcv'], 'L0_xattn_Wp': _L0_xattn_in['Wp'], 'L0_xattn_bp': _L0_xattn_in['bp'], 'L0_ffn_hasher_w': _L0_ffn_in['hasher_w'], 'L0_ffn_keys': _L0_ffn_in['keys'], 'L0_ffn_values_down': _L0_ffn_in['values_down'], 'L0_ffn_values_up': _L0_ffn_in['values_up'], 'L0_ffn_scale': _L0_ffn_in['scale'], 'L1_xattn_Wq': _L1_xattn_in['Wq'], 'L1_xattn_Wkv': _L1_xattn_in['Wkv'], 'L1_xattn_Wo': _L1_xattn_in['Wo'], 'L1_ffn_w1': _L1_ffn_in['w1'], 'L1_ffn_conv_w': _L1_ffn_in['conv_w'], 'L1_ffn_conv_b': _L1_ffn_in['conv_b'], 'L1_ffn_w2': _L1_ffn_in['w2'], 'L2_xattn_ln1_g': _L2_xattn_in['ln1_g'], 'L2_xattn_ln1_b': _L2_xattn_in['ln1_b'], 'L2_xattn_ln2_g': _L2_xattn_in['ln2_g'], 'L2_xattn_ln2_b': _L2_xattn_in['ln2_b'], 'L2_xattn_a1_wq': _L2_xattn_in['a1_wq'], 'L2_xattn_a1_wk': _L2_xattn_in['a1_wk'], 'L2_xattn_a1_wv': _L2_xattn_in['a1_wv'], 'L2_xattn_a1_li1_w': _L2_xattn_in['a1_li1_w'], 'L2_xattn_a1_li1_b': _L2_xattn_in['a1_li1_b'], 'L2_xattn_a1_lnx_g': _L2_xattn_in['a1_lnx_g'], 'L2_xattn_a1_lnx_b': _L2_xattn_in['a1_lnx_b'], 'L2_xattn_a1_lny_g': _L2_xattn_in['a1_lny_g'], 'L2_xattn_a1_lny_b': _L2_xattn_in['a1_lny_b'], 'L2_xattn_a1_ln3_g': _L2_xattn_in['a1_ln3_g'], 'L2_xattn_a1_ln3_b': _L2_xattn_in['a1_ln3_b'], 'L2_xattn_a1_li2_w': _L2_xattn_in['a1_li2_w'], 'L2_xattn_a1_li2_b': _L2_xattn_in['a1_li2_b'], 'L2_xattn_a1_li3_w': _L2_xattn_in['a1_li3_w'], 'L2_xattn_a1_li3_b': _L2_xattn_in['a1_li3_b'], 'L2_xattn_a2_wq': _L2_xattn_in['a2_wq'], 'L2_xattn_a2_wk': _L2_xattn_in['a2_wk'], 'L2_xattn_a2_wv': _L2_xattn_in['a2_wv'], 'L2_xattn_a2_li1_w': _L2_xattn_in['a2_li1_w'], 'L2_xattn_a2_li1_b': _L2_xattn_in['a2_li1_b'], 'L2_xattn_a2_lnx_g': _L2_xattn_in['a2_lnx_g'], 'L2_xattn_a2_lnx_b': _L2_xattn_in['a2_lnx_b'], 'L2_xattn_a2_lny_g': _L2_xattn_in['a2_lny_g'], 'L2_xattn_a2_lny_b': _L2_xattn_in['a2_lny_b'], 'L2_xattn_a2_ln3_g': _L2_xattn_in['a2_ln3_g'], 'L2_xattn_a2_ln3_b': _L2_xattn_in['a2_ln3_b'], 'L2_xattn_a2_li2_w': _L2_xattn_in['a2_li2_w'], 'L2_xattn_a2_li2_b': _L2_xattn_in['a2_li2_b'], 'L2_xattn_a2_li3_w': _L2_xattn_in['a2_li3_w'], 'L2_xattn_a2_li3_b': _L2_xattn_in['a2_li3_b'], 'L2_ffn_Wg': _L2_ffn_in['Wg'], 'L2_ffn_ln_scale': _L2_ffn_in['ln_scale'], 'L2_ffn_ln_bias': _L2_ffn_in['ln_bias'], 'L2_ffn_W1': _L2_ffn_in['W1'], 'L2_ffn_b1': _L2_ffn_in['b1'], 'L2_ffn_W2': _L2_ffn_in['W2'], 'L2_ffn_b2': _L2_ffn_in['b2'], 'L3_xattn_Wq': _L3_xattn_in['Wq'], 'L3_xattn_bq': _L3_xattn_in['bq'], 'L3_xattn_Wk': _L3_xattn_in['Wk'], 'L3_xattn_bk': _L3_xattn_in['bk'], 'L3_xattn_Wv': _L3_xattn_in['Wv'], 'L3_xattn_bv': _L3_xattn_in['bv'], 'L3_xattn_Wo': _L3_xattn_in['Wo'], 'L3_xattn_bo': _L3_xattn_in['bo'], 'L3_ffn_Wg': _L3_ffn_in['Wg'], 'L3_ffn_We_gate': _L3_ffn_in['We_gate'], 'L3_ffn_We_up': _L3_ffn_in['We_up'], 'L3_ffn_We_down': _L3_ffn_in['We_down'], 'L3_ffn_Ws_gate': _L3_ffn_in['Ws_gate'], 'L3_ffn_Ws_up': _L3_ffn_in['Ws_up'], 'L3_ffn_Ws_down': _L3_ffn_in['Ws_down'], 'L3_ffn_Wsg': _L3_ffn_in['Wsg']}

def reference(x, ctx_512, L0_xattn_Wk, L0_xattn_bk, L0_xattn_Wq, L0_xattn_bq, L0_xattn_Wv, L0_xattn_bv, L0_xattn_Wck, L0_xattn_bck, L0_xattn_Wcq, L0_xattn_bcq, L0_xattn_Wcv, L0_xattn_bcv, L0_xattn_Wp, L0_xattn_bp, L0_ffn_hasher_w, L0_ffn_keys, L0_ffn_values_down, L0_ffn_values_up, L0_ffn_scale, L1_xattn_Wq, L1_xattn_Wkv, L1_xattn_Wo, L1_ffn_w1, L1_ffn_conv_w, L1_ffn_conv_b, L1_ffn_w2, L2_xattn_ln1_g, L2_xattn_ln1_b, L2_xattn_ln2_g, L2_xattn_ln2_b, L2_xattn_a1_wq, L2_xattn_a1_wk, L2_xattn_a1_wv, L2_xattn_a1_li1_w, L2_xattn_a1_li1_b, L2_xattn_a1_lnx_g, L2_xattn_a1_lnx_b, L2_xattn_a1_lny_g, L2_xattn_a1_lny_b, L2_xattn_a1_ln3_g, L2_xattn_a1_ln3_b, L2_xattn_a1_li2_w, L2_xattn_a1_li2_b, L2_xattn_a1_li3_w, L2_xattn_a1_li3_b, L2_xattn_a2_wq, L2_xattn_a2_wk, L2_xattn_a2_wv, L2_xattn_a2_li1_w, L2_xattn_a2_li1_b, L2_xattn_a2_lnx_g, L2_xattn_a2_lnx_b, L2_xattn_a2_lny_g, L2_xattn_a2_lny_b, L2_xattn_a2_ln3_g, L2_xattn_a2_ln3_b, L2_xattn_a2_li2_w, L2_xattn_a2_li2_b, L2_xattn_a2_li3_w, L2_xattn_a2_li3_b, L2_ffn_Wg, L2_ffn_ln_scale, L2_ffn_ln_bias, L2_ffn_W1, L2_ffn_b1, L2_ffn_W2, L2_ffn_b2, L3_xattn_Wq, L3_xattn_bq, L3_xattn_Wk, L3_xattn_bk, L3_xattn_Wv, L3_xattn_bv, L3_xattn_Wo, L3_xattn_bo, L3_ffn_Wg, L3_ffn_We_gate, L3_ffn_We_up, L3_ffn_We_down, L3_ffn_Ws_gate, L3_ffn_Ws_up, L3_ffn_Ws_down, L3_ffn_Wsg):
    import jax
    import jax.numpy as jnp

    def _L0_xattn_ref(x, cross_input, Wk, bk, Wq, bq, Wv, bv, Wck, bck, Wcq, bcq, Wcv, bcv, Wp, bp):
        import jax, jax.numpy as jnp
        import numpy as np
        B, T, TC, C, CC, H = (2, 256, 64, 128, 64, 16)
        D = C // H

        def _heads(t):
            b, l, _ = t.shape
            return t.reshape(b, l, H, D).transpose(0, 2, 1, 3)
        scale = np.float32(1.0 / np.sqrt(D))
        q = _heads(x @ Wq + bq)
        k = _heads(x @ Wk + bk)
        v = _heads(x @ Wv + bv)
        att = jnp.einsum('bhqd,bhkd->bhqk', q, k) * scale
        causal = jnp.tril(jnp.ones((T, T), bool))
        att = jnp.where(causal[None, None], att, -jnp.inf)
        y = jnp.einsum('bhqk,bhkd->bhqd', jax.nn.softmax(att, axis=-1), v)
        qc = _heads(x @ Wcq + bcq)
        kc = _heads(cross_input @ Wck + bck)
        vc = _heads(cross_input @ Wcv + bcv)
        attc = jnp.einsum('bhqd,bhkd->bhqk', qc, kc) * scale
        y = y + jnp.einsum('bhqk,bhkd->bhqd', jax.nn.softmax(attc, axis=-1), vc)
        y = y.transpose(0, 2, 1, 3).reshape(x.shape[0], T, C)
        return y @ Wp + bp

    def _L0_ffn_ref(x, hasher_w, keys, values_down, values_up, scale):
        import jax, jax.numpy as jnp
        import numpy as np
        TOP_K = 4
        h = jnp.einsum('btd,pd->btp', x, hasher_w)
        sim = jnp.einsum('btp,np->btn', h, keys)
        vals, idx = jax.lax.top_k(sim, TOP_K)
        w = jax.nn.softmax(vals, axis=-1)
        out = jnp.zeros_like(x)
        for k in range(TOP_K):
            ik = idx[..., k]
            vd = values_down[ik]
            vu = values_up[ik]
            proj = jax.nn.silu(jnp.einsum('btd,btdp->btp', x, vd))
            o = jnp.einsum('btp,btpd->btd', proj, vu)
            out = out + o * w[..., k:k + 1]
        return x + out * scale

    def _L1_xattn_ref(x, z, Wq, Wkv, Wo):
        import jax, jax.numpy as jnp
        import numpy as np
        DIM = 128
        LATENT_DIM = 64
        NUM_HEADS = 16
        HEAD_DIM = DIM // NUM_HEADS
        SCALE = HEAD_DIM ** (-0.5)
        B, xN, _ = x.shape
        _, zN, _ = z.shape
        Q = (x @ Wq.T).reshape(B, xN, NUM_HEADS, HEAD_DIM)
        KV = (z @ Wkv.T).reshape(B, zN, 2, NUM_HEADS, HEAD_DIM)
        K = KV[:, :, 0]
        V = KV[:, :, 1]
        attn = jnp.einsum('bqhd,bkhd->bhqk', Q, K) * SCALE
        attn = jax.nn.softmax(attn, axis=-1)
        O = jnp.einsum('bhqk,bkhd->bqhd', attn, V).reshape(B, xN, DIM)
        return O @ Wo.T

    def _L1_ffn_ref(x, w1, conv_w, conv_b, w2):
        import jax, jax.numpy as jnp
        import numpy as np
        B, S, D_MODEL, D_HIDDEN = (4, 256, 128, 512)

        def act_quant(x):
            scale = 127.0 / jnp.clip(jnp.max(jnp.abs(x), axis=-1, keepdims=True), 1e-05)
            return jnp.clip(jnp.round(x * scale), -128, 127) / scale

        def weight_quant(w):
            scale = 1.0 / jnp.clip(jnp.mean(jnp.abs(w)), 1e-05)
            return jnp.clip(jnp.round(w * scale), -1, 1) / scale

        def bit_linear(x, w):
            xq = x + jax.lax.stop_gradient(act_quant(x) - x)
            wq = w + jax.lax.stop_gradient(weight_quant(w) - w)
            return jnp.einsum('bsd,hd->bsh', xq, wq)

        def depthwise_conv1d(x_bcl, w, b):
            y = jax.lax.conv_general_dilated(x_bcl, w, window_strides=(1,), padding=[(1, 1)], dimension_numbers=('NCH', 'OIH', 'NCH'), feature_group_count=x_bcl.shape[1])
            return y + b[None, :, None]
        h = bit_linear(x, w1)
        h = depthwise_conv1d(h.transpose(0, 2, 1), conv_w, conv_b)
        h = h.transpose(0, 2, 1)
        h = jax.nn.silu(h)
        return bit_linear(h, w2)

    def _L2_xattn_ref(xx, ee, ln1_g, ln1_b, ln2_g, ln2_b, a1_wq, a1_wk, a1_wv, a1_li1_w, a1_li1_b, a1_lnx_g, a1_lnx_b, a1_lny_g, a1_lny_b, a1_ln3_g, a1_ln3_b, a1_li2_w, a1_li2_b, a1_li3_w, a1_li3_b, a2_wq, a2_wk, a2_wv, a2_li1_w, a2_li1_b, a2_lnx_g, a2_lnx_b, a2_lny_g, a2_lny_b, a2_ln3_g, a2_ln3_b, a2_li2_w, a2_li2_b, a2_li3_w, a2_li3_b, training):
        import jax, jax.numpy as jnp
        import numpy as np
        H, D, C1, C2, S, M, B, W = (16, 32, 128, 64, 256, 64, 2, 4)

        def _ln(x, g, b):
            m = jnp.mean(x, -1, keepdims=True)
            v = jnp.var(x, -1, keepdims=True)
            return (x - m) * jax.lax.rsqrt(v + 1e-05) * g + b

        def _mha(x, y, wq, wk, wv, li1_w, li1_b, lnx_g, lnx_b, lny_g, lny_b, ln3_g, ln3_b, li2_w, li2_b, li3_w, li3_b, causal):
            xn = _ln(x, lnx_g, lnx_b)
            yn = _ln(y, lny_g, lny_b)
            q = jnp.einsum('bsc,hcd->bhsd', xn, wq)
            k = jnp.einsum('btc,hcd->bhtd', yn, wk)
            v = jnp.einsum('btc,hcd->bhtd', yn, wv)
            a = jax.nn.softmax(jnp.einsum('bhsd,bhtd->bhst', q, k) * D ** (-0.5), axis=-1)
            if causal:
                s, t = (a.shape[-2], a.shape[-1])
                mask = (jnp.arange(t)[None, :] > jnp.arange(s)[:, None]).astype(a.dtype)
                a = a * mask
            o = jnp.einsum('bhst,bhtd->bhsd', a, v)
            o = o.transpose(0, 2, 1, 3).reshape(x.shape[0], x.shape[1], H * D)
            x_out = x + o @ li1_w + li1_b
            h = jax.nn.gelu(_ln(x_out, ln3_g, ln3_b) @ li2_w + li2_b, approximate=False)
            return x_out + h @ li3_w + li3_b
        x = _ln(xx, ln1_g, ln1_b)
        x = x + _mha(x, x, a1_wq, a1_wk, a1_wv, a1_li1_w, a1_li1_b, a1_lnx_g, a1_lnx_b, a1_lny_g, a1_lny_b, a1_ln3_g, a1_ln3_b, a1_li2_w, a1_li2_b, a1_li3_w, a1_li3_b, causal=True)
        x = _ln(x, ln2_g, ln2_b)
        return x + _mha(x, ee, a2_wq, a2_wk, a2_wv, a2_li1_w, a2_li1_b, a2_lnx_g, a2_lnx_b, a2_lny_g, a2_lny_b, a2_ln3_g, a2_ln3_b, a2_li2_w, a2_li2_b, a2_li3_w, a2_li3_b, causal=False)

    def _L2_ffn_ref(x, Wg, ln_scale, ln_bias, W1, b1, W2, b2):
        import jax, jax.numpy as jnp
        import numpy as np
        B, T, D, E, H = (8, 256, 128, 8, 32)
        LN_EPS = 1e-05
        Bs, Ts, Ds = x.shape
        xt = x.reshape(Bs * Ts, Ds)
        logits = xt @ Wg.T
        top1 = jnp.argmax(logits, axis=-1)
        mu = jnp.mean(xt, axis=-1, keepdims=True)
        var = jnp.mean(jnp.square(xt - mu), axis=-1, keepdims=True)
        xhat = (xt - mu) * jax.lax.rsqrt(var + LN_EPS)
        n_experts = Wg.shape[0]

        def body(y, p):
            s_e, b_e, w1, bb1, w2, bb2, eid = p
            h = jax.nn.gelu((xhat * s_e + b_e) @ w1 + bb1, approximate=False)
            out = h @ w2 + bb2
            mask = (top1 == eid)[:, None].astype(out.dtype)
            return (y + mask * out, None)
        y0 = jnp.zeros_like(xt)
        y, _ = jax.lax.scan(body, y0, (ln_scale, ln_bias, W1, b1, W2, b2, jnp.arange(n_experts)))
        return y.reshape(Bs, Ts, Ds)

    def _L3_xattn_ref(q, k, v, Wq, bq, Wk, bk, Wv, bv, Wo, bo):
        import jax, jax.numpy as jnp
        import numpy as np
        HEADS = 16
        D_MODEL = 128
        IMG_MODEL = 64
        D_K = D_MODEL // HEADS
        B, LQ, _ = q.shape
        LKV = k.shape[1]
        qh = (q @ Wq + bq).reshape(B, LQ, HEADS, D_K).transpose(0, 2, 1, 3)
        kh = (k @ Wk + bk).reshape(B, LKV, HEADS, D_K).transpose(0, 2, 1, 3)
        vh = (v @ Wv + bv).reshape(B, LKV, HEADS, D_K).transpose(0, 2, 1, 3)
        scale = 1.0 / np.sqrt(D_K)
        scores = jnp.einsum('bhqd,bhkd->bhqk', qh, kh) * scale
        attn = jax.nn.softmax(scores, axis=-1)
        out = jnp.einsum('bhqk,bhkd->bhqd', attn, vh)
        concat = out.transpose(0, 2, 1, 3).reshape(B, LQ, D_MODEL)
        return concat @ Wo + bo

    def _L3_ffn_ref(x, Wg, We_gate, We_up, We_down, Ws_gate, Ws_up, Ws_down, Wsg):
        import jax, jax.numpy as jnp
        import numpy as np
        DIM = 128
        MOE_HID = 64
        SHARED_HID = 256
        N_EXPERTS = 16
        TOP_K = 2
        NORM_TOPK_PROB = True
        B, S, D = x.shape
        xt = x.reshape(-1, D)
        gates = jax.nn.softmax(xt @ Wg.T, axis=-1)
        scores, inds = jax.lax.top_k(gates, TOP_K)
        if NORM_TOPK_PROB:
            scores = scores / jnp.sum(scores, axis=-1, keepdims=True)
        g = jnp.einsum('td,ehd->teh', xt, We_gate)
        u = jnp.einsum('td,ehd->teh', xt, We_up)
        h = jax.nn.silu(g) * u
        y_all = jnp.einsum('teh,edh->ted', h, We_down)
        y_sel = jnp.take_along_axis(y_all, inds[:, :, None], axis=1)
        y = jnp.sum(y_sel * scores[:, :, None], axis=1)
        shared = jax.nn.silu(xt @ Ws_gate.T) * (xt @ Ws_up.T) @ Ws_down.T
        y = y + jax.nn.sigmoid(xt @ Wsg.T) * shared
        return y.reshape(B, S, D)
    x = x + _L0_xattn_ref(_layernorm(x, axis=-1), ctx_512, L0_xattn_Wk, L0_xattn_bk, L0_xattn_Wq, L0_xattn_bq, L0_xattn_Wv, L0_xattn_bv, L0_xattn_Wck, L0_xattn_bck, L0_xattn_Wcq, L0_xattn_bcq, L0_xattn_Wcv, L0_xattn_bcv, L0_xattn_Wp, L0_xattn_bp)
    x = x + _L0_ffn_ref(_layernorm(x, axis=-1), L0_ffn_hasher_w, L0_ffn_keys, L0_ffn_values_down, L0_ffn_values_up, L0_ffn_scale)
    x = x + _L1_xattn_ref(_layernorm(x, axis=-1), ctx_512, L1_xattn_Wq, L1_xattn_Wkv, L1_xattn_Wo)
    x = x + _L1_ffn_ref(_layernorm(x, axis=-1), L1_ffn_w1, L1_ffn_conv_w, L1_ffn_conv_b, L1_ffn_w2)
    x = x + _L2_xattn_ref(_layernorm(x, axis=-1), ctx_512, L2_xattn_ln1_g, L2_xattn_ln1_b, L2_xattn_ln2_g, L2_xattn_ln2_b, L2_xattn_a1_wq, L2_xattn_a1_wk, L2_xattn_a1_wv, L2_xattn_a1_li1_w, L2_xattn_a1_li1_b, L2_xattn_a1_lnx_g, L2_xattn_a1_lnx_b, L2_xattn_a1_lny_g, L2_xattn_a1_lny_b, L2_xattn_a1_ln3_g, L2_xattn_a1_ln3_b, L2_xattn_a1_li2_w, L2_xattn_a1_li2_b, L2_xattn_a1_li3_w, L2_xattn_a1_li3_b, L2_xattn_a2_wq, L2_xattn_a2_wk, L2_xattn_a2_wv, L2_xattn_a2_li1_w, L2_xattn_a2_li1_b, L2_xattn_a2_lnx_g, L2_xattn_a2_lnx_b, L2_xattn_a2_lny_g, L2_xattn_a2_lny_b, L2_xattn_a2_ln3_g, L2_xattn_a2_ln3_b, L2_xattn_a2_li2_w, L2_xattn_a2_li2_b, L2_xattn_a2_li3_w, L2_xattn_a2_li3_b, 0)
    x = x + _L2_ffn_ref(_layernorm(x, axis=-1), L2_ffn_Wg, L2_ffn_ln_scale, L2_ffn_ln_bias, L2_ffn_W1, L2_ffn_b1, L2_ffn_W2, L2_ffn_b2)
    x = x + _L3_xattn_ref(_layernorm(x, axis=-1), ctx_512, ctx_512, L3_xattn_Wq, L3_xattn_bq, L3_xattn_Wk, L3_xattn_bk, L3_xattn_Wv, L3_xattn_bv, L3_xattn_Wo, L3_xattn_bo)
    x = x + _L3_ffn_ref(_layernorm(x, axis=-1), L3_ffn_Wg, L3_ffn_We_gate, L3_ffn_We_up, L3_ffn_We_down, L3_ffn_Ws_gate, L3_ffn_Ws_up, L3_ffn_Ws_down, L3_ffn_Wsg)
    return x

_drawn_inputs = setup_inputs


def setup_inputs(seed=0):
    import zlib

    import numpy as np

    out = dict(_drawn_inputs(seed))
    spreads = {'L0_xattn_bk': (0.0, 0.8),
     'L0_xattn_bq': (0.0, 0.467),
     'L0_xattn_bv': (0.0, 0.1),
     'L0_xattn_bck': (0.0, 0.8),
     'L0_xattn_bcq': (0.0, 0.398),
     'L0_xattn_bcv': (0.0, 0.1),
     'L0_xattn_bp': (0.0, 0.1),
     'L2_xattn_ln1_g': (1.0, 0.2),
     'L2_xattn_ln1_b': (0.0, 0.1),
     'L2_xattn_ln2_g': (1.0, 0.2),
     'L2_xattn_ln2_b': (0.0, 0.1),
     'L2_xattn_a1_li1_b': (0.0, 0.333),
     'L2_xattn_a1_lnx_g': (1.0, 0.6),
     'L2_xattn_a1_lnx_b': (0.0, 0.8),
     'L2_xattn_a1_lny_g': (1.0, 0.6),
     'L2_xattn_a1_lny_b': (0.0, 0.8),
     'L2_xattn_a1_ln3_g': (1.0, 0.6),
     'L2_xattn_a1_ln3_b': (0.0, 0.8),
     'L2_xattn_a1_li2_b': (0.0, 0.8),
     'L2_xattn_a1_li3_b': (0.0, 0.349),
     'L2_xattn_a2_li1_b': (0.0, 0.337),
     'L2_xattn_a2_lnx_g': (1.0, 0.6),
     'L2_xattn_a2_lnx_b': (0.0, 0.8),
     'L2_xattn_a2_lny_g': (1.0, 0.6),
     'L2_xattn_a2_lny_b': (0.0, 0.8),
     'L2_xattn_a2_ln3_g': (1.0, 0.6),
     'L2_xattn_a2_ln3_b': (0.0, 0.8),
     'L2_xattn_a2_li2_b': (0.0, 0.8),
     'L2_xattn_a2_li3_b': (0.0, 0.334),
     'L2_ffn_ln_scale': (1.0, 0.6),
     'L2_ffn_ln_bias': (0.0, 0.8),
     'L2_ffn_b1': (0.0, 0.8),
     'L2_ffn_b2': (0.0, 0.345),
     'L3_xattn_bq': (0.0, 0.8),
     'L3_xattn_bk': (0.0, 0.8),
     'L3_xattn_bv': (0.0, 0.384),
     'L3_xattn_bo': (0.0, 0.342)}
    factors = {'L0_ffn_hasher_w': 8.0,
     'L0_ffn_keys': 8.0,
     'L0_ffn_values_down': 8.0,
     'L0_ffn_values_up': 8.0,
     'L2_xattn_a1_wq': 8.0,
     'L2_xattn_a1_wk': 8.0,
     'L2_xattn_a1_wv': 7.023,
     'L2_xattn_a1_li1_w': 7.012,
     'L2_xattn_a1_li2_w': 4.253,
     'L2_xattn_a1_li3_w': 3.78,
     'L2_xattn_a2_wq': 8.0,
     'L2_xattn_a2_wk': 8.0,
     'L2_xattn_a2_wv': 5.993,
     'L2_xattn_a2_li1_w': 5.912,
     'L2_xattn_a2_li2_w': 4.274,
     'L2_xattn_a2_li3_w': 3.932,
     'L2_ffn_W1': 8.0,
     'L2_ffn_W2': 8.0,
     'L3_ffn_Wg': 8.0,
     'L3_ffn_We_gate': 8.0,
     'L3_ffn_We_up': 8.0,
     'L3_ffn_We_down': 8.0,
     'L3_ffn_Ws_gate': 8.0,
     'L3_ffn_Ws_up': 8.0,
     'L3_ffn_Ws_down': 8.0,
     'L3_ffn_Wsg': 8.0}
    for name, (base, spread) in spreads.items():
        noise = np.random.default_rng([zlib.crc32(name.encode()), seed]).standard_normal(out[name].shape)
        drawn = base * np.exp(spread * noise) if base else spread * noise
        out[name] = jnp.asarray(drawn.astype(out[name].dtype))
    for name, factor in factors.items():
        out[name] = (out[name] * factor).astype(out[name].dtype)
    return out
```

```python
from contextlib import ExitStack

import concourse.bass as bass
from concourse import mybir

F32 = mybir.dt.float32
BF16 = mybir.dt.bfloat16
U32 = mybir.dt.uint32
ALU = mybir.AluOpType
ACT = mybir.ActivationFunctionType
AX = mybir.AxisListType

P = 128
BATCH, TOK, C, CC, NKEY = 16, 256, 128, 64, 1601
HEADS = 16
QUADS = HEADS // 4
QT = TOK // P
FTOK = 512
FT = FTOK // P
FSTEPS = BATCH * TOK // FTOK
EPS = 1e-5
K_PART = (0, 0, 0, 1, 1, 2)
Q_PART = (0, 1, 2, 0, 1, 0)
SLOTS = len(K_PART)
MAXROW = 8 * SLOTS
P_BUFS = 4
LAG = 2


def key_tiles(nk):
    return [(t * P, min(P, nk - t * P)) for t in range((nk + P - 1) // P)]


def key_chunks(nk):
    n = (nk + 511) // 512
    cuts = [nk * i // n for i in range(n + 1)]
    return [(cuts[i], cuts[i + 1] - cuts[i]) for i in range(n)]


class Sems:

    def __init__(self, nc, ctx, stage, names):
        self.work = {n: ctx.enter_context(nc.semaphore(f"{stage}_{n}")) for n in names + ["iter_done"]}
        self.go = {e: ctx.enter_context(nc.semaphore(f"{stage}_go_{e}")) for e in ("pe", "act", "dve", "pool")}

    def __getitem__(self, name):
        return self.work[name]

    def end_iteration(self, eng, who):
        eng.drain().then_inc(self["iter_done"], 1)
        eng.wait_ge(self.go[who], 1)
        eng.sem_clear(self.go[who])

    def next_iteration(self, sp):
        sp.wait_ge(self["iter_done"], 4)
        nums = sorted(s.num for s in self.work.values())
        if nums[-1] - nums[0] + 1 == len(nums):
            sp.sem_clear(range(nums[0], nums[-1] + 1))
        else:
            for s in self.work.values():
                sp.sem_clear(s)
        for s in self.go.values():
            sp.sem_inc(s, 1)


class Chain:

    def __init__(self, eng, sem):
        self.eng, self.sem, self.n = eng, sem, 0

    def __call__(self, ins):
        ins.then_inc(self.sem, 1)
        self.n += 1
        self.eng.wait_ge(self.sem, self.n)


class Mem:

    def __init__(self, nc, ctx, stage):
        self.nc, self.ctx, self.stage = nc, ctx, stage

    def __call__(self, name, shape, dt=F32):
        return self.ctx.enter_context(self.nc.sbuf_tensor(f"{self.stage}_{name}", shape, dt))


def load_weights(nc, ctx, stage, pairs, prepare=None):
    s_w = ctx.enter_context(nc.semaphore(f"{stage}_weights"))
    s_c = ctx.enter_context(nc.semaphore(f"{stage}_constants"))
    with nc.Block() as block:
        @block.sync
        def _(sp):
            for dst, src in pairs:
                sp.dma_start(dst, src).then_inc(s_w, 16)
            sp.wait_ge(s_w, 16 * len(pairs))
            sp.sem_clear(s_w)

        @block.gpsimd
        def _(pool):
            if prepare:
                prepare(pool, Chain(pool, s_c))
                pool.sem_clear(s_c)



def ln_stats(dve, S, L, tiles, rows=None):
    for t, x in enumerate(tiles):
        ins = dve.bn_stats(L.st[0:x.shape[0], t, :], x)
    L.chain(ins)
    for t, x in enumerate(tiles):
        ins = dve.bn_aggr(L.mv[0:x.shape[0], t, :], L.st[0:x.shape[0], t, :])
    ins.then_inc(S["ln_var"], 1)
    L.count += 1
    dve.wait_ge(S["ln_rstd"], L.count)


def ln_apply(dve, L, t, out, x):
    n = x.shape[0]
    return dve.tensor_scalar(out, x, L.mv[0:n, t, 0:1], L.rs[0:n, t, 0:1], ALU.subtract, ALU.mult)


def ln_rstd(pool, S, L, k, nt):
    pool.wait_ge(S["ln_var"], k + 1)
    pool.tensor_scalar(L.ve[:, 0:nt, :], L.mv[:, 0:nt, 1:2], EPS, None, ALU.add).then_inc(S["ln_eps"], 1)
    pool.wait_ge(S["ln_eps"], k + 1)
    pool.tensor_tensor(L.rs[:, 0:nt, :], L.ve[:, 0:nt, :], L.mh[:, 0:nt, :], ALU.pow).then_inc(S["ln_rstd"], 1)


LN_SEMS = ["ln_var", "ln_eps", "ln_rstd"]


class LnMem:
    def __init__(self, sb, n):
        self.n = n
        self.st = sb("ln_st", [P, n, 6])
        self.mv = sb("ln_mv", [P, n, 2])
        self.ve = sb("ln_ve", [P, n, 1])
        self.rs = sb("ln_rs", [P, n, 1])
        self.mh = sb("ln_mh", [P, n, 1])

    def prepare(self, pool, chain):
        chain(pool.memset(self.mh[:, :, :], -0.5))
        chain(pool.memset(self.mv[:, :, :], 0.0))

    def begin(self, chain):
        self.chain, self.count = chain, 0



class Source:

    def __init__(self, nk, mask, idx0, unit0, quad0):
        self.nk, self.mask = nk, mask
        self.tiles, self.chunks = key_tiles(nk), key_chunks(nk)
        self.T = len(self.tiles)
        self.NU = QT * 4 * len(self.chunks)
        self.idx0, self.unit0, self.quad0 = idx0, unit0, quad0

    def unit(self, k):
        nc_ = len(self.chunks)
        return k // (4 * nc_), k // nc_ % 4, k % nc_

    def schedule(self):
        last_unit, turn = (self.T - 4, self.T - 2) if self.T > 4 else (0, self.T - 1)
        steps = [(g, t) for g in range(QUADS) for t in range(self.T)]
        plan = [("unit", 0, k) for k in range(self.NU)] + [("turn", 0, 0)]
        for n, (g, t) in enumerate(steps):
            plan.append(("scores", g, t))
            if g + 1 < QUADS and t <= last_unit:
                plan += [("unit", g + 1, k) for k in range(self.NU * t // (last_unit + 1),
                                                           self.NU * (t + 1) // (last_unit + 1))]
            if g + 1 < QUADS and t == turn:
                plan.append(("turn", g + 1, 0))
            if n >= LAG:
                plan.append(("pv",) + steps[n - LAG])
        plan += [("pv",) + s for s in steps[-LAG:]]
        return plan


CORE_SEMS = ["max_scores", "max_taken", "max_rows", "max_turned", "max_ready", "scores", "probs", "masked", "rest",
             "pv", "heads_out", "sums_wide", "sums_inv", "heads_ok", "proj"]


def make_sources(specs):
    out, i, u, q = [], 0, 0, 0
    for nk, mask in specs:
        s = Source(nk, mask, i, u, q)
        out.append(s)
        i, u, q = i + QUADS * s.T, u + QUADS * s.NU, q + QUADS
    return out


def core_pe(pe, S, A, s):
    def unit(g, k):
        u = s.unit0 + g * s.NU + k
        qt, h, c = s.unit(k)
        c0, n = s.chunks[c]
        if k == 0 and s.quad0 + g >= 1:
            pe.wait_ge(S["max_ready"], s.quad0 + g)
        if u >= 2:
            pe.wait_ge(S["max_taken"], u - 1)
        pe.matmul(A.bank[2 + u % 2][:, 0:n], A.q_max(s, g, h, qt), A.k_max(s, g, h, c0, n),
                  start=True, stop=True).then_inc(S["max_scores"], 1)

    def turn(g):
        pe.wait_ge(S["max_rows"], s.quad0 + g + 1)
        for qt in range(QT):
            ins = pe.transpose(A.bank[2][0:4, qt * P:(qt + 1) * P], A.negmax[:, qt, :], A.ident[:, :])
        ins.then_inc(S["max_turned"], 1)

    def scores(g, t):
        i = s.idx0 + g * s.T + t
        if i >= 2:
            pe.wait_ge(S["probs"], i - 1)
        if t == 0:
            A.wait_max(pe, s.quad0 + g)
        for h in range(4):
            k0, n = s.tiles[t]
            ins = A.scores(pe, A.S4[0:n, i % 2, h % 2, h // 2 * TOK:(h // 2 + 1) * TOK], s, g, h, k0, n)
        ins.then_inc(S["scores"], 1)

    def pv(g, t):
        i = s.idx0 + g * s.T + t
        pe.wait_ge(S["rest"], i + 1)
        if t == 0:
            A.wait_out(pe, s.quad0 + g)
        A.pv(pe, s, g, t, i % P_BUFS).then_inc(S["pv"], 1)

    for what, g, j in s.schedule():
        {"unit": unit, "turn": lambda g, _: turn(g), "scores": scores, "pv": pv}[what](g, j)


def core_act(act, S, A, s):
    for what, g, t in s.schedule():
        i = s.idx0 + g * s.T + t
        if what == "scores":
            act.wait_ge(S["scores"], i + 1)
            if i >= P_BUFS:
                act.wait_ge(S["pv"], i - P_BUFS + 1)
            n = s.tiles[t][1]
            act.activation(A.probs[0:n, i % P_BUFS, :].rearrange("p (a q) -> p a q", a=2), A.S4[0:n, i % 2, :, :],
                           ACT.Exp, scale=A.scale).then_inc(S["probs"], 1)
        if what == "pv" and t == s.T - 1:
            act.wait_ge(S["pv"], i + 1)
            A.take_out(act, s.quad0 + g).then_inc(S["heads_out"], 1)


def core_pool(pool, S, A, s):
    for g in range(QUADS):
        for t in range(s.T):
            i = s.idx0 + g * s.T + t
            k0, n = s.tiles[t]
            b = i % P_BUFS
            if i:
                pool.wait_ge(S["rest"], i)
            pool.wait_ge(S["probs"], i + 1)
            pr = A.probs[0:n, b, :]
            if s.mask == "causal":
                pool.affine_select(out=pr, in_=pr, pattern=[[0, 4], [1, TOK]], compare_op=ALU.is_ge, fill=0.0,
                                   base=-k0, channel_multiplier=-1).then_inc(S["masked"], 1)
                pool.wait_ge(S["masked"], i + 1)
            if s.mask == "after":
                pool.affine_select(out=A.kept[0:n, b, :], in_=pr, pattern=[[0, 4], [-1, TOK]], compare_op=ALU.is_gt,
                                   fill=0.0, base=k0, channel_multiplier=1).then_inc(S["masked"], 1)
                pool.wait_ge(S["masked"], i + 1)
                pool.tensor_tensor(A.kept_rest[0:n, b, :], A.kept[0:n, b, :], A.high(A.kept, b, n), ALU.subtract)
            pool.tensor_tensor(A.rest[0:n, b, :], pr, A.high(A.probs, b, n), ALU.subtract).then_inc(S["rest"], 1)


def core_dve(dve, S, A, s, chain):
    for what, g, k in s.schedule():
        if what == "unit":
            u = s.unit0 + g * s.NU + k
            qt, h, c = s.unit(k)
            n = s.chunks[c][1]
            dve.wait_ge(S["max_scores"], u + 1)
            if s.mask == "causal":
                if u:
                    dve.wait_ge(S["max_taken"], u)
                dve.tensor_tensor_reduce(A.junk[:, 0:n], A.bank[2 + u % 2][:, 0:n], A.past[:, qt, :], 1.0, -3.0e38,
                                         ALU.add, ALU.max, A.unit_max[:, qt, h, c:c + 1]).then_inc(S["max_taken"], 1)
            else:
                dve.tensor_reduce(A.unit_max[:, qt, h, c:c + 1], A.bank[2 + u % 2][:, 0:n], AX.X,
                                  ALU.max).then_inc(S["max_taken"], 1)
            if k == s.NU - 1:
                dve.wait_ge(S["max_taken"], u + 1)
                dve.tensor_reduce(A.negmax[:, :, :], A.unit_max[:, :, :, 0:len(s.chunks)], AX.X, ALU.max,
                                  negate=True).then_inc(S["max_rows"], 1)
        if what == "turn":
            dve.wait_ge(S["max_turned"], s.quad0 + g + 1)
            dve.tensor_copy(A.negmax_row[0:4, (s.quad0 + g) % 2, :],
                            A.bank[2][0:4, 0:TOK]).then_inc(S["max_ready"], 1)


def tail_pe(pe, S, A, n):
    for k in range(n):
        if k == 0:
            pe.wait_ge(S["heads_out"], A.quads)
        if k >= 4:
            pe.wait_ge(S["sums_inv"], k - 3)
        pe.matmul(A.S4[0:A.rows, k % 4 // 2, k % 2, :], A.spread[:, :], A.heads[:, 2 * k:2 * k + 2, :],
                  start=True, stop=True).then_inc(S["sums_wide"], 1)
    pe.wait_ge(S["heads_ok"], n)
    for qt in range(QT):
        for k in range(2 * n):
            ins = pe.matmul(A.bank[3][:, qt * C:(qt + 1) * C], A.heads[:, k, qt * P:(qt + 1) * P], A.w_out(k),
                            start=(k == 0), stop=(k == 2 * n - 1))
    ins.then_inc(S["proj"], 1)


def tail_dve(dve, S, A, n):
    for k in range(n):
        dve.wait_ge(S["sums_wide"], k + 1)
        inv = A.inv[:, k % 2, :]
        dve.reciprocal(inv, A.S4[0:A.rows, k % 4 // 2, k % 2, :]).then_inc(S["sums_inv"], 1)
        dve.wait_ge(S["sums_inv"], k + 1)
        v = A.heads[:, 2 * k:2 * k + 2, :].rearrange("p g q -> p (g q)")
        dve.tensor_tensor(v, v, inv, ALU.mult).then_inc(S["heads_ok"], 1)
    dve.wait_ge(S["proj"], 1)


class Core:

    def __init__(self, G, sb, rows, n_heads_out, scale):
        self.S4, self.bank, self.ident = G.S4, G.bank, G.ident
        self.rows, self.scale = rows, scale
        self.probs = sb("probs", [P, P_BUFS, 4 * TOK])
        self.rest = sb("rest", [P, P_BUFS, 4 * TOK], BF16)
        self.unit_max = sb("unit_max", [P, QT, 4, 4])
        self.negmax = sb("negmax", [P, QT, 4])
        self.negmax_row = sb("negmax_row", [4, 2, TOK], BF16)
        self.heads = sb("heads", [rows, n_heads_out, TOK])
        self.inv = sb("inv", [rows, 2, 2 * TOK])

    def high(self, t, b, n):
        return t[0:n, b, :].bitcast(BF16)[:, 1::2]

    @staticmethod
    def place(h):
        return slice(h % 2 * 512 + h // 2 * TOK, h % 2 * 512 + (h // 2 + 1) * TOK)



def attention8(nc, G, stage, x_in, x_out, w, with_self):
    specs = [(TOK, "causal")] * with_self + [(NKEY, None)]
    sources = make_sources(specs)
    ns = len(sources)
    k_col = [ns * TOK + sum(s.nk for s in sources[:i]) for i in range(ns)]
    W = ns * TOK + sum(s.nk for s in sources)
    self_src, cross = sources[0], sources[-1]
    parts_dram = nc.dram_tensor(f"{stage}_parts_dram", [3, P, W], BF16, kind="Internal").ap()

    with ExitStack() as ctx:
        sb = Mem(nc, ctx, stage)
        A = Core(G, sb, P, QUADS * ns, 8 ** -0.5)
        A.quads = QUADS * ns
        x_sb = sb("x", [P, QT, C])
        xn = sb("xn", [P, QT, C])
        xnT = sb("xnT", [C, TOK])
        ctxT = sb("ctxT", [CC, NKEY])
        qk = sb("qk", [P, W])
        parts = sb("parts", [P, 3, W], BF16)
        stack = sb("stack", [P, HEADS // 2, W], BF16)
        v_f = [sb(f"v_f{i}", [P, s.T, P]) for i, s in enumerate(sources)]
        v_parts = [sb(f"v_parts{i}", [P, s.T, HEADS, 32], BF16) for i, s in enumerate(sources)]
        A.past = G.past
        A.junk = sb("junk", [P, TOK]) if with_self else None
        L = LnMem(sb, QT)
        names_w = ["wq_c", "wk_c", "wv_c", "w_out", "bq_c", "bk_c", "bv_c", "b_out"]
        if with_self:
            names_w += ["wq_s", "wk_s", "wv_s", "bq_s", "bk_s", "bv_s"]
        W_sb = {n: sb(n, list(w[n].shape)) for n in names_w}
        A.spread = G.spread8

        S = Sems(nc, ctx, stage, ["x_in", "ctx_in", "xn", "xnT_ps", "xnT", "kc_ps", "kc", "vc_ps", "qs_ps", "qk",
                                  "vs_ps", "v_own", "v_all", "part0", "left", "part1", "part2", "parts_out",
                                  "stacked", "max_in", "res", "x_out", "dve_own"] + LN_SEMS + CORE_SEMS)

        def prepare(pool, chain):
            for base in (32, 96):
                chain(pool.memset(stack[base:base + 32, :, :], 1.0))
            for vf, vp in zip(v_f, v_parts):
                chain(pool.memset(vf[:, :, :], 0.0))
                chain(pool.memset(vp[:, :, :, 24:25], 1.0))
                chain(pool.memset(vp[:, :, :, 25:32], 0.0))
            L.prepare(pool, chain)

        load_weights(nc, ctx, stage, [(W_sb[n][...], w[n]) for n in names_w], prepare)

        A.w_out = lambda k: W_sb["w_out"][:, k % QUADS, :]

        def rows(g, h):
            head = 4 * g + h
            return head % 2 * 64, head // 2

        def q_of(s, g, h, c0, n, depth):
            r, pair = rows(g, h)
            c0 += sources.index(s) * TOK
            return stack[r:r + depth, pair, c0:c0 + n]

        def k_of(s, g, h, c0, n, depth):
            r, pair = rows(g, h)
            c0 += k_col[sources.index(s)]
            return stack[r:r + depth, pair, c0:c0 + n]

        A.q_max = lambda s, g, h, qt: q_of(s, g, h, qt * P, P, MAXROW)
        A.k_max = lambda s, g, h, c0, n: k_of(s, g, h, c0, n, MAXROW)
        A.wait_max = lambda pe, quad: pe.wait_ge(S["max_in"], 64 * (quad + 1))

        def scores(pe, out, s, g, h, k0, n):
            return pe.matmul(out, k_of(s, g, h, k0, n, MAXROW + 1), q_of(s, g, h, 0, TOK, MAXROW + 1),
                             start=True, stop=True)

        def wait_out(pe, quad):
            if quad >= 2:
                pe.wait_ge(S["heads_out"], quad - 1)

        def pv(pe, s, g, t, b):
            n = s.tiles[t][1]
            for h in range(4):
                out = A.bank[(s.quad0 + g) % 2][32 * h:32 * h + 32, 0:TOK]
                v = v_parts[sources.index(s)][0:n, t, 4 * g + h, :]
                pe.matmul(out, v, A.high(A.probs, b, n)[:, A.place(h)], start=(t == 0), stop=False)
                ins = pe.matmul(out, v, A.rest[0:n, b, A.place(h)], start=False, stop=(t == s.T - 1))
            return ins

        A.scores, A.wait_out, A.pv = scores, wait_out, pv
        A.take_out = lambda act, quad: act.activation(
            A.heads[:, quad, :], A.bank[quad % 2][:, 0:TOK], ACT.Copy)

        kc_bank = [A.S4[:, a, c, :] for a in range(2) for c in range(2)]
        vc_bank = A.bank
        xnT_ps = kc_bank[0][:, 0:TOK]
        qs_ps, ks_ps, vs_ps = kc_bank[1], kc_bank[2][:, 0:TOK], kc_bank[3][:, 0:QT * P]

        with nc.Block() as block:
            @block.sync
            def _(sp):
                with sp.Fori(0, BATCH) as b:
                    sp.dma_start(x_sb[:, :, :], x_in[b].rearrange("(t p) c -> p t c", p=P)).then_inc(S["x_in"], 16)
                    sp.dma_start(ctxT[:, :], G.ctxT[b]).then_inc(S["ctx_in"], 16)
                    for i, part in enumerate(("part0", "part1", "part2")):
                        sp.wait_ge(S[part], 1)
                        sp.dma_start(parts_dram[i], parts[:, i, :]).then_inc(S["parts_out"], 16)
                    sp.wait_ge(S["parts_out"], 48)
                    for cols, part_of in ((slice(0, ns * TOK), Q_PART), (slice(ns * TOK, W), K_PART)):
                        for slot in range(SLOTS):
                            src = parts_dram[part_of[slot]].rearrange("(h a d) n -> a d h n", a=2, d=8)
                            for a in range(2):
                                r = 64 * a + 8 * slot
                                sp.dma_start(stack[r:r + 8, :, cols], src[a][:, :, cols]).then_inc(S["stacked"], 16)
                    for s in sources:
                        q0 = sources.index(s) * TOK
                        for g in range(QUADS):
                            quad = s.quad0 + g
                            sp.wait_ge(S["max_ready"], quad + 1)
                            for h in range(4):
                                r, pair = rows(g, h)
                                sp.dma_start(stack[r + MAXROW:r + MAXROW + 1, pair, q0:q0 + TOK],
                                             A.negmax_row[h:h + 1, quad % 2, :]).then_inc(S["max_in"], 16)
                    sp.wait_ge(S["res"], 1)
                    sp.dma_start(x_out[b].rearrange("(t p) c -> p t c", p=P), xn[:, :, :]).then_inc(S["x_out"], 16)
                    sp.wait_ge(S["x_out"], 16)
                    S.next_iteration(sp)

            @block.tensor
            def _(pe):
                with pe.Fori(0, BATCH) as b:
                    pe.wait_ge(S["ctx_in"], 16)
                    for c, (c0, n) in enumerate(cross.chunks):
                        pe.matmul(kc_bank[c][:, 0:n], W_sb["wk_c"][:, :], ctxT[:, c0:c0 + n],
                                  start=True, stop=True).then_inc(S["kc_ps"], 1)
                    for t, (k0, n) in enumerate(cross.tiles):
                        out = vc_bank[t // 4][0:n, t % 4 * P:(t % 4 + 1) * P]
                        ins = pe.matmul(out, ctxT[:, k0:k0 + n], W_sb["wv_c"][:, :], start=True, stop=True)
                        if t % 4 == 3 or t == cross.T - 1:
                            ins.then_inc(S["vc_ps"], 1)
                    pe.wait_ge(S["xn"], 1)
                    pe.wait_ge(S["kc"], 1)
                    for t in range(QT):
                        ins = pe.transpose(xnT_ps[:, t * P:(t + 1) * P], xn[:, t, :], A.ident[:, :])
                    ins.then_inc(S["xnT_ps"], 1)
                    pe.wait_ge(S["xnT"], 1)
                    pe.wait_ge(S["kc"], 4)
                    if with_self:
                        pe.matmul(qs_ps[:, 0:TOK], W_sb["wq_s"][:, :], xnT[:, :], start=True, stop=True)
                        pe.matmul(ks_ps, W_sb["wk_s"][:, :], xnT[:, :], start=True, stop=True)
                        for t in range(self_src.T):
                            ins = pe.matmul(vs_ps[:, t * P:(t + 1) * P], xnT[:, t * P:(t + 1) * P], W_sb["wv_s"][:, :],
                                            start=True, stop=True)
                        ins.then_inc(S["vs_ps"], 1)
                    pe.matmul(qs_ps[:, (ns - 1) * TOK:ns * TOK], W_sb["wq_c"][:, :], xnT[:, :],
                              start=True, stop=True).then_inc(S["qs_ps"], 1)
                    pe.wait_ge(S["qk"], 1)
                    pe.wait_ge(S["v_all"], 1)
                    pe.wait_ge(S["stacked"], 16 * 4 * SLOTS)
                    for s in sources:
                        core_pe(pe, S, A, s)
                    tail_pe(pe, S, A, 2 * ns)
                    S.end_iteration(pe, "pe")

            @block.scalar
            def _(act):
                with act.Fori(0, BATCH) as b:
                    for c, (c0, n) in enumerate(cross.chunks):
                        act.wait_ge(S["kc_ps"], c + 1)
                        act.activation(qk[:, k_col[-1] + c0:k_col[-1] + c0 + n], kc_bank[c][:, 0:n], ACT.Identity,
                                       bias=W_sb["bk_c"][:, 0:1]).then_inc(S["kc"], 1)
                    act.wait_ge(S["xnT_ps"], 1)
                    act.activation(xnT[:, :], xnT_ps, ACT.Copy).then_inc(S["xnT"], 1)
                    act.wait_ge(S["qs_ps"], 1)
                    if with_self:
                        act.activation(qk[:, 0:TOK], qs_ps[:, 0:TOK], ACT.Identity, bias=W_sb["bq_s"][:, 0:1])
                        act.activation(qk[:, k_col[0]:k_col[0] + TOK], ks_ps, ACT.Identity, bias=W_sb["bk_s"][:, 0:1])
                    act.activation(qk[:, (ns - 1) * TOK:ns * TOK], qs_ps[:, (ns - 1) * TOK:ns * TOK], ACT.Identity,
                                   bias=W_sb["bq_c"][:, 0:1]).then_inc(S["qk"], 1)
                    for s in sources:
                        core_act(act, S, A, s)
                    S.end_iteration(act, "act")

            @block.vector
            def _(dve):
                with dve.Fori(0, BATCH) as b:
                    chain = Chain(dve, S["dve_own"])
                    L.begin(chain)
                    dve.wait_ge(S["x_in"], 16)
                    ln_stats(dve, S, L, [x_sb[:, t, :] for t in range(QT)])
                    for t in range(QT):
                        ins = ln_apply(dve, L, t, xn[:, t, :], x_sb[:, t, :])
                    ins.then_inc(S["xn"], 1)
                    for j in range(3):
                        dve.wait_ge(S["vc_ps"], j + 1)
                        dve.tensor_tensor(v_f[-1][:, 4 * j:4 * j + 4, :].rearrange("p t n -> p (t n)"), vc_bank[j][:, :],
                                          W_sb["bv_c"][:, :], ALU.add)
                    dve.wait_ge(S["vc_ps"], 4)
                    n = cross.tiles[-1][1]
                    chain(dve.tensor_tensor(v_f[-1][0:n, 12, :], vc_bank[3][0:n, 0:P], W_sb["bv_c"][0:n, 0:P], ALU.add))
                    if with_self:
                        dve.wait_ge(S["vs_ps"], 1)
                        chain(dve.tensor_tensor(v_f[0][:, :, :].rearrange("p t n -> p (t n)"), vs_ps,
                                                W_sb["bv_s"][:, 0:2 * P], ALU.add))
                    dve.wait_ge(S["qk"], 1)
                    dve.tensor_copy(parts[:, 0, :], qk[:, :]).then_inc(S["part0"], 1)
                    dve.wait_ge(S["left"], 1)
                    dve.tensor_copy(parts[:, 1, :], qk[:, :]).then_inc(S["part1"], 1)
                    for vf, vp in zip(v_f, v_parts):
                        v = vf[:, :, :].rearrange("p t (h d) -> p (t h) d", d=8)
                        p = vp[:, :, :, :].rearrange("p t h d -> p (t h) d")
                        chain(dve.tensor_copy(p[:, :, 0:8], v))
                        chain(dve.tensor_tensor(v, v, p[:, :, 0:8], ALU.subtract))
                        chain(dve.tensor_copy(p[:, :, 8:16], v))
                        ins = dve.tensor_tensor(p[:, :, 16:24], v, p[:, :, 8:16], ALU.subtract)
                        if vf is v_f[-1]:
                            ins.then_inc(S["v_all"], 1)
                    for s in sources:
                        core_dve(dve, S, A, s, chain)
                    for t in range(QT):
                        ins = dve.tensor_tensor(x_sb[:, t, :], x_sb[:, t, :], W_sb["b_out"][:, :], ALU.add)
                    chain(ins)
                    tail_dve(dve, S, A, 2 * ns)
                    dve.tensor_tensor(xn[:, :, :].rearrange("p t c -> p (t c)"), A.bank[3][:, 0:TOK],
                                      x_sb[:, :, :].rearrange("p t c -> p (t c)"), ALU.add).then_inc(S["res"], 1)
                    S.end_iteration(dve, "dve")

            @block.gpsimd
            def _(pool):
                with pool.Fori(0, BATCH) as b:
                    ln_rstd(pool, S, L, 0, QT)
                    pool.wait_ge(S["part0"], 1)
                    pool.tensor_tensor(qk[:, :], qk[:, :], parts[:, 0, :], ALU.subtract).then_inc(S["left"], 1)
                    pool.wait_ge(S["part1"], 1)
                    pool.tensor_tensor(parts[:, 2, :], qk[:, :], parts[:, 1, :], ALU.subtract).then_inc(S["part2"], 1)
                    for s in sources:
                        core_pool(pool, S, A, s)
                    S.end_iteration(pool, "pool")



D32 = 32
V_COLS = 3 * D32 + 1


def attention32(nc, G, stage, x_in, x1_out, x_out, w, own_keys):
    nk, cy = (TOK, C) if own_keys else (NKEY, CC)
    s, = make_sources([(nk, "after" if own_keys else None)])
    with ExitStack() as ctx:
        sb = Mem(nc, ctx, stage)
        A = Core(G, sb, V_COLS, HEADS, D32 ** -0.5)
        A.quads, A.spread = QUADS, G.spread32
        x_sb = sb("x", [P, QT, C])
        x1 = sb("x1", [P, QT, C]) if own_keys else x_sb
        xn = sb("xn", [P, QT, C])
        xqT = sb("xqT", [C, TOK])
        yT = sb("yT", [cy, nk])
        q_f, q_b = sb("q_f", [P, QUADS, 4, TOK]), sb("q_b", [P, QUADS, 4, TOK], BF16)
        k_f, k_b = sb("k_f", [P, QUADS, nk]), sb("k_b", [P, QUADS, nk], BF16)
        v_left = sb("v_left", [P, 2, HEADS * D32])
        v_parts = sb("v_parts", [P, s.T, HEADS, V_COLS], BF16)
        row_of = sb("row_of", [P, 4, P], BF16)
        names_w = ["wq", "wk", "wv", "w_out", "b_out", "lnx_g", "lnx_b", "lny_g", "lny_b"] + ["ln1_g", "ln1_b"] * own_keys
        W_sb = {n: sb(n, list(w[n].shape)) for n in names_w}
        row_of_f = sb("row_of_f", [P, 4, P])
        A.negmax_row = sb("negmax_rows", [P, 2, TOK], BF16)
        if own_keys:
            A.kept = sb("kept", [P, P_BUFS, 4 * TOK])
            A.kept_rest = sb("kept_rest", [P, P_BUFS, 4 * TOK], BF16)
            ones_col = sb("ones_col", [P, V_COLS], BF16)
            L = LnMem(sb, QT)
        else:
            ctx_sb = sb("ctx", [P, s.T, CC])
            L = LnMem(sb, s.T)

        S = Sems(nc, ctx, stage, ["x_in", "ctx_in", "x1", "x1_out", "xn", "yn", "ring_ps", "ring", "v_ps", "v_left",
                                  "v_mid", "v_parts", "qk_b", "res", "x_out", "dve_own"] + LN_SEMS + CORE_SEMS)

        def prepare(pool, chain):
            chain(pool.memset(v_parts[:, :, :, 3 * D32:V_COLS], 0.0 if own_keys else 1.0))
            if own_keys:
                chain(pool.memset(ones_col[:, 0:3 * D32], 0.0))
                chain(pool.memset(ones_col[:, 3 * D32:V_COLS], 1.0))
            else:
                chain(pool.memset(ctx_sb[:, :, :], 0.0))
            chain(pool.memset(A.negmax_row[:, :, :], 0.0))
            chain(pool.memset(q_f[:, :, :, :], 0.0))
            L.prepare(pool, chain)

        load_weights(nc, ctx, stage, [(W_sb[n][...], w[n]) for n in names_w] + [(row_of_f[:, :, :], G.row_of)], prepare)
        with nc.Block() as block:
            @block.vector
            def _(dve):
                dve.tensor_copy(row_of[:, :, :], row_of_f[:, :, :])

        A.w_out = lambda k: W_sb["w_out"][:, k, :]
        A.q_max = lambda s, g, h, qt: q_b[:, g, h, qt * P:(qt + 1) * P]
        A.k_max = lambda s, g, h, c0, n: k_b[:, g, c0:c0 + n]
        A.wait_max = lambda pe, quad: pe.wait_ge(S["max_ready"], quad + 1)

        def scores(pe, out, s, g, h, k0, n):
            pe.matmul(out, k_f[:, g, k0:k0 + n], q_f[:, g, h, :], start=True, stop=False)
            return pe.matmul(out, row_of[:, h, 0:n], A.negmax_row[:, g % 2, :], start=False, stop=True)

        def wait_out(pe, quad):
            if quad >= 1:
                pe.wait_ge(S["heads_out"], quad)

        def pv(pe, s, g, t, b):
            n = s.tiles[t][1]
            for h in range(4):
                out = A.bank[h % 2][0:V_COLS, h // 2 * TOK:(h // 2 + 1) * TOK]
                v, last = v_parts[0:n, t, 4 * g + h, :], t == s.T - 1
                opens = t == 0 and h // 2 == 0
                if own_keys:
                    pe.matmul(out, ones_col[0:n, :], A.high(A.probs, b, n)[:, A.place(h)], start=opens, stop=False,
                              skip_group_check=True)
                    pe.matmul(out, ones_col[0:n, :], A.rest[0:n, b, A.place(h)], start=False, stop=False,
                              skip_group_check=True)
                    high, rest, opens = A.high(A.kept, b, n), A.kept_rest, False
                else:
                    high, rest = A.high(A.probs, b, n), A.rest
                pe.matmul(out, v, high[:, A.place(h)], start=opens, stop=False, skip_group_check=True)
                ins = pe.matmul(out, v, rest[0:n, b, A.place(h)], start=False, stop=last, skip_group_check=True)
            return ins

        def take_out(act, quad):
            for a in range(2):
                ins = act.activation(A.heads[:, 4 * quad + a:4 * quad + 4:2, :],
                                     A.bank[a][0:V_COLS, :].rearrange("p (h q) -> p h q", h=2), ACT.Copy)
            return ins

        A.scores, A.wait_out, A.pv, A.take_out = scores, wait_out, pv, take_out

        ring = []
        if not own_keys:
            ring += [("ctx", t, min(t + 4, s.T)) for t in range(0, s.T, 4)]
        ring += [("x", 0, 0)] + [("q", g, 0) for g in range(QUADS)]
        ring += [("k", g, c) for g in range(QUADS) for c in range(len(s.chunks))]
        after_x = ring.index(("x", 0, 0)) + 1
        ring_bank = [A.S4[:, a, c, :] for a in range(2) for c in range(2)]

        with nc.Block() as block:
            @block.sync
            def _(sp):
                with sp.Fori(0, BATCH) as b:
                    sp.dma_start(x_sb[:, :, :], x_in[b].rearrange("(t p) c -> p t c", p=P)).then_inc(S["x_in"], 16)
                    if own_keys:
                        sp.wait_ge(S["x1"], 1)
                        sp.dma_start(x1_out[b].rearrange("(t p) c -> p t c", p=P), x1[:, :, :]).then_inc(S["x1_out"], 16)
                        sp.wait_ge(S["x1_out"], 16)
                    else:
                        full = nk // P * P
                        sp.dma_start(ctx_sb[:, 0:nk // P, :],
                                     G.ctx[b, 0:full].rearrange("(t p) c -> p t c", p=P)).then_inc(S["ctx_in"], 16)
                        sp.dma_start(ctx_sb[0:nk - full, nk // P, :], G.ctx[b, full:nk]).then_inc(S["ctx_in"], 16)
                    sp.wait_ge(S["res"], 1)
                    sp.dma_start(x_out[b].rearrange("(t p) c -> p t c", p=P), xn[:, :, :]).then_inc(S["x_out"], 16)
                    sp.wait_ge(S["x_out"], 16)
                    S.next_iteration(sp)

            @block.tensor
            def _(pe):
                with pe.Fori(0, BATCH) as b:
                    if not own_keys:
                        pe.wait_ge(S["yn"], 1)
                    for i, (what, g, c) in enumerate(ring):
                        bank = ring_bank[i % 4]
                        if i >= 4:
                            pe.wait_ge(S["ring"], i - 3)
                        if i == after_x:
                            pe.wait_ge(S["ring"], after_x)
                        if what == "ctx":
                            for t in range(g, c):
                                k0, n = s.tiles[t]
                                ins = pe.transpose(bank[0:CC, (t - g) * P:(t - g) * P + n], ctx_sb[0:n, t, :],
                                                   A.ident[0:n, 0:n])
                        if what == "x":
                            pe.wait_ge(S["xn"], 1)
                            for t in range(QT):
                                ins = pe.transpose(bank[:, t * P:(t + 1) * P], xn[:, t, :], A.ident[:, :])
                        if what == "q":
                            ins = pe.matmul(bank[:, 0:TOK], W_sb["wq"][:, g * P:(g + 1) * P], xqT[:, :], start=True, stop=True)
                        if what == "k":
                            c0, n = s.chunks[c]
                            ins = pe.matmul(bank[:, 0:n], W_sb["wk"][:, g * P:(g + 1) * P], yT[:, c0:c0 + n],
                                            start=True, stop=True)
                        ins.then_inc(S["ring_ps"], 1)
                    for t, (k0, n) in enumerate(s.tiles):
                        if t >= 4:
                            pe.wait_ge(S["v_left"], t - 3)
                        pe.matmul(A.bank[t % 4][0:n, :], yT[:, k0:k0 + n], W_sb["wv"][:, :],
                                  start=True, stop=True).then_inc(S["v_ps"], 1)
                    pe.wait_ge(S["ring"], len(ring))
                    pe.wait_ge(S["qk_b"], 2)
                    pe.wait_ge(S["v_parts"], s.T)
                    core_pe(pe, S, A, s)
                    tail_pe(pe, S, A, HEADS // 2)
                    S.end_iteration(pe, "pe")

            @block.scalar
            def _(act):
                with act.Fori(0, BATCH) as b:
                    for i, (what, g, c) in enumerate(ring):
                        bank = ring_bank[i % 4]
                        act.wait_ge(S["ring_ps"], i + 1)
                        if what == "ctx":
                            k0 = g * P
                            n = s.tiles[c - 1][0] + s.tiles[c - 1][1] - k0
                            ins = act.activation(yT[:, k0:k0 + n], bank[0:CC, 0:n], ACT.Identity,
                                                 bias=W_sb["lny_b"][:, 0:1], scale=W_sb["lny_g"][:, 0:1])
                        if what == "x":
                            if own_keys:
                                act.activation(yT[:, :], bank[:, 0:TOK], ACT.Identity, bias=W_sb["lny_b"][:, 0:1],
                                               scale=W_sb["lny_g"][:, 0:1])
                            ins = act.activation(xqT[:, :], bank[:, 0:TOK], ACT.Identity, bias=W_sb["lnx_b"][:, 0:1],
                                                 scale=W_sb["lnx_g"][:, 0:1])
                        if what == "q":
                            for h in range(4):
                                r = slice(D32 * h, D32 * h + D32)
                                ins = act.activation(q_f[r, g, h, :], bank[r, 0:TOK], ACT.Copy)
                        if what == "k":
                            c0, n = s.chunks[c]
                            ins = act.activation(k_f[:, g, c0:c0 + n], bank[:, 0:n], ACT.Copy)
                        ins.then_inc(S["ring"], 1)
                    core_act(act, S, A, s)
                    S.end_iteration(act, "act")

            @block.vector
            def _(dve):
                with dve.Fori(0, BATCH) as b:
                    chain = Chain(dve, S["dve_own"])
                    L.begin(chain)
                    if not own_keys:
                        dve.wait_ge(S["ctx_in"], 32)
                        ctx_tiles = [ctx_sb[0:n, t, :] for t, (_, n) in enumerate(s.tiles)]
                        ln_stats(dve, S, L, ctx_tiles)
                        for t, tile in enumerate(ctx_tiles):
                            ins = ln_apply(dve, L, t, tile, tile)
                        ins.then_inc(S["yn"], 1)
                    dve.wait_ge(S["x_in"], 16)
                    tiles = lambda m: [m[:, t, :] for t in range(QT)]
                    if own_keys:
                        ln_stats(dve, S, L, tiles(x_sb))
                        for t in range(QT):
                            ins = ln_apply(dve, L, t, x_sb[:, t, :], x_sb[:, t, :])
                        chain(ins)
                        ln_stats(dve, S, L, tiles(x_sb))
                        for t in range(QT):
                            ins = ln_apply(dve, L, t, x1[:, t, :], x_sb[:, t, :])
                        chain(ins)
                        for t in range(QT):
                            ins = dve.tensor_tensor(x1[:, t, :], x1[:, t, :], W_sb["ln1_g"][:, :], ALU.mult)
                        chain(ins)
                        for t in range(QT):
                            ins = dve.tensor_tensor(x1[:, t, :], x1[:, t, :], W_sb["ln1_b"][:, :], ALU.add)
                        ins.then_inc(S["x1"], 1)
                        dve.wait_ge(S["x1"], 1)
                    ln_stats(dve, S, L, tiles(x1))
                    for t in range(QT):
                        ins = ln_apply(dve, L, t, xn[:, t, :], x1[:, t, :])
                    ins.then_inc(S["xn"], 1)
                    for t, (_, n) in enumerate(s.tiles):
                        dve.wait_ge(S["v_ps"], t + 1)
                        if t >= 2:
                            dve.wait_ge(S["v_parts"], t - 1)
                        first = v_parts[0:n, t, :, 0:D32]
                        v = A.bank[t % 4][0:n, :].rearrange("p (h d) -> p h d", d=D32)
                        chain(dve.tensor_copy(first, v))
                        dve.tensor_tensor(v_left[0:n, t % 2, :].rearrange("p (h d) -> p h d", d=D32), v, first,
                                          ALU.subtract).then_inc(S["v_left"], 1)
                    dve.wait_ge(S["ring"], len(ring))
                    dve.tensor_copy(q_b[:, :, :, :], q_f[:, :, :, :]).then_inc(S["qk_b"], 1)
                    dve.tensor_copy(k_b[:, :, :], k_f[:, :, :]).then_inc(S["qk_b"], 1)
                    core_dve(dve, S, A, s, chain)
                    for t in range(QT):
                        ins = dve.tensor_tensor(x_sb[:, t, :], x1[:, t, :], W_sb["b_out"][:, :], ALU.add)
                    chain(ins)
                    tail_dve(dve, S, A, HEADS // 2)
                    dve.tensor_tensor(xn[:, :, :].rearrange("p t c -> p (t c)"), A.bank[3][:, 0:TOK],
                                      x_sb[:, :, :].rearrange("p t c -> p (t c)"), ALU.add).then_inc(S["res"], 1)
                    S.end_iteration(dve, "dve")

            @block.gpsimd
            def _(pool):
                with pool.Fori(0, BATCH) as b:
                    if own_keys:
                        for k in range(3):
                            ln_rstd(pool, S, L, k, QT)
                    else:
                        ln_rstd(pool, S, L, 0, s.T)
                        ln_rstd(pool, S, L, 1, QT)
                    for t, (_, n) in enumerate(s.tiles):
                        pool.wait_ge(S["v_left"], t + 1)
                        left = v_left[0:n, t % 2, :].rearrange("p (h d) -> p h d", d=D32)
                        second = v_parts[0:n, t, :, D32:2 * D32]
                        pool.tensor_copy(second, left).then_inc(S["v_mid"], 1)
                        pool.wait_ge(S["v_mid"], t + 1)
                        pool.tensor_tensor(v_parts[0:n, t, :, 2 * D32:3 * D32], left, second,
                                           ALU.subtract).then_inc(S["v_parts"], 1)
                        pool.wait_ge(S["v_parts"], t + 1)
                    core_pool(pool, S, A, s)
                    S.end_iteration(pool, "pool")



def token_tiles(x):
    return x.rearrange("b t c -> (b t) c").rearrange("(s t p) c -> s p t c", t=FT, p=P)


class Banks:

    def __init__(self, G):
        self.all = [G.S4[:, a, c, :] for a in range(2) for c in range(2)] + [b[:, :] for b in G.bank]


def flat(t):
    return t.rearrange("p t c -> p (t c)")


def transpose_tiles(pe, bank, tiles, ident):
    for t, tile in enumerate(tiles):
        ins = pe.transpose(bank[0:tile.shape[1], t * P:(t + 1) * P], tile, ident[:, :])
    return ins


def mlp32(nc, G, stage, xo_in, skip_in, add_in, out, w, last_ln):
    KH = w["li2_w"].shape[1] // P
    with ExitStack() as ctx:
        sb = Mem(nc, ctx, stage)
        banks = Banks(G).all
        names_w = ["li2_w", "li2_b", "li3_w", "li3_b", "ln3_g", "ln3_b"] + ["ln2_g", "ln2_b"] * last_ln
        W_sb = {n: sb(n, list(w[n].shape)) for n in names_w}
        xo, skip, add, xn = (sb(n, [P, FT, C]) for n in ("xo", "skip", "add", "xn"))
        nT = sb("nT", [C, FTOK])
        hT = sb("hT", [P, KH, FTOK])
        L = LnMem(sb, FT)
        S = Sems(nc, ctx, stage, ["xo_in", "skip_in", "add_in", "xn", "xnT_ps", "nT", "h_ps", "h", "y_ps", "res",
                                  "x_out", "dve_own"] + LN_SEMS)
        load_weights(nc, ctx, stage, [(W_sb[n][...], w[n]) for n in names_w], L.prepare)

        with nc.Block() as block:
            @block.sync
            def _(sp):
                with sp.Fori(0, FSTEPS) as i:
                    sp.dma_start(xo[:, :, :], token_tiles(xo_in)[i]).then_inc(S["xo_in"], 16)
                    sp.dma_start(skip[:, :, :], token_tiles(skip_in)[i]).then_inc(S["skip_in"], 16)
                    if not last_ln:
                        sp.dma_start(add[:, :, :], token_tiles(add_in)[i]).then_inc(S["add_in"], 16)
                    sp.wait_ge(S["res"], 1)
                    sp.dma_start(token_tiles(out)[i], xn[:, :, :]).then_inc(S["x_out"], 16)
                    sp.wait_ge(S["x_out"], 16)
                    S.next_iteration(sp)

            @block.tensor
            def _(pe):
                with pe.Fori(0, FSTEPS) as i:
                    pe.wait_ge(S["xn"], 1)
                    transpose_tiles(pe, banks[4], [xn[:, t, :] for t in range(FT)], G.ident).then_inc(S["xnT_ps"], 1)
                    pe.wait_ge(S["nT"], 1)
                    for k in range(KH):
                        pe.matmul(banks[k], W_sb["li2_w"][:, k * P:(k + 1) * P], nT[:, :],
                                  start=True, stop=True).then_inc(S["h_ps"], 1)
                    pe.wait_ge(S["h"], KH)
                    for t in range(FT):
                        for k in range(KH):
                            ins = pe.matmul(banks[5][:, t * C:(t + 1) * C], hT[:, k, t * P:(t + 1) * P],
                                            W_sb["li3_w"][:, k, :], start=(k == 0), stop=(k == KH - 1))
                    ins.then_inc(S["y_ps"], 1)
                    S.end_iteration(pe, "pe")

            @block.scalar
            def _(act):
                with act.Fori(0, FSTEPS) as i:
                    act.wait_ge(S["xnT_ps"], 1)
                    act.activation(nT[:, :], banks[4], ACT.Identity, bias=W_sb["ln3_b"][:, 0:1],
                                   scale=W_sb["ln3_g"][:, 0:1]).then_inc(S["nT"], 1)
                    for k in range(KH):
                        act.wait_ge(S["h_ps"], k + 1)
                        act.activation(hT[:, k, :], banks[k], ACT.Gelu,
                                       bias=W_sb["li2_b"][:, k:k + 1]).then_inc(S["h"], 1)
                    S.end_iteration(act, "act")

            @block.vector
            def _(dve):
                with dve.Fori(0, FSTEPS) as i:
                    chain = Chain(dve, S["dve_own"])
                    L.begin(chain)
                    dve.wait_ge(S["xo_in"], 16)
                    ln_stats(dve, S, L, [xo[:, t, :] for t in range(FT)])
                    for t in range(FT):
                        ins = ln_apply(dve, L, t, xn[:, t, :], xo[:, t, :])
                    ins.then_inc(S["xn"], 1)
                    dve.wait_ge(S["skip_in"], 16)
                    chain(dve.tensor_tensor(flat(skip[:, :, :]), flat(skip[:, :, :]), flat(xo[:, :, :]), ALU.add))
                    for t in range(FT):
                        ins = dve.tensor_tensor(skip[:, t, :], skip[:, t, :], W_sb["li3_b"][:, :], ALU.add)
                    chain(ins)
                    if not last_ln:
                        dve.wait_ge(S["add_in"], 16)
                        chain(dve.tensor_tensor(flat(skip[:, :, :]), flat(skip[:, :, :]), flat(add[:, :, :]), ALU.add))
                    dve.wait_ge(S["y_ps"], 1)
                    if not last_ln:
                        dve.tensor_tensor(flat(xn[:, :, :]), flat(skip[:, :, :]), banks[5], ALU.add).then_inc(S["res"], 1)
                    else:
                        chain(dve.tensor_tensor(flat(skip[:, :, :]), flat(skip[:, :, :]), banks[5], ALU.add))
                        ln_stats(dve, S, L, [skip[:, t, :] for t in range(FT)])
                        for t in range(FT):
                            ins = ln_apply(dve, L, t, xn[:, t, :], skip[:, t, :])
                        chain(ins)
                        for t in range(FT):
                            ins = dve.tensor_tensor(xn[:, t, :], xn[:, t, :], W_sb["ln2_g"][:, :], ALU.mult)
                        chain(ins)
                        for t in range(FT):
                            ins = dve.tensor_tensor(xn[:, t, :], xn[:, t, :], W_sb["ln2_b"][:, :], ALU.add)
                        ins.then_inc(S["res"], 1)
                    S.end_iteration(dve, "dve")

            @block.gpsimd
            def _(pool):
                with pool.Fori(0, FSTEPS) as i:
                    for k in range(1 + last_ln):
                        ln_rstd(pool, S, L, k, FT)
                    S.end_iteration(pool, "pool")


def experts(nc, G, stage, x_in, out, w, kind):
    K_TOP = {"hash": 4, "top1": 1, "shared": 2}[kind]
    E = {"hash": 32, "top1": 8, "shared": 16}[kind]
    EG = E + (kind == "shared")
    NH = w["w_down"].shape[1]
    with ExitStack() as ctx:
        sb = Mem(nc, ctx, stage)
        banks = Banks(G).all
        names_w = {"hash": ["hasher", "keys", "scale"], "top1": ["gate", "ln_scale", "ln_bias", "b1", "b2"],
                   "shared": ["gate", "w_gate"]}[kind] + ["w_up", "w_down", "spread", "iota"]
        W_sb = {n: sb(n, list(w[n].shape)) for n in names_w}
        x, z = sb("x", [P, FT, C]), sb("z", [P, FT, C])
        res = sb("res", [P, FT, C])
        xh = sb("xh", [P, FT, C]) if kind == "top1" else None
        zT = sb("zT", [C, FTOK])
        xhT = sb("xhT", [C, FTOK]) if kind == "top1" else zT
        hashT = sb("hashT", [32, FTOK])
        logits = sb("logits", [P, FT, EG])
        best, best_f = sb("best", [P, FT, 8]), sb("best_f", [P, FT, 8])
        best_i = sb("best_i", [P, FT, 8], U32)
        weight = sb("weight", [P, FT, 8])
        total, inv = sb("total", [P, FT, 1]), sb("inv", [P, FT, 1])
        sig = sb("sig", [P, FT, 1])
        term = sb("term", [P, FT, E])
        gates = sb("gates", [P, FT, EG])
        gatesT = sb("gatesT", [EG, FTOK])
        act_out = sb("act_out", [P, NH, FTOK])
        hT = sb("hT", [P, NH, FTOK])
        L = LnMem(sb, FT)
        S = Sems(nc, ctx, stage, ["x_in", "z", "xh", "zT_ps", "zT", "hash_ps", "hash", "logits_ps", "logits", "best", "weight",
                                  "gates", "gT_ps", "gT", "up_ps", "act", "h", "y_ps", "res", "x_out",
                                  "dve_own"] + LN_SEMS)
        load_weights(nc, ctx, stage, [(W_sb[n][...], w[n]) for n in names_w], L.prepare)

        if kind == "top1":
            s_bias = ctx.enter_context(nc.semaphore(f"{stage}_bias"))
            HID = NH * P // E
            with nc.Block() as block:
                @block.tensor
                def _(pe):
                    for e in range(E):
                        r = e % (P // HID) * HID
                        ins = pe.matmul(banks[0][r:r + HID, e // (P // HID):e // (P // HID) + 1],
                                        W_sb["w_up"][:, e * HID:(e + 1) * HID], W_sb["ln_bias"][:, e:e + 1],
                                        start=True, stop=True)
                    ins.then_inc(s_bias, 1)

                @block.vector
                def _(dve):
                    dve.wait_ge(s_bias, 1)
                    dve.sem_clear(s_bias)
                    dve.tensor_tensor(W_sb["b1"][:, :], W_sb["b1"][:, :], banks[0][:, 0:NH], ALU.add)
                    for e in range(E):
                        w1 = W_sb["w_up"][:, e * HID:(e + 1) * HID]
                        dve.tensor_scalar(w1, w1, W_sb["ln_scale"][:, e:e + 1], None, ALU.mult)

        gate_w = W_sb["gate"] if kind != "hash" else None
        per_tile = 3 if kind == "shared" else 2

        def tile_banks(k):
            return [banks[2 + (k % 2) * per_tile + j] for j in range(per_tile)]

        def has_own_gate(k):
            return kind == "shared"

        with nc.Block() as block:
            @block.sync
            def _(sp):
                with sp.Fori(0, FSTEPS) as i:
                    sp.dma_start(x[:, :, :], token_tiles(x_in)[i]).then_inc(S["x_in"], 16)
                    sp.wait_ge(S["res"], 1)
                    sp.dma_start(token_tiles(out)[i], res[:, :, :]).then_inc(S["x_out"], 16)
                    sp.wait_ge(S["x_out"], 16)
                    S.next_iteration(sp)

            @block.tensor
            def _(pe):
                with pe.Fori(0, FSTEPS) as i:
                    pe.wait_ge(S["z"], 1)
                    transpose_tiles(pe, banks[0], [z[:, t, :] for t in range(FT)], G.ident).then_inc(S["zT_ps"], 1)
                    pe.wait_ge(S["zT"], 1)
                    keys, keyed = gate_w, zT
                    if kind == "hash":
                        pe.matmul(banks[0][0:32, :], W_sb["hasher"][:, :], zT[:, :], start=True, stop=True).then_inc(S["hash_ps"], 1)
                        pe.wait_ge(S["hash"], 1)
                        keys, keyed = W_sb["keys"], hashT
                    for t in range(FT):
                        ins = pe.matmul(banks[1][:, t * EG:(t + 1) * EG], keyed[:, t * P:(t + 1) * P], keys[:, :],
                                        start=True, stop=True)
                    ins.then_inc(S["logits_ps"], 1)
                    if kind == "top1":
                        pe.wait_ge(S["xh"], 1)
                        transpose_tiles(pe, banks[0], [xh[:, t, :] for t in range(FT)], G.ident).then_inc(S["zT_ps"], 1)
                        pe.wait_ge(S["zT"], 2)
                    pe.wait_ge(S["gates"], 1)
                    transpose_tiles(pe, banks[0], [gates[:, t, :] for t in range(FT)], G.ident).then_inc(S["gT_ps"], 1)
                    pe.wait_ge(S["gT"], 1)
                    for k in range(NH):
                        tb = tile_banks(k)
                        cols = slice(k * P, (k + 1) * P)
                        if k >= 2:
                            pe.wait_ge(S["act"], k - 1)
                            pe.wait_ge(S["h"], k - 1)
                        pe.matmul(tb[0], W_sb["w_gate" if kind == "shared" else "w_up"][:, cols], xhT[:, :],
                                  start=True, stop=True)
                        if kind == "shared":
                            pe.matmul(tb[2], W_sb["w_up"][:, cols], zT[:, :], start=True, stop=True)
                        pe.matmul(tb[1], W_sb["spread"][:, cols], gatesT[:, :], start=True, stop=True).then_inc(S["up_ps"], 1)
                    pe.wait_ge(S["h"], NH)
                    for t in range(FT):
                        o = banks[1][:, t * C:(t + 1) * C]
                        if kind == "top1":
                            pe.matmul(o, gatesT[:, t * P:(t + 1) * P], W_sb["b2"][:, :], start=True, stop=False)
                        for k in range(NH):
                            ins = pe.matmul(o, hT[:, k, t * P:(t + 1) * P], W_sb["w_down"][:, k, :],
                                            start=(k == 0 and kind != "top1"), stop=(k == NH - 1))
                    ins.then_inc(S["y_ps"], 1)
                    S.end_iteration(pe, "pe")

            @block.scalar
            def _(act):
                with act.Fori(0, FSTEPS) as i:
                    act.wait_ge(S["zT_ps"], 1)
                    act.activation(zT[:, :], banks[0], ACT.Copy).then_inc(S["zT"], 1)
                    if kind == "hash":
                        act.wait_ge(S["hash_ps"], 1)
                        act.activation(hashT[:, :], banks[0][0:32, :], ACT.Copy).then_inc(S["hash"], 1)
                    if kind == "top1":
                        act.wait_ge(S["zT_ps"], 2)
                        act.activation(xhT[:, :], banks[0], ACT.Copy).then_inc(S["zT"], 1)
                    if kind != "top1":
                        act.wait_ge(S["best"], 1)
                        ins = act.activation(weight[:, :, :], best[:, :, :], ACT.Exp)
                        if kind == "shared":
                            ins = act.activation(sig[:, :, :], logits[:, :, E:EG], ACT.Exp, scale=-1.0)
                        ins.then_inc(S["weight"], 1)
                    act.wait_ge(S["gT_ps"], 1)
                    act.activation(gatesT[:, :], banks[0][0:EG, :], ACT.Copy).then_inc(S["gT"], 1)
                    for k in range(NH):
                        act.wait_ge(S["up_ps"], k + 1)
                        if kind == "top1":
                            ins = act.activation(act_out[:, k, :], tile_banks(k)[0], ACT.Gelu, bias=W_sb["b1"][:, k:k + 1])
                        else:
                            ins = act.activation(act_out[:, k, :], tile_banks(k)[0], ACT.Silu)
                        ins.then_inc(S["act"], 1)
                    S.end_iteration(act, "act")

            @block.vector
            def _(dve):
                with dve.Fori(0, FSTEPS) as i:
                    chain = Chain(dve, S["dve_own"])
                    L.begin(chain)
                    dve.wait_ge(S["x_in"], 16)
                    ln_stats(dve, S, L, [x[:, t, :] for t in range(FT)])
                    for t in range(FT):
                        ins = ln_apply(dve, L, t, z[:, t, :], x[:, t, :])
                    ins.then_inc(S["z"], 1)
                    dve.wait_ge(S["z"], 1)
                    if kind == "top1":
                        ln_stats(dve, S, L, [z[:, t, :] for t in range(FT)])
                        for t in range(FT):
                            ins = ln_apply(dve, L, t, xh[:, t, :], z[:, t, :])
                        ins.then_inc(S["xh"], 1)
                    dve.wait_ge(S["logits_ps"], 1)
                    chain(dve.tensor_copy(flat(logits[:, :, :]), banks[1][:, 0:FT * EG]))
                    for t in range(FT):
                        ins = dve.max(best[:, t, :], logits[:, t, 0:E])
                    chain(ins)
                    for t in range(FT):
                        ins = dve.max_index(best_i[:, t, :], best[:, t, :], logits[:, t, 0:E])
                    chain(ins)
                    chain(dve.tensor_copy(best_f[:, :, :], best_i[:, :, :]))
                    if kind == "top1":
                        for t in range(FT):
                            ins = dve.tensor_scalar(gates[:, t, :], W_sb["iota"][:, :], best_f[:, t, 0:1], None, ALU.is_equal)
                        ins.then_inc(S["gates"], 1)
                    else:
                        chain(dve.tensor_copy(total[:, :, :], best[:, :, 0:1]))
                        for t in range(FT):
                            ins = dve.tensor_scalar(best[:, t, :], best[:, t, :], total[:, t, :], None, ALU.subtract)
                        ins.then_inc(S["best"], 1)
                        dve.wait_ge(S["weight"], 1)
                        chain(dve.tensor_reduce(total[:, :, :], weight[:, :, 0:K_TOP], AX.X, ALU.add))
                        chain(dve.reciprocal(inv[:, :, :], total[:, :, :]))
                        for t in range(FT):
                            ins = dve.tensor_scalar(weight[:, t, :], weight[:, t, :], inv[:, t, :], None, ALU.mult)
                        chain(ins)
                        for k in range(K_TOP):
                            for t in range(FT):
                                ins = dve.tensor_scalar(gates[:, t, 0:E] if k == 0 else term[:, t, :], W_sb["iota"][:, :],
                                                        best_f[:, t, k:k + 1], weight[:, t, k:k + 1], ALU.is_equal, ALU.mult)
                            chain(ins)
                            if k:
                                chain(dve.tensor_tensor(gates[:, :, 0:E], gates[:, :, 0:E], term[:, :, :], ALU.add))
                        if kind == "shared":
                            chain(dve.tensor_scalar(sig[:, :, :], sig[:, :, :], 1.0, None, ALU.add))
                            chain(dve.reciprocal(gates[:, :, E:EG], sig[:, :, :]))
                        dve.tensor_copy(total[:, :, :], inv[:, :, :]).then_inc(S["gates"], 1)
                    for k in range(NH):
                        dve.wait_ge(S["act"], k + 1)
                        tb = tile_banks(k)
                        if kind == "shared":
                            chain(dve.tensor_tensor(act_out[:, k, :], act_out[:, k, :], tb[2], ALU.mult))
                        dve.tensor_tensor(hT[:, k, :], act_out[:, k, :], tb[1], ALU.mult).then_inc(S["h"], 1)
                    if kind == "hash":
                        chain(dve.tensor_tensor(flat(x[:, :, :]), flat(x[:, :, :]), flat(z[:, :, :]), ALU.add))
                    dve.wait_ge(S["y_ps"], 1)
                    if kind == "hash":
                        ins = dve.scalar_tensor_tensor(out=flat(res[:, :, :]), in0=banks[1], scalar=W_sb["scale"][:, 0:1],
                                                       in1=flat(x[:, :, :]), op0=ALU.mult, op1=ALU.add)
                    else:
                        ins = dve.tensor_tensor(flat(res[:, :, :]), banks[1], flat(x[:, :, :]), ALU.add)
                    ins.then_inc(S["res"], 1)
                    S.end_iteration(dve, "dve")

            @block.gpsimd
            def _(pool):
                with pool.Fori(0, FSTEPS) as i:
                    for k in range(1 + (kind == "top1")):
                        ln_rstd(pool, S, L, k, FT)
                    S.end_iteration(pool, "pool")


ROUND = 1.5 * 2.0 ** 23


def bit_ffn(nc, G, stage, x_in, out, w):
    KH = w["w1"].shape[1] // P
    NB = FTOK // TOK
    with ExitStack() as ctx:
        sb = Mem(nc, ctx, stage)
        banks = Banks(G).all
        W_sb = {n: sb(n, list(w[n].shape)) for n in ("w1", "w2", "conv_w", "conv_b")}
        x, z, res = (sb(n, [P, FT, C]) for n in ("x", "z", "res"))
        top, unit, per = (sb(n, [P, FT, 1]) for n in ("top", "unit", "per"))
        zT = sb("zT", [C, FTOK])
        hp = sb("hp", [P, KH, NB, TOK + 2])
        cv = sb("cv", [P, KH, NB, TOK])
        sT = sb("sT", [P, KH, FTOK])
        s_tok = sb("s_tok", [P, FT, KH * P])
        ones = sb("ones", [P, P])
        wsum, wall, wstep, wper = (sb(n, [P, 2]) for n in ("wsum", "wall", "wstep", "wper"))
        L = LnMem(sb, FT)
        S = Sems(nc, ctx, stage, ["x_in", "z", "zT_ps", "zT", "h_ps", "hp", "cv", "sT", "st_ps", "s_tok", "sq", "sqT_ps",
                                  "sqT", "y_ps", "res", "x_out", "dve_own"] + LN_SEMS)

        def prepare(pool, chain):
            chain(pool.memset(hp[:, :, :, :], 0.0))
            chain(pool.memset(ones[:, :], 1.0))
            L.prepare(pool, chain)

        load_weights(nc, ctx, stage, [(W_sb[n][...], w[n]) for n in W_sb], prepare)

        s_sum, s_all = (ctx.enter_context(nc.semaphore(f"{stage}_{n}")) for n in ("wsum", "wall"))
        s_own = ctx.enter_context(nc.semaphore(f"{stage}_wown"))
        with nc.Block() as block:
            @block.tensor
            def _(pe):
                pe.wait_ge(s_sum, 1)
                pe.sem_clear(s_sum)
                pe.matmul(banks[0][:, 0:2], ones[:, :], wsum[:, :], start=True, stop=True).then_inc(s_all, 1)

            @block.vector
            def _(dve):
                chain = Chain(dve, s_own)
                both = [W_sb["w1"][:, :], W_sb["w2"][:, :, :].rearrange("p k c -> p (k c)")]
                for j, m in enumerate(both):
                    ins = dve.tensor_reduce(wsum[:, j:j + 1], m, AX.X, ALU.add, apply_absolute_value=True)
                ins.then_inc(s_sum, 1)
                dve.wait_ge(s_all, 1)
                dve.sem_clear(s_all)
                chain(dve.tensor_scalar(wper[:, :], banks[0][:, 0:2], 1.0 / (KH * P * C), 1e-5, ALU.mult, ALU.max))
                chain(dve.reciprocal(wstep[:, :], wper[:, :]))
                for j, m in enumerate(both):
                    chain(dve.tensor_scalar(m, m, wstep[:, j:j + 1], ROUND, ALU.mult, ALU.add))
                    chain(dve.tensor_scalar(m, m, ROUND, 1.0, ALU.subtract, ALU.min))
                    chain(dve.tensor_scalar(m, m, -1.0, wper[:, j:j + 1], ALU.max, ALU.mult))
                dve.sem_clear(s_own)

        def quantise(dve, chain, tiles):
            for t, m in enumerate(tiles):
                ins = dve.tensor_reduce(top[:, t, :], m, AX.X, ALU.max, apply_absolute_value=True)
            chain(ins)
            chain(dve.tensor_scalar(top[:, :, :], top[:, :, :], 1e-5, None, ALU.max))
            chain(dve.reciprocal(unit[:, :, :], top[:, :, :]))
            chain(dve.tensor_scalar(unit[:, :, :], unit[:, :, :], 127.0, None, ALU.mult))
            chain(dve.reciprocal(per[:, :, :], unit[:, :, :]))
            for t, m in enumerate(tiles):
                ins = dve.tensor_scalar(m, m, unit[:, t, :], ROUND, ALU.mult, ALU.add)
            chain(ins)
            for t, m in enumerate(tiles):
                ins = dve.tensor_scalar(m, m, ROUND, 127.0, ALU.subtract, ALU.min)
            chain(ins)
            for t, m in enumerate(tiles):
                ins = dve.tensor_scalar(m, m, -128.0, per[:, t, :], ALU.max, ALU.mult)
            return ins

        with nc.Block() as block:
            @block.sync
            def _(sp):
                with sp.Fori(0, FSTEPS) as i:
                    sp.dma_start(x[:, :, :], token_tiles(x_in)[i]).then_inc(S["x_in"], 16)
                    sp.wait_ge(S["res"], 1)
                    sp.dma_start(token_tiles(out)[i], res[:, :, :]).then_inc(S["x_out"], 16)
                    sp.wait_ge(S["x_out"], 16)
                    S.next_iteration(sp)

            @block.tensor
            def _(pe):
                with pe.Fori(0, FSTEPS) as i:
                    pe.wait_ge(S["z"], 1)
                    transpose_tiles(pe, banks[4], [z[:, t, :] for t in range(FT)], G.ident).then_inc(S["zT_ps"], 1)
                    pe.wait_ge(S["zT"], 1)
                    for k in range(KH):
                        pe.matmul(banks[k], W_sb["w1"][:, k * P:(k + 1) * P], zT[:, :], start=True, stop=True).then_inc(S["h_ps"], 1)
                    pe.wait_ge(S["hp"], KH)
                    pe.wait_ge(S["sT"], KH)
                    for t in range(FT):
                        for k in range(KH):
                            ins = pe.transpose(banks[t][:, k * P:(k + 1) * P], sT[:, k, t * P:(t + 1) * P], G.ident[:, :])
                        ins.then_inc(S["st_ps"], 1)
                    pe.wait_ge(S["sq"], 1)
                    for k in range(KH):
                        for t in range(FT):
                            ins = pe.transpose(banks[4 + k][:, t * P:(t + 1) * P], s_tok[:, t, k * P:(k + 1) * P], G.ident[:, :])
                        ins.then_inc(S["sqT_ps"], 1)
                    pe.wait_ge(S["sqT"], KH)
                    for t in range(FT):
                        for k in range(KH):
                            ins = pe.matmul(banks[0][:, t * C:(t + 1) * C], sT[:, k, t * P:(t + 1) * P], W_sb["w2"][:, k, :],
                                            start=(k == 0), stop=(k == KH - 1))
                    ins.then_inc(S["y_ps"], 1)
                    S.end_iteration(pe, "pe")

            @block.scalar
            def _(act):
                with act.Fori(0, FSTEPS) as i:
                    act.wait_ge(S["zT_ps"], 1)
                    act.activation(zT[:, :], banks[4], ACT.Copy).then_inc(S["zT"], 1)
                    for k in range(KH):
                        act.wait_ge(S["h_ps"], k + 1)
                        act.activation(hp[:, k, :, 1:TOK + 1], banks[k].rearrange("p (b t) -> p b t", b=NB),
                                       ACT.Copy).then_inc(S["hp"], 1)
                    for k in range(KH):
                        act.wait_ge(S["cv"], k + 1)
                        act.activation(sT[:, k, :], cv[:, k, :, :].rearrange("p b t -> p (b t)"), ACT.Silu,
                                       bias=W_sb["conv_b"][:, k:k + 1]).then_inc(S["sT"], 1)
                    for t in range(FT):
                        act.wait_ge(S["st_ps"], t + 1)
                        act.activation(s_tok[:, t, :], banks[t], ACT.Copy).then_inc(S["s_tok"], 1)
                    for k in range(KH):
                        act.wait_ge(S["sqT_ps"], k + 1)
                        act.activation(sT[:, k, :], banks[4 + k], ACT.Copy).then_inc(S["sqT"], 1)
                    S.end_iteration(act, "act")

            @block.vector
            def _(dve):
                with dve.Fori(0, FSTEPS) as i:
                    chain = Chain(dve, S["dve_own"])
                    L.begin(chain)
                    dve.wait_ge(S["x_in"], 16)
                    ln_stats(dve, S, L, [x[:, t, :] for t in range(FT)])
                    for t in range(FT):
                        ins = ln_apply(dve, L, t, z[:, t, :], x[:, t, :])
                    chain(ins)
                    quantise(dve, chain, [z[:, t, :] for t in range(FT)]).then_inc(S["z"], 1)
                    for k in range(KH):
                        dve.wait_ge(S["hp"], k + 1)
                        chain(dve.tensor_scalar(cv[:, k, :, :], hp[:, k, :, 0:TOK], W_sb["conv_w"][:, k, 0:1], None, ALU.mult))
                        for j in (1, 2):
                            ins = dve.scalar_tensor_tensor(out=cv[:, k, :, :], in0=hp[:, k, :, j:j + TOK],
                                                           scalar=W_sb["conv_w"][:, k, j:j + 1], in1=cv[:, k, :, :],
                                                           op0=ALU.mult, op1=ALU.add)
                            if j == 1:
                                chain(ins)
                        ins.then_inc(S["cv"], 1)
                    dve.wait_ge(S["s_tok"], FT)
                    quantise(dve, chain, [s_tok[:, t, :] for t in range(FT)]).then_inc(S["sq"], 1)
                    dve.wait_ge(S["y_ps"], 1)
                    dve.tensor_tensor(flat(res[:, :, :]), banks[0], flat(x[:, :, :]), ALU.add).then_inc(S["res"], 1)
                    S.end_iteration(dve, "dve")

            @block.gpsimd
            def _(pool):
                with pool.Fori(0, FSTEPS) as i:
                    ln_rstd(pool, S, L, 0, FT)
                    S.end_iteration(pool, "pool")


def stages(nc, G, d, sub, out):
    def scratch(name):
        return nc.dram_tensor(f"{name}_dram", [BATCH, TOK, C], F32, kind="Internal").ap()

    x = [d["x"]] + [scratch(f"x_after_{i}") for i in range(7)] + [out]
    own_x1, own_xo, mid_x, cross_xo = (scratch(n) for n in ("own_x1", "own_xo", "mid_x", "cross_xo"))
    attention8(nc, G, "a0", x[0], x[1], sub("a0_"), True)
    experts(nc, G, "f0", x[1], x[2], sub("f0_"), "hash")
    attention8(nc, G, "a1", x[2], x[3], sub("a1_"), False)
    bit_ffn(nc, G, "f1", x[3], x[4], sub("f1_"))
    attention32(nc, G, "own", x[4], own_x1, own_xo, sub("own_"), True)
    mlp32(nc, G, "own_mlp", own_xo, own_x1, None, mid_x, sub("own_"), True)
    attention32(nc, G, "cross", mid_x, None, cross_xo, sub("cross_"), False)
    mlp32(nc, G, "cross_mlp", cross_xo, mid_x, x[4], x[5], sub("cross_"), False)
    experts(nc, G, "f2", x[5], x[6], sub("f2_"), "top1")
    attention8(nc, G, "a3", x[6], x[7], sub("a3_"), False)
    experts(nc, G, "f3", x[7], x[8], sub("f3_"), "shared")



class Globals:
    pass


def program(nc, d, out):
    with ExitStack() as ctx:
        G = Globals()
        G.S4 = ctx.enter_context(nc.psum_tensor("scores_ps", [P, 2, 2, 512], F32))
        G.bank = [ctx.enter_context(nc.psum_tensor(f"bank{i}", [P, 512], F32)) for i in range(4)]
        sb = Mem(nc, ctx, "shared")
        G.ident = sb("ident", [P, P])
        G.spread8 = sb("spread8", [P, P])
        G.spread32 = sb("spread32", [97, 97])
        G.past = sb("past", [P, QT, TOK])
        load_weights(nc, ctx, "shared", [(G.ident[:, :], d["ident"]), (G.spread8[:, :], d["spread8"]),
                                         (G.spread32[:, :], d["spread32"]), (G.past[:, :, :], d["past"])])
        G.ctxT, G.ctx = d["ctxT"], d["ctx_512"]
        G.row_of = d["row_of"]
        sub = lambda pre: {k[len(pre):]: v for k, v in d.items() if k.startswith(pre)}
        stages(nc, G, d, sub, out)



def layout(i):
    import numpy as np

    f = np.float32
    a = {"x": i["x"], "ctx_512": i["ctx_512"], "ctxT": i["ctx_512"].transpose(0, 2, 1)}
    a["ident"] = np.eye(P, dtype=f)
    r = np.arange(P)
    a["spread8"] = ((r[:, None] % 32 == 24) & (r[:, None] // 32 == r[None, :] // 32)).astype(f)
    a["spread32"] = np.repeat((np.arange(97) == 96).astype(f)[:, None], 97, axis=1)
    q = (np.arange(QT)[None, :, None] * P + r[:, None, None])
    a["past"] = np.where(np.arange(TOK)[None, None, :] <= q, f(0), f(-1e30)).astype(f)

    def rep(v, n=1):
        return np.broadcast_to(np.tile(v, n), (P, n * v.size))

    def col(v):
        return v.reshape(-1, 1) if v.size <= P else v.reshape(-1, P).T

    def out8(wo):
        o = np.zeros((P, QUADS, C), f)
        for g in range(QUADS):
            for h in range(4):
                for part in range(3):
                    r0 = 32 * h + 8 * part
                    o[r0:r0 + 8, g] = wo[(4 * g + h) * 8:(4 * g + h + 1) * 8]
        return o

    z = np.zeros(C, f)
    n = "L0_xattn_"
    a.update({"a0_wq_s": i[n + "Wq"], "a0_wk_s": i[n + "Wk"], "a0_wv_s": i[n + "Wv"], "a0_bq_s": col(i[n + "bq"]),
              "a0_bk_s": col(i[n + "bk"]), "a0_bv_s": rep(i[n + "bv"], 4),
              "a0_wq_c": i[n + "Wcq"], "a0_wk_c": i[n + "Wck"], "a0_wv_c": i[n + "Wcv"], "a0_bq_c": col(i[n + "bcq"]),
              "a0_bk_c": col(i[n + "bck"]), "a0_bv_c": rep(i[n + "bcv"], 4),
              "a0_w_out": out8(i[n + "Wp"]), "a0_b_out": rep(i[n + "bp"])})
    n = "L1_xattn_"
    a.update({"a1_wq_c": i[n + "Wq"].T, "a1_wk_c": i[n + "Wkv"][0:C].T, "a1_wv_c": i[n + "Wkv"][C:].T,
              "a1_bq_c": col(z), "a1_bk_c": col(z), "a1_bv_c": rep(z, 4),
              "a1_w_out": out8(i[n + "Wo"].T), "a1_b_out": rep(z)})
    n = "L3_xattn_"
    a.update({"a3_wq_c": i[n + "Wq"], "a3_wk_c": i[n + "Wk"], "a3_wv_c": i[n + "Wv"], "a3_bq_c": col(i[n + "bq"]),
              "a3_bk_c": col(i[n + "bk"]), "a3_bv_c": rep(i[n + "bv"], 4),
              "a3_w_out": out8(i[n + "Wo"]), "a3_b_out": rep(i[n + "bo"])})
    for stage, pre in (("own_", "L2_xattn_a1_"), ("cross_", "L2_xattn_a2_")):
        for m in "qkv":
            a[stage + "w" + m] = i[pre + "w" + m].transpose(1, 0, 2).reshape(i[pre + "w" + m].shape[1], -1)
        o = np.zeros((97, HEADS, C), f)
        for part in range(3):
            o[32 * part:32 * part + 32] = i[pre + "li1_w"].reshape(HEADS, 32, C).transpose(1, 0, 2)
        a.update({stage + "w_out": o, stage + "b_out": rep(i[pre + "li1_b"]),
                  stage + "li2_w": i[pre + "li2_w"], stage + "li2_b": col(i[pre + "li2_b"]),
                  stage + "li3_w": i[pre + "li3_w"].reshape(-1, P, C).transpose(1, 0, 2),
                  stage + "li3_b": rep(i[pre + "li3_b"])})
        for v in ("lnx", "lny", "ln3"):
            a[f"{stage}{v}_g"], a[f"{stage}{v}_b"] = col(i[f"{pre}{v}_g"]), col(i[f"{pre}{v}_b"])
    for v in ("ln1", "ln2"):
        a[f"own_{v}_g"], a[f"own_{v}_b"] = rep(i[f"L2_xattn_{v}_g"]), rep(i[f"L2_xattn_{v}_b"])
    a["row_of"] = np.broadcast_to(np.eye(P, dtype=f)[:, 0:4, None], (P, 4, P))

    def spread(experts, hidden):
        return np.repeat(np.eye(experts, dtype=f), hidden, axis=1)

    def iota(n):
        return np.broadcast_to(np.arange(n, dtype=f), (P, n))

    def down(v):
        return v.reshape(-1, P, C).transpose(1, 0, 2)

    n = "L0_ffn_"
    a.update({"f0_hasher": i[n + "hasher_w"].T, "f0_keys": i[n + "keys"].T,
              "f0_scale": np.broadcast_to(i[n + "scale"], (P, 1)),
              "f0_w_up": i[n + "values_down"].transpose(1, 0, 2).reshape(C, -1),
              "f0_w_down": down(i[n + "values_up"].reshape(-1, C)), "f0_spread": spread(32, 32), "f0_iota": iota(32)})
    n = "L1_ffn_"
    a.update({"f1_w1": i[n + "w1"].T, "f1_w2": down(i[n + "w2"].T),
              "f1_conv_w": i[n + "conv_w"].reshape(-1, P, 3).transpose(1, 0, 2), "f1_conv_b": col(i[n + "conv_b"])})
    n = "L2_ffn_"
    a.update({"f2_gate": i[n + "Wg"].T, "f2_ln_scale": i[n + "ln_scale"].T, "f2_ln_bias": i[n + "ln_bias"].T,
              "f2_b1": col(i[n + "b1"].reshape(-1)), "f2_b2": i[n + "b2"],
              "f2_w_up": i[n + "W1"].transpose(1, 0, 2).reshape(C, -1), "f2_w_down": down(i[n + "W2"].reshape(-1, C)),
              "f2_spread": spread(8, 32), "f2_iota": iota(8)})
    n = "L3_ffn_"
    share = np.zeros((17, 256), f)
    share[16] = 1
    a.update({"f3_gate": np.concatenate([i[n + "Wg"], i[n + "Wsg"]]).T,
              "f3_w_gate": np.concatenate([i[n + "We_gate"].reshape(-1, C), i[n + "Ws_gate"]]).T,
              "f3_w_up": np.concatenate([i[n + "We_up"].reshape(-1, C), i[n + "Ws_up"]]).T,
              "f3_w_down": down(np.concatenate([i[n + "We_down"].transpose(0, 2, 1).reshape(-1, C), i[n + "Ws_down"].T])),
              "f3_spread": np.concatenate([np.pad(spread(16, 64), ((0, 1), (0, 0))), share], axis=1),
              "f3_iota": iota(16)})
    return {k: np.ascontiguousarray(v) for k, v in a.items()}


def kernel(**inputs):
    import numpy as np
    import concourse.bacc as bacc
    from concourse.bass_utils import run_bass_kernel_spmd

    nc = bacc.Bacc("TRN2", target_bir_lowering=False, num_devices=1)
    arrays = layout({k: np.asarray(v) for k, v in inputs.items()})
    d = {k: nc.dram_tensor(f"in_{k}", v.shape, mybir.dt.from_np(v.dtype), kind="ExternalInput").ap()
         for k, v in arrays.items()}
    out = nc.dram_tensor("out_0", (BATCH, TOK, C), F32, kind="ExternalOutput").ap()
    program(nc, d, out)
    r = run_bass_kernel_spmd(nc, [{f"in_{k}": v for k, v in arrays.items()}], core_ids=[0])
    return r.results[0]["out_0"]
```

```python
from contextlib import ExitStack

import concourse.bass as bass
from concourse import mybir

F32 = mybir.dt.float32
BF16 = mybir.dt.bfloat16
U32 = mybir.dt.uint32
ALU = mybir.AluOpType
ACT = mybir.ActivationFunctionType
AX = mybir.AxisListType

P = 128
BATCH, TOK, C, CC, NKEY = 16, 256, 128, 64, 1601
HEADS = 16
QUADS = HEADS // 4
QT = TOK // P
FTOK = 512
FT = FTOK // P
FSTEPS = BATCH * TOK // FTOK
EPS = 1e-5
K_PART = (0, 0, 0, 1, 1, 2)
Q_PART = (0, 1, 2, 0, 1, 0)
SLOTS = len(K_PART)
ROWS8 = 64 + 8 * SLOTS
MAXROW = ROWS8
V8 = 9
P_BUFS = 5
LAG = 2
LAG8 = 3


def key_tiles(nk):
    return [(t * P, min(P, nk - t * P)) for t in range((nk + P - 1) // P)]


def key_chunks(nk):
    n = (nk + 511) // 512
    cuts = [nk * i // n for i in range(n + 1)]
    return [(cuts[i], cuts[i + 1] - cuts[i]) for i in range(n)]


class Sems:

    def __init__(self, nc, ctx, stage, names):
        self.work = {n: ctx.enter_context(nc.semaphore(f"{stage}_{n}")) for n in names + ["iter_done"]}
        self.go = {e: ctx.enter_context(nc.semaphore(f"{stage}_go_{e}")) for e in ("pe", "act", "dve", "pool")}

    def __getitem__(self, name):
        return self.work[name]

    def end_iteration(self, eng, who):
        eng.drain().then_inc(self["iter_done"], 1)
        eng.wait_ge(self.go[who], 1)
        eng.sem_clear(self.go[who])

    def next_iteration(self, sp):
        sp.wait_ge(self["iter_done"], 4)
        nums = sorted(s.num for s in self.work.values())
        if nums[-1] - nums[0] + 1 == len(nums):
            sp.sem_clear(range(nums[0], nums[-1] + 1))
        else:
            for s in self.work.values():
                sp.sem_clear(s)
        for s in self.go.values():
            sp.sem_inc(s, 1)


class Chain:

    def __init__(self, eng, sem):
        self.eng, self.sem, self.n = eng, sem, 0

    def __call__(self, ins):
        ins.then_inc(self.sem, 1)
        self.n += 1
        self.eng.wait_ge(self.sem, self.n)


class Mem:

    def __init__(self, nc, ctx, stage):
        self.nc, self.ctx, self.stage = nc, ctx, stage

    def __call__(self, name, shape, dt=F32):
        return self.ctx.enter_context(self.nc.sbuf_tensor(f"{self.stage}_{name}", shape, dt))


def load_weights(nc, ctx, stage, pairs, prepare=None):
    s_w = ctx.enter_context(nc.semaphore(f"{stage}_weights"))
    s_c = ctx.enter_context(nc.semaphore(f"{stage}_constants"))
    with nc.Block() as block:
        @block.sync
        def _(sp):
            for dst, src in pairs:
                sp.dma_start(dst, src).then_inc(s_w, 16)
            sp.wait_ge(s_w, 16 * len(pairs))
            sp.sem_clear(s_w)

        @block.gpsimd
        def _(pool):
            if prepare:
                prepare(pool, Chain(pool, s_c))
                pool.sem_clear(s_c)



def ln_stats(dve, S, L, tiles, rows=None):
    for t, x in enumerate(tiles):
        ins = dve.bn_stats(L.st[0:x.shape[0], t, :], x)
    L.chain(ins)
    for t, x in enumerate(tiles):
        ins = dve.bn_aggr(L.mv[0:x.shape[0], t, :], L.st[0:x.shape[0], t, :])
    ins.then_inc(S["ln_var"], 1)
    L.count += 1
    dve.wait_ge(S["ln_rstd"], L.count)


def ln_apply(dve, L, t, out, x):
    n = x.shape[0]
    return dve.tensor_scalar(out, x, L.mv[0:n, t, 0:1], L.rs[0:n, t, 0:1], ALU.subtract, ALU.mult)


def ln_rstd(pool, S, L, k, nt):
    pool.wait_ge(S["ln_var"], k + 1)
    pool.tensor_scalar(L.ve[:, 0:nt, :], L.mv[:, 0:nt, 1:2], EPS, None, ALU.add).then_inc(S["ln_eps"], 1)
    pool.wait_ge(S["ln_eps"], k + 1)
    pool.tensor_tensor(L.rs[:, 0:nt, :], L.ve[:, 0:nt, :], L.mh[:, 0:nt, :], ALU.pow).then_inc(S["ln_rstd"], 1)


LN_SEMS = ["ln_var", "ln_eps", "ln_rstd"]


class LnMem:
    def __init__(self, sb, n):
        self.n = n
        self.st = sb("ln_st", [P, n, 6])
        self.mv = sb("ln_mv", [P, n, 2])
        self.ve = sb("ln_ve", [P, n, 1])
        self.rs = sb("ln_rs", [P, n, 1])
        self.mh = sb("ln_mh", [P, n, 1])

    def prepare(self, pool, chain):
        chain(pool.memset(self.mh[:, :, :], -0.5))
        chain(pool.memset(self.mv[:, :, :], 0.0))

    def begin(self, chain):
        self.chain, self.count = chain, 0



class Source:

    def __init__(self, nk, mask, idx0, unit0, quad0):
        self.nk, self.mask = nk, mask
        self.tiles, self.chunks = key_tiles(nk), key_chunks(nk)
        self.T = len(self.tiles)
        self.NU = QT * 4 * len(self.chunks)
        self.idx0, self.unit0, self.quad0 = idx0, unit0, quad0

    def unit(self, k):
        nc_ = len(self.chunks)
        return k // (4 * nc_), k // nc_ % 4, k % nc_

    def schedule(self):
        last_unit, turn = (self.T - 4, self.T - 2) if self.T > 4 else (0, self.T - 1)
        steps = [(g, t) for g in range(QUADS) for t in range(self.T)]
        plan = [("unit", 0, k) for k in range(self.NU)] + [("turn", 0, 0)]
        for n, (g, t) in enumerate(steps):
            plan.append(("scores", g, t))
            if g + 1 < QUADS and t <= last_unit:
                plan += [("unit", g + 1, k) for k in range(self.NU * t // (last_unit + 1),
                                                           self.NU * (t + 1) // (last_unit + 1))]
            if g + 1 < QUADS and t == turn:
                plan.append(("turn", g + 1, 0))
            if n >= LAG:
                plan.append(("pv",) + steps[n - LAG])
        plan += [("pv",) + s for s in steps[-LAG:]]
        return plan


CORE_SEMS = ["max_scores", "max_taken", "max_rows", "max_turned", "max_ready", "scores", "probs", "masked", "rest",
             "pv", "heads_out", "sums_wide", "sums_inv", "heads_ok", "proj"]


def make_sources(specs):
    out, i, u, q = [], 0, 0, 0
    for nk, mask in specs:
        s = Source(nk, mask, i, u, q)
        out.append(s)
        i, u, q = i + QUADS * s.T, u + QUADS * s.NU, q + QUADS
    return out


def core_pe(pe, S, A, s):
    def unit(g, k):
        u = s.unit0 + g * s.NU + k
        qt, h, c = s.unit(k)
        c0, n = s.chunks[c]
        if k == 0 and s.quad0 + g >= 1:
            pe.wait_ge(S["max_ready"], s.quad0 + g)
        if u >= 2:
            pe.wait_ge(S["max_taken"], u - 1)
        pe.matmul(A.bank[2 + u % 2][:, 0:n], A.q_max(s, g, h, qt), A.k_max(s, g, h, c0, n),
                  start=True, stop=True).then_inc(S["max_scores"], 1)

    def turn(g):
        pe.wait_ge(S["max_rows"], s.quad0 + g + 1)
        for qt in range(QT):
            ins = pe.transpose(A.bank[2][0:4, qt * P:(qt + 1) * P], A.negmax[:, qt, :], A.ident[:, :])
        ins.then_inc(S["max_turned"], 1)

    def scores(g, t):
        i = s.idx0 + g * s.T + t
        if i >= 2:
            pe.wait_ge(S["probs"], i - 1)
        if t == 0:
            A.wait_max(pe, s.quad0 + g)
        for h in range(4):
            k0, n = s.tiles[t]
            ins = A.scores(pe, A.S4[0:n, i % 2, h % 2, h // 2 * TOK:(h // 2 + 1) * TOK], s, g, h, k0, n)
        ins.then_inc(S["scores"], 1)

    def pv(g, t):
        i = s.idx0 + g * s.T + t
        pe.wait_ge(S["rest"], i + 1)
        if t == 0:
            A.wait_out(pe, s.quad0 + g)
        A.pv(pe, s, g, t, i % P_BUFS).then_inc(S["pv"], 1)

    for what, g, j in s.schedule():
        {"unit": unit, "turn": lambda g, _: turn(g), "scores": scores, "pv": pv}[what](g, j)


def core_act(act, S, A, s):
    for what, g, t in s.schedule():
        i = s.idx0 + g * s.T + t
        if what == "scores":
            act.wait_ge(S["scores"], i + 1)
            if i >= P_BUFS:
                act.wait_ge(S["pv"], i - P_BUFS + 1)
            n = s.tiles[t][1]
            act.activation(A.probs[0:n, i % P_BUFS, :].rearrange("p (a q) -> p a q", a=2), A.S4[0:n, i % 2, :, :],
                           ACT.Exp, scale=A.scale).then_inc(S["probs"], 1)
        if what == "pv" and t == s.T - 1:
            act.wait_ge(S["pv"], i + 1)
            A.take_out(act, s.quad0 + g).then_inc(S["heads_out"], 1)


def core_pool(pool, S, A, s):
    for g in range(QUADS):
        for t in range(s.T):
            i = s.idx0 + g * s.T + t
            k0, n = s.tiles[t]
            b = i % P_BUFS
            if i:
                pool.wait_ge(S["rest"], i)
            pool.wait_ge(S["probs"], i + 1)
            pr = A.probs[0:n, b, :]
            if s.mask == "causal":
                pool.affine_select(out=pr, in_=pr, pattern=[[0, 4], [1, TOK]], compare_op=ALU.is_ge, fill=0.0,
                                   base=-k0, channel_multiplier=-1).then_inc(S["masked"], 1)
                pool.wait_ge(S["masked"], i + 1)
            if s.mask == "after":
                pool.affine_select(out=A.kept[0:n, b, :], in_=pr, pattern=[[0, 4], [-1, TOK]], compare_op=ALU.is_gt,
                                   fill=0.0, base=k0, channel_multiplier=1).then_inc(S["masked"], 1)
                pool.wait_ge(S["masked"], i + 1)
                pool.tensor_tensor(A.kept_rest[0:n, b, :], A.kept[0:n, b, :], A.high(A.kept, b, n), ALU.subtract)
            pool.tensor_tensor(A.rest[0:n, b, :], pr, A.high(A.probs, b, n), ALU.subtract).then_inc(S["rest"], 1)


def core_dve(dve, S, A, s, chain):
    for what, g, k in s.schedule():
        if what == "unit":
            u = s.unit0 + g * s.NU + k
            qt, h, c = s.unit(k)
            n = s.chunks[c][1]
            dve.wait_ge(S["max_scores"], u + 1)
            if s.mask == "causal":
                if u:
                    dve.wait_ge(S["max_taken"], u)
                dve.tensor_tensor_reduce(A.junk[:, 0:n], A.bank[2 + u % 2][:, 0:n], A.past[:, qt, :], 1.0, -3.0e38,
                                         ALU.add, ALU.max, A.unit_max[:, qt, h, c:c + 1]).then_inc(S["max_taken"], 1)
            else:
                dve.tensor_reduce(A.unit_max[:, qt, h, c:c + 1], A.bank[2 + u % 2][:, 0:n], AX.X,
                                  ALU.max).then_inc(S["max_taken"], 1)
            if k == s.NU - 1:
                dve.wait_ge(S["max_taken"], u + 1)
                dve.tensor_reduce(A.negmax[:, :, :], A.unit_max[:, :, :, 0:len(s.chunks)], AX.X, ALU.max,
                                  negate=True).then_inc(S["max_rows"], 1)
        if what == "turn":
            dve.wait_ge(S["max_turned"], s.quad0 + g + 1)
            dve.tensor_copy(A.negmax_row[0:4, (s.quad0 + g) % 2, :],
                            A.bank[2][0:4, 0:TOK]).then_inc(S["max_ready"], 1)


def tail_pe(pe, S, A, n):
    for k in range(n):
        if k == 0:
            pe.wait_ge(S["heads_out"], A.quads)
        if k >= 4:
            pe.wait_ge(S["sums_inv"], k - 3)
        pe.matmul(A.S4[0:A.rows, k % 4 // 2, k % 2, :], A.spread[:, :], A.heads[:, 2 * k:2 * k + 2, :],
                  start=True, stop=True).then_inc(S["sums_wide"], 1)
    pe.wait_ge(S["heads_ok"], n)
    for qt in range(QT):
        for k in range(2 * n):
            ins = pe.matmul(A.bank[3][:, qt * C:(qt + 1) * C], A.heads[:, k, qt * P:(qt + 1) * P], A.w_out(k),
                            start=(k == 0), stop=(k == 2 * n - 1))
    ins.then_inc(S["proj"], 1)


def tail_dve(dve, S, A, n):
    for k in range(n):
        dve.wait_ge(S["sums_wide"], k + 1)
        inv = A.inv[:, k % 2, :]
        dve.reciprocal(inv, A.S4[0:A.rows, k % 4 // 2, k % 2, :]).then_inc(S["sums_inv"], 1)
        dve.wait_ge(S["sums_inv"], k + 1)
        v = A.heads[:, 2 * k:2 * k + 2, :].rearrange("p g q -> p (g q)")
        dve.tensor_tensor(v, v, inv, ALU.mult).then_inc(S["heads_ok"], 1)
    dve.wait_ge(S["proj"], 1)


class Core:

    def __init__(self, G, sb, scale):
        self.S4, self.bank, self.ident = G.S4, G.bank, G.ident
        self.scale = scale
        self.probs = sb("probs", [P, P_BUFS, 4 * TOK])
        self.rest = sb("rest", [P, P_BUFS, 4 * TOK], BF16)
        self.unit_max = sb("unit_max", [P, QT, 4, 4])
        self.negmax = sb("negmax", [P, QT, 4])
        self.negmax_row = sb("negmax_row", [4, 2, TOK], BF16)

    def high(self, t, b, n):
        return t[0:n, b, :].bitcast(BF16)[:, 1::2]

    @staticmethod
    def place(h):
        return slice(h % 2 * 512 + h // 2 * TOK, h % 2 * 512 + (h // 2 + 1) * TOK)



POOL_COLS = 704
POOL_HEADS = 2
PIECES = 4


class Ev:

    def __init__(self, kind, s=None, g=0, t=0, i=0, k=0, nxt=False, job=None, src=0, j=0, c=0, part=0, quad=0):
        self.kind, self.s, self.g, self.t, self.i, self.k, self.nxt = kind, s, g, t, i, k, nxt
        self.job, self.src, self.j, self.c, self.part, self.quad = job, src, j, c, part, quad


def schedule8(sources, side, with_core, with_next):
    cross, own = sources[0], sources[1:]
    steps = [(s, g, t) for s in sources for g in range(QUADS) for t in range(s.T)] if with_core else []
    turns, plan = {}, []

    windows, at = [], 0
    for g in range(1, QUADS):
        windows.append((cross, g, False, at, cross.T * g - 2))
        at = cross.T * g - 2
    for s in own:
        for g in range(QUADS):
            windows.append((s, g, False, at, at + 2 + g // (QUADS - 1)))
            at += 2 + g // (QUADS - 1)
    if not steps:
        windows, at = [], max(n for n, _, _ in side) + 1
    if with_next:
        windows.append((cross, 0, True, at, max(at + 1, len(steps) - 2)))

    def step(n):
        for s, g, nxt, start, end in windows:
            if n == end:
                turns[s, g, nxt] = len(turns)
                plan.append(Ev("side", s=s, g=g, nxt=nxt, job="turn"))
        for s, g, nxt, start, end in windows:
            for k in range(s.NU):
                if start + k * (end - start) // s.NU == n:
                    plan.append(Ev("unit", s=s, g=g, k=k, nxt=nxt))
        for when, kind, k in side:
            if when == n and (with_core if kind in ENDING8 else with_next):
                plan.append(Ev("side" if kind not in OTHER8 else kind, job=kind, **k))

    for n, (s, g, t) in enumerate(steps):
        plan.append(Ev("scores", s=s, g=g, t=t, i=n))
        step(n)
        if n >= 1:
            plan.append(Ev("rest", i=n - 1))
        if n >= LAG8:
            ps, pg, pt = steps[n - LAG8]
            plan.append(Ev("pv", s=ps, g=pg, t=pt, i=n - LAG8))
    if steps:
        plan.append(Ev("rest", i=len(steps) - 1))
        for i in range(len(steps) - LAG8, len(steps)):
            plan.append(Ev("pv", s=steps[i][0], g=steps[i][1], t=steps[i][2], i=i))
    for n in range(len(steps), max(len(steps) + 8, at + 2)):
        step(n)

    u = k = q = 0
    for e in plan:
        if e.kind == "unit":
            e.u, e.last = u, e.k == e.s.NU - 1
            u += 1
        if e.kind == "side":
            e.n = k
            k += 1
            if e.job == "turn":
                e.q = q
                q += 1
        if e.kind == "scores":
            e.turn = turns.get((e.s, e.g, False)) if e.t == 0 else None
    return plan, q


OTHER8 = ("ln_stats", "ln_rstd", "ln_apply", "part0", "left", "part1", "part2", "write", "stack", "v_first", "v_left",
          "v_second", "v_third", "divide")
ENDING8 = ("divide", "heads_turned", "proj")


def attention8(nc, G, stage, x_in, x_out, w, with_self):
    sources = make_sources([(NKEY, None)] + [(TOK, "causal")] * with_self)
    ns = len(sources)
    cross = sources[0]
    q_col = [i * TOK for i in range(ns)]
    k_col = [ns * TOK + sum(s.nk for s in sources[:i]) for i in range(ns)]
    W = ns * TOK + sum(s.nk for s in sources)
    n_steps = QUADS * sum(s.T for s in sources)
    n_quads = QUADS * ns
    parts_dram = nc.dram_tensor(f"{stage}_parts_dram", [3, P, W], BF16, kind="Internal").ap()

    def last_step(quad):
        return sum(s.T for s in sources for g in range(QUADS) if sources.index(s) * QUADS + g <= quad)

    side = [(1 + c, "k_cross", {"c": c}) for c in range(len(cross.chunks))]
    side += [(5 + j, "v_cross", {"j": j}) for j in range((cross.T + 3) // 4)]
    side += [(3, "ln_stats", {}), (5, "ln_rstd", {}), (8, "ln_apply", {}), (10, "x_turned", {}), (12, "q", {})]
    if with_self:
        side += [(13, "k_own", {}), (14, "v_own", {})]
    side += [(15, "part0", {})] + [(16 + j, "left", {"j": j}) for j in range(PIECES)]
    side += [(17, "write", {"part": 0}), (16 + PIECES, "part1", {}), (18 + PIECES, "write", {"part": 1})]
    side += [(18 + PIECES + j, "part2", {"j": j}) for j in range(PIECES)]
    side += [(19 + 2 * PIECES, "write", {"part": 2}), (20 + 2 * PIECES, "stack", {})]
    for i in range(ns):
        side += [(28 + 4 * i + j, kind, {"src": i}) for j, kind in enumerate(("v_first", "v_left", "v_second", "v_third"))]
    side += [(min(last_step(quad) + LAG8 + 2, n_steps + 1), "divide", {"quad": quad}) for quad in range(n_quads)]
    side += [(n_steps + 2, "heads_turned", {}), (n_steps + 3, "proj", {})]

    with ExitStack() as ctx:
        sb = Mem(nc, ctx, stage)
        A = Core(G, sb, 8 ** -0.5)
        x_sb = [sb(f"x{p}", [P, QT, C]) for p in range(2)]
        xn = sb("xn", [P, QT, C])
        xnT = sb("xnT", [C, TOK])
        ctxT = sb("ctxT", [CC, NKEY])
        qk = sb("qk", [P, W])
        parts = sb("parts", [P, 3, W], BF16)
        k_stack = [sb(f"k_stack{p}", [P, HEADS // 2, W - ns * TOK], BF16) for p in range(2)]
        q_stack = [sb(f"q_stack{p}", [P, HEADS, ns * TOK], BF16) for p in range(2)]
        v_f = [sb(f"v_f{i}", [P, s.T, P]) for i, s in enumerate(sources)]
        v_parts = [[sb(f"v_parts{i}{p}", [P, s.T, HEADS, 3, V8], BF16) for i, s in enumerate(sources)] for p in range(2)]
        junk = sb("junk", [P, 2, TOK]) if with_self else None
        raw = sb("raw", [P, n_quads, 4 * QT, 3 * V8])
        heads = sb("heads", [P, 4 * QT, V8])
        inv = sb("inv1", [P, 4 * QT, 1])
        attn = sb("attn", [P, QT, C])
        more = sb("more", [P, 4 * QT, 8])
        attnT = sb("attnT", [C, TOK])
        L = LnMem(sb, QT)
        names_w = ["wq_c", "wk_c", "wv_c", "bq_c", "bk_c", "b_out", "w_plain", "bv_c"]
        if with_self:
            names_w += ["wq_s", "wk_s", "wv_s", "bq_s", "bk_s", "bv_s"]
        W_sb = {n: sb(n, list(w[n].shape)) for n in names_w}
        wq, wk, wv, bq, bk, bv = ([W_sb[f"{n}_{x}"] for x in "cs"[0:ns]] for n in ("wq", "wk", "wv", "bq", "bk", "bv"))
        out_bank, side_bank, max_bank = G.bank[0], G.bank[1], G.bank[2:4]

        S = Sems(nc, ctx, stage, ["x_in", "ctx_in", "ln_done", "side_ps", "side_done", "part0", "left", "part1", "part2",
                                  "parts_out", "stacked", "max_in0", "max_in1", "v_first", "v_left", "v_second", "v_third",
                                  "rest_dve", "divided", "res", "x_out", "dve_own"] + LN_SEMS + CORE_SEMS)

        def prepare(pool, chain):
            for ks, qs in zip(k_stack, q_stack):
                chain(pool.memset(qs[:, :, :], 0.0))
                chain(pool.memset(ks[32:64, :, :], 0.0))
                chain(pool.memset(ks[96:P, :, :], 1.0))
            for vps in v_parts:
                for vp in vps:
                    chain(pool.memset(vp[:, :, :, 0, 8:9], 1.0))
                    chain(pool.memset(vp[:, :, :, 1:3, 8:9], 0.0))
            for vf in v_f:
                chain(pool.memset(vf[:, :, :], 0.0))
            L.prepare(pool, chain)

        load_weights(nc, ctx, stage, [(W_sb[n][...], w[n]) for n in names_w], prepare)

        s_bias = ctx.enter_context(nc.semaphore(f"{stage}_bias"))
        with nc.Block() as block:
            @block.tensor
            def _(pe):
                for i in range(ns):
                    ins = pe.matmul(side_bank[:, 0:C], bv[i][:, :], W_sb["w_plain"][:, :], start=(i == 0), stop=(i == ns - 1))
                ins.then_inc(s_bias, 1)

            @block.vector
            def _(dve):
                dve.wait_ge(s_bias, 1)
                dve.sem_clear(s_bias)
                dve.tensor_tensor(W_sb["b_out"][:, :], W_sb["b_out"][:, :], side_bank[:, 0:C], ALU.add)

        def q_of(p, g, h, n, c0, m, depth):
            head = 4 * g + h
            return q_stack[p][0:depth, head:head + n, c0:c0 + m]

        def k_of(p, g, h, c0, n, depth):
            return k_stack[p][0:depth, (4 * g + h) // 2, c0 - ns * TOK:c0 - ns * TOK + n]

        def keys_of(s, qt, c):
            c0, n = s.chunks[c]
            return (c0, min(n, (qt + 1) * P)) if s.mask else (c0, n)

        def first_query(s, t):
            return t * P if s.mask else 0

        def last_tile(s, qt):
            return qt if s.mask else s.T - 1

        def by_head(m):
            return m.rearrange("p (h q) -> p h q", q=TOK)

        def rows_in(turn):
            return 16 * (turn // 2 + 1)

        def piece(j):
            return slice(W * j // PIECES, W * (j + 1) // PIECES)

        def quad_of(e):
            return sources.index(e.s) * QUADS + e.g

        def idx(e):
            return sources.index(e.s)


        def seg_sync(sp, plan, n_turns, p, cur, nxt):
            if nxt is not None:
                sp.dma_start(x_sb[1 - p][:, :, :], x_in[nxt].rearrange("(t p) c -> p t c", p=P)).then_inc(S["x_in"], 16)
                sp.dma_start(ctxT[:, :], G.ctxT[nxt]).then_inc(S["ctx_in"], 16)
            for e in plan:
                if e.kind == "write":
                    sp.wait_ge(S[f"part{e.part}"], PIECES if e.part == 2 else 1)
                    sp.dma_start(parts_dram[e.part], parts[:, e.part, :]).then_inc(S["parts_out"], 16)
                if e.kind == "stack":
                    sp.wait_ge(S["parts_out"], 48)
                    for slot in range(SLOTS):
                        k_src, q_src = (parts_dram[part_of[slot]].rearrange("(h a d) n -> a d h n", a=2, d=8)
                                        for part_of in (K_PART, Q_PART))
                        for a in range(2):
                            r = slice(64 * a + 8 * slot, 64 * a + 8 * slot + 8)
                            sp.dma_start(k_stack[1 - p][r, :, :], k_src[a][:, :, ns * TOK:W]).then_inc(S["stacked"], 16)
                            sp.dma_start(q_stack[1 - p][r, a::2, :], q_src[a][:, :, 0:ns * TOK]).then_inc(S["stacked"], 16)
                if e.kind == "side" and e.job == "turn":
                    sp.wait_ge(S["side_done"], e.n + 1)
                    if e.nxt:
                        sp.wait_ge(S["stacked"], 16 * 4 * SLOTS)
                    c0 = q_col[idx(e)]
                    sp.dma_start(q_stack[1 - p if e.nxt else p][MAXROW:MAXROW + 1, 4 * e.g:4 * e.g + 4, c0:c0 + TOK],
                                 A.negmax_row[0:4, e.q % 2, :]).then_inc(S[f"max_in{e.q % 2}"], 16)
            for k in range(min(n_turns, 2)):
                sp.wait_ge(S[f"max_in{k}"], rows_in(n_turns - 1 - (n_turns - 1 - k) % 2))
            if cur is not None:
                sp.wait_ge(S["res"], 1)
                sp.dma_start(x_out[cur].rearrange("(t p) c -> p t c", p=P), xn[:, :, :]).then_inc(S["x_out"], 16)
                sp.wait_ge(S["x_out"], 16)
            S.next_iteration(sp)

        def seg_pe(pe, plan, p, cur, nxt):
            for e in plan:
                if e.kind == "unit":
                    q = 1 - p if e.nxt else p
                    qt, h, c = e.s.unit(e.k)
                    c0, n = keys_of(e.s, qt, c)
                    if e.k == 0 and e.nxt:
                        pe.wait_ge(S["stacked"], 16 * 4 * SLOTS)
                    if e.u >= 2:
                        pe.wait_ge(S["max_taken"], e.u - 1)
                    pe.matmul(max_bank[e.u % 2][:, 0:n], q_of(q, e.g, h, 1, q_col[idx(e)] + qt * P, P, ROWS8),
                              k_of(q, e.g, h, k_col[idx(e)] + c0, n, ROWS8),
                              start=True, stop=True).then_inc(S["max_scores"], 1)
                if e.kind == "scores":
                    k0, n = e.s.tiles[e.t]
                    if e.i >= 2:
                        pe.wait_ge(S["probs"], e.i - 1)
                    if e.turn is not None:
                        pe.wait_ge(S[f"max_in{e.turn % 2}"], rows_in(e.turn))
                    q0 = first_query(e.s, e.t)
                    for h in (0, 2):
                        out = A.S4[0:n, e.i % 2, h // 2, :].rearrange("p (h q) -> p h q", q=TOK)[:, :, q0:TOK]
                        ins = pe.matmul(out, k_of(p, e.g, h, k_col[idx(e)] + k0, n, MAXROW + 1),
                                        q_of(p, e.g, h, 2, q_col[idx(e)] + q0, TOK - q0, MAXROW + 1), start=True, stop=True)
                    ins.then_inc(S["scores"], 1)
                if e.kind == "pv":
                    n, b = e.s.tiles[e.t][1], e.i % P_BUFS
                    pe.wait_ge(S["rest"], e.i + 1)
                    pe.wait_ge(S["rest_dve"], e.i + 1)
                    if e.t == 0 and quad_of(e) >= 1:
                        pe.wait_ge(S["heads_out"], quad_of(e))
                    for j in range(4 * QT):
                        h, qt = j // QT, j % QT
                        if qt * P < first_query(e.s, e.t):
                            continue
                        out, v = out_bank[:, j * 3 * V8:(j + 1) * 3 * V8], v_parts[p][idx(e)][0:n, e.t, 4 * e.g + h, :, :]
                        at = slice(h * TOK + qt * P, h * TOK + qt * P + P)
                        pe.matmul(out, A.high(A.probs, b, n)[:, at], v, start=(e.t == 0 and j == 0), stop=False,
                                  skip_group_check=True)
                        ins = pe.matmul(out, A.rest[0:n, b, at], v, start=False, stop=(e.t == last_tile(e.s, qt)),
                                        skip_group_check=True)
                    ins.then_inc(S["pv"], 1)
                if e.kind == "side":
                    if e.n >= 1:
                        pe.wait_ge(S["side_done"], e.n)
                    if e.job == "turn":
                        pe.wait_ge(S["max_rows"], e.q + 1)
                        for qt in range(QT):
                            ins = pe.transpose(side_bank[0:4, qt * P:(qt + 1) * P], A.negmax[:, qt, :], A.ident[:, :])
                    if e.job == "k_cross":
                        pe.wait_ge(S["ctx_in"], 16)
                        c0, n = cross.chunks[e.c]
                        ins = pe.matmul(side_bank[:, 0:n], wk[0][:, :], ctxT[:, c0:c0 + n], start=True, stop=True)
                    if e.job == "v_cross":
                        for t in range(4 * e.j, min(4 * e.j + 4, cross.T)):
                            k0, n = cross.tiles[t]
                            ins = pe.matmul(side_bank[0:n, t % 4 * P:(t % 4 + 1) * P], ctxT[:, k0:k0 + n], wv[0][:, :],
                                            start=True, stop=True)
                    if e.job == "x_turned":
                        pe.wait_ge(S["ln_done"], 1)
                        for t in range(QT):
                            ins = pe.transpose(side_bank[:, t * P:(t + 1) * P], xn[:, t, :], A.ident[:, :])
                    if e.job == "q":
                        for i in range(ns):
                            ins = pe.matmul(side_bank[:, q_col[i]:q_col[i] + TOK], wq[i][:, :], xnT[:, :], start=True, stop=True)
                    if e.job == "k_own":
                        ins = pe.matmul(side_bank[:, 0:TOK], wk[1][:, :], xnT[:, :], start=True, stop=True)
                    if e.job == "v_own":
                        for t in range(QT):
                            ins = pe.matmul(side_bank[:, t * P:(t + 1) * P], xnT[:, t * P:(t + 1) * P], wv[1][:, :],
                                            start=True, stop=True)
                    if e.job == "heads_turned":
                        pe.wait_ge(S["divided"], n_quads)
                        for t in range(QT):
                            ins = pe.transpose(side_bank[:, t * P:(t + 1) * P], attn[:, t, :], A.ident[:, :])
                    if e.job == "proj":
                        for t in range(QT):
                            ins = pe.matmul(side_bank[:, t * C:(t + 1) * C], attnT[:, t * P:(t + 1) * P], W_sb["w_plain"][:, :],
                                            start=True, stop=True)
                    ins.then_inc(S["side_ps"], 1)
            S.end_iteration(pe, "pe")

        def seg_act(act, plan, p, cur, nxt):
            for e in plan:
                if e.kind == "scores":
                    n, b = e.s.tiles[e.t][1], e.i % P_BUFS
                    act.wait_ge(S["scores"], e.i + 1)
                    if e.i >= P_BUFS:
                        act.wait_ge(S["pv"], e.i - P_BUFS + 1)
                    q0 = first_query(e.s, e.t)
                    act.activation(by_head(A.probs[0:n, b, :])[:, :, q0:TOK],
                                   A.S4[0:n, e.i % 2, :, :].rearrange("p a (h q) -> p (a h) q", q=TOK)[:, :, q0:TOK],
                                   ACT.Exp, scale=A.scale).then_inc(S["probs"], 1)
                if e.kind == "pv" and e.t == e.s.T - 1:
                    act.wait_ge(S["pv"], e.i + 1)
                    act.activation(raw[:, quad_of(e), :, :].rearrange("p a k -> p (a k)"),
                                   out_bank[:, 0:4 * QT * 3 * V8], ACT.Copy).then_inc(S["heads_out"], 1)
                if e.kind == "side" and e.job not in ("turn", "proj"):
                    act.wait_ge(S["side_ps"], e.n + 1)
                    if e.job == "k_cross":
                        c0, n = cross.chunks[e.c]
                        ins = act.activation(qk[:, k_col[0] + c0:k_col[0] + c0 + n], side_bank[:, 0:n], ACT.Identity,
                                             bias=bk[0][:, 0:1])
                    if e.job == "v_cross":
                        t0, t1 = 4 * e.j, min(4 * e.j + 4, cross.T)
                        n = cross.tiles[t1 - 1][1]
                        ins = act.activation(v_f[0][0:n, t0:t1, :].rearrange("p t n -> p (t n)"),
                                             side_bank[0:n, 0:(t1 - t0) * P], ACT.Copy)
                    if e.job == "x_turned":
                        ins = act.activation(xnT[:, :], side_bank[:, 0:TOK], ACT.Copy)
                    if e.job == "heads_turned":
                        ins = act.activation(attnT[:, :], side_bank[:, 0:TOK], ACT.Copy)
                    if e.job == "q":
                        for i in range(ns):
                            ins = act.activation(qk[:, q_col[i]:q_col[i] + TOK], side_bank[:, q_col[i]:q_col[i] + TOK],
                                                 ACT.Identity, bias=bq[i][:, 0:1])
                    if e.job == "k_own":
                        ins = act.activation(qk[:, k_col[1]:k_col[1] + TOK], side_bank[:, 0:TOK], ACT.Identity, bias=bk[1][:, 0:1])
                    if e.job == "v_own":
                        ins = act.activation(v_f[1][:, :, :].rearrange("p t n -> p (t n)"), side_bank[:, 0:TOK], ACT.Copy)
                    ins.then_inc(S["side_done"], 1)
                    side_seen = e.n + 1
                if e.kind == "part0":
                    act.wait_ge(S["side_done"], side_seen)
                    act.activation(parts[:, 0, :], qk[:, :], ACT.Copy).then_inc(S["part0"], 1)
                if e.kind == "part1":
                    act.wait_ge(S["left"], PIECES)
                    act.activation(parts[:, 1, :], qk[:, :], ACT.Copy).then_inc(S["part1"], 1)
                if e.kind in ("v_first", "v_second"):
                    part = 0 if e.kind == "v_first" else 1
                    if e.kind == "v_second":
                        act.wait_ge(S["v_left"], e.src + 1)
                    act.activation(v_parts[1 - p][e.src][:, :, :, part, 0:8].rearrange("p t h d -> p (t h) d"),
                                   v_f[e.src][:, :, :].rearrange("p t (h d) -> p (t h) d", d=8),
                                   ACT.Copy).then_inc(S[e.kind], 1)
            S.end_iteration(act, "act")

        def seg_dve(dve, plan, p, cur, nxt):
            chain = Chain(dve, S["dve_own"])
            L.begin(chain)
            for e in plan:
                if e.kind == "unit":
                    qt, h, c = e.s.unit(e.k)
                    n = keys_of(e.s, qt, c)[1]
                    dve.wait_ge(S["max_scores"], e.u + 1)
                    if e.s.mask == "causal":
                        if e.u >= 2:
                            dve.wait_ge(S["max_taken"], e.u - 1)
                        dve.tensor_tensor_reduce(junk[:, e.u % 2, 0:n], max_bank[e.u % 2][:, 0:n], G.past[:, qt, 0:n], 1.0, -3.0e38,
                                                 ALU.add, ALU.max, A.unit_max[:, qt, h, c:c + 1]).then_inc(S["max_taken"], 1)
                    else:
                        dve.tensor_reduce(A.unit_max[:, qt, h, c:c + 1], max_bank[e.u % 2][:, 0:n], AX.X,
                                          ALU.max).then_inc(S["max_taken"], 1)
                    if e.last:
                        dve.wait_ge(S["max_taken"], e.u + 1)
                        dve.tensor_reduce(A.negmax[:, :, :], A.unit_max[:, :, :, 0:len(e.s.chunks)], AX.X, ALU.max,
                                          negate=True).then_inc(S["max_rows"], 1)
                if e.kind == "side" and e.job == "turn":
                    dve.wait_ge(S["side_ps"], e.n + 1)
                    if e.q >= 2:
                        dve.wait_ge(S[f"max_in{e.q % 2}"], rows_in(e.q - 2))
                    dve.tensor_copy(A.negmax_row[0:4, e.q % 2, :], side_bank[0:4, 0:TOK]).then_inc(S["side_done"], 1)
                if e.kind == "rest":
                    s, g, t = steps_of[e.i]
                    n, b = s.tiles[t][1], e.i % P_BUFS
                    dve.wait_ge(S["probs"], e.i + 1)
                    if s.mask:
                        dve.wait_ge(S["masked"], e.i + 1 - cross.T * QUADS)
                        q = slice(first_query(s, t), TOK)
                        out, pr, hi = (by_head(m)[:, POOL_HEADS:4, q] for m in
                                       (A.rest[0:n, b, :], A.probs[0:n, b, :], A.high(A.probs, b, n)))
                    else:
                        out, pr, hi = (m[:, POOL_COLS:4 * TOK] for m in
                                       (A.rest[0:n, b, :], A.probs[0:n, b, :], A.high(A.probs, b, n)))
                    dve.tensor_tensor(out, pr, hi, ALU.subtract).then_inc(S["rest_dve"], 1)
                if e.kind == "ln_stats":
                    dve.wait_ge(S["x_in"], 16)
                    for t in range(QT):
                        ins = dve.bn_stats(L.st[:, t, :], x_sb[1 - p][:, t, :])
                    chain(ins)
                    for t in range(QT):
                        ins = dve.bn_aggr(L.mv[:, t, :], L.st[:, t, :])
                    ins.then_inc(S["ln_var"], 1)
                if e.kind == "ln_apply":
                    dve.wait_ge(S["ln_rstd"], 1)
                    for t in range(QT):
                        ins = ln_apply(dve, L, t, xn[:, t, :], x_sb[1 - p][:, t, :])
                    ins.then_inc(S["ln_done"], 1)
                if e.kind in ("v_left", "v_third"):
                    vf = v_f[e.src][:, :, :].rearrange("p t (h d) -> p (t h) d", d=8)
                    vp = v_parts[1 - p][e.src][:, :, :, :, 0:8].rearrange("p t h k d -> p (t h) k d")
                    if e.kind == "v_left":
                        dve.wait_ge(S["v_first"], e.src + 1)
                        dve.tensor_tensor(vf, vf, vp[:, :, 0, :], ALU.subtract).then_inc(S["v_left"], 1)
                    else:
                        dve.wait_ge(S["v_second"], e.src + 1)
                        dve.tensor_tensor(vp[:, :, 2, :], vf, vp[:, :, 1, :], ALU.subtract).then_inc(S["v_third"], 1)
                if e.kind == "divide":
                    i, g = e.quad // QUADS, e.quad % QUADS
                    dve.wait_ge(S["heads_out"], e.quad + 1)
                    chain(dve.tensor_reduce(heads[:, :, :], raw[:, e.quad, :, :].rearrange("p a (k d) -> p a d k", d=V8),
                                            AX.X, ALU.add))
                    chain(dve.reciprocal(inv[:, :, :], heads[:, :, 8:9]))
                    out = attn[:, :, 32 * g:32 * g + 32].rearrange("p t (h d) -> p h t d", d=8)
                    by = lambda m: m.rearrange("p (h t) d -> p h t d", t=QT)
                    to = out if i == 0 else by(more[:, :, :])
                    ins = dve.tensor_tensor(to, by(heads[:, :, 0:8]), by(inv[:, :, 0:1].to_broadcast([P, 4 * QT, 8])), ALU.mult)
                    if i:
                        chain(ins)
                        ins = dve.tensor_tensor(out, out, by(more[:, :, :]), ALU.add)
                    ins.then_inc(S["divided"], 1)
                    dve.wait_ge(S["divided"], e.quad + 1)
                if e.kind == "side" and e.job == "proj":
                    for t in range(QT):
                        ins = dve.tensor_tensor(x_sb[p][:, t, :], x_sb[p][:, t, :], W_sb["b_out"][:, :], ALU.add)
                    chain(ins)
                    dve.wait_ge(S["side_ps"], e.n + 1)
                    dve.tensor_tensor(xn[:, :, :].rearrange("p t c -> p (t c)"), side_bank[:, 0:TOK],
                                      x_sb[p][:, :, :].rearrange("p t c -> p (t c)"), ALU.add).then_inc(S["res"], 1)
            S.end_iteration(dve, "dve")

        def seg_pool(pool, plan, p, cur, nxt):
            for e in plan:
                if e.kind == "scores":
                    s, b, i = e.s, e.i % P_BUFS, e.i
                    k0, n = s.tiles[e.t]
                    pool.wait_ge(S["probs"], i + 1)
                    out, pr, hi = A.rest[0:n, b, :], A.probs[0:n, b, :], A.high(A.probs, b, n)
                    if s.mask:
                        q0 = first_query(s, e.t)
                        some = by_head(pr)[:, :, q0:q0 + P]
                        pool.affine_select(out=some, in_=some, pattern=[[0, 4], [1, P]], compare_op=ALU.is_ge, fill=0.0,
                                           base=q0 - k0, channel_multiplier=-1).then_inc(S["masked"], 1)
                        pool.wait_ge(S["masked"], i + 1 - cross.T * QUADS)
                        out, pr, hi = (by_head(m)[:, 0:POOL_HEADS, q0:TOK] for m in (out, pr, hi))
                    else:
                        out, pr, hi = (m[:, 0:POOL_COLS] for m in (out, pr, hi))
                    pool.tensor_tensor(out, pr, hi, ALU.subtract).then_inc(S["rest"], 1)
                    pool.wait_ge(S["rest"], i + 1)
                if e.kind == "ln_rstd":
                    ln_rstd(pool, S, L, 0, QT)
                    pool.wait_ge(S["ln_rstd"], 1)
                if e.kind == "left":
                    if e.j == 0:
                        pool.wait_ge(S["part0"], 1)
                    c = piece(e.j)
                    pool.tensor_tensor(qk[:, c], qk[:, c], parts[:, 0, c], ALU.subtract).then_inc(S["left"], 1)
                    pool.wait_ge(S["left"], e.j + 1)
                if e.kind == "part2":
                    if e.j == 0:
                        pool.wait_ge(S["part1"], 1)
                    c = piece(e.j)
                    pool.tensor_tensor(parts[:, 2, c], qk[:, c], parts[:, 1, c], ALU.subtract).then_inc(S["part2"], 1)
                    pool.wait_ge(S["part2"], e.j + 1)
            S.end_iteration(pool, "pool")

        steps_of = [(s, g, t) for s in sources for g in range(QUADS) for t in range(s.T)]
        first, first_turns = schedule8(sources, side, False, True)
        middle, middle_turns = schedule8(sources, side, True, True)
        last, last_turns = schedule8(sources, side, True, False)

        def batches(eng, seg, turns=False):
            def run(plan, n, p, cur, nxt):
                if turns:
                    seg(eng, plan, n, p, cur, nxt)
                else:
                    seg(eng, plan, p, cur, nxt)
            run(first, first_turns, 1, None, 0)
            with eng.Fori(0, BATCH // 2 - 1) as i:
                run(middle, middle_turns, 0, i * 2, i * 2 + 1)
                run(middle, middle_turns, 1, i * 2 + 1, i * 2 + 2)
            run(middle, middle_turns, 0, BATCH - 2, BATCH - 1)
            run(last, last_turns, 1, BATCH - 1, None)

        with nc.Block() as block:
            @block.sync
            def _(sp):
                batches(sp, seg_sync, True)

            @block.tensor
            def _(pe):
                batches(pe, seg_pe)

            @block.scalar
            def _(act):
                batches(act, seg_act)

            @block.vector
            def _(dve):
                batches(dve, seg_dve)

            @block.gpsimd
            def _(pool):
                batches(pool, seg_pool)



D32 = 32
V_COLS = 3 * D32 + 1


def attention32(nc, G, stage, x_in, x1_out, x_out, w, own_keys):
    nk, cy = (TOK, C) if own_keys else (NKEY, CC)
    s, = make_sources([(nk, "after" if own_keys else None)])
    with ExitStack() as ctx:
        sb = Mem(nc, ctx, stage)
        A = Core(G, sb, D32 ** -0.5)
        A.rows = V_COLS
        A.heads, A.inv = sb("heads", [V_COLS, HEADS, TOK]), sb("inv", [V_COLS, 2, 2 * TOK])
        A.quads, A.spread = QUADS, G.spread32
        x_sb = sb("x", [P, QT, C])
        x1 = sb("x1", [P, QT, C]) if own_keys else x_sb
        xn = sb("xn", [P, QT, C])
        xqT = sb("xqT", [C, TOK])
        yT = sb("yT", [cy, nk])
        q_f, q_b = sb("q_f", [P, QUADS, 4, TOK]), sb("q_b", [P, QUADS, 4, TOK], BF16)
        k_f, k_b = sb("k_f", [P, QUADS, nk]), sb("k_b", [P, QUADS, nk], BF16)
        v_left = sb("v_left", [P, 2, HEADS * D32])
        v_parts = sb("v_parts", [P, s.T, HEADS, V_COLS], BF16)
        row_of = sb("row_of", [P, 4, P], BF16)
        names_w = ["wq", "wk", "wv", "w_out", "b_out", "lnx_g", "lnx_b", "lny_g", "lny_b"] + ["ln1_g", "ln1_b"] * own_keys
        W_sb = {n: sb(n, list(w[n].shape)) for n in names_w}
        row_of_f = sb("row_of_f", [P, 4, P])
        A.negmax_row = sb("negmax_rows", [P, 2, TOK], BF16)
        if own_keys:
            A.kept = sb("kept", [P, P_BUFS, 4 * TOK])
            A.kept_rest = sb("kept_rest", [P, P_BUFS, 4 * TOK], BF16)
            ones_col = sb("ones_col", [P, V_COLS], BF16)
            L = LnMem(sb, QT)
        else:
            ctx_sb = sb("ctx", [P, s.T, CC])
            L = LnMem(sb, s.T)

        S = Sems(nc, ctx, stage, ["x_in", "ctx_in", "x1", "x1_out", "xn", "yn", "ring_ps", "ring", "v_ps", "v_left",
                                  "v_mid", "v_parts", "qk_b", "res", "x_out", "dve_own"] + LN_SEMS + CORE_SEMS)

        def prepare(pool, chain):
            chain(pool.memset(v_parts[:, :, :, 3 * D32:V_COLS], 0.0 if own_keys else 1.0))
            if own_keys:
                chain(pool.memset(ones_col[:, 0:3 * D32], 0.0))
                chain(pool.memset(ones_col[:, 3 * D32:V_COLS], 1.0))
            else:
                chain(pool.memset(ctx_sb[:, :, :], 0.0))
            chain(pool.memset(A.negmax_row[:, :, :], 0.0))
            chain(pool.memset(q_f[:, :, :, :], 0.0))
            L.prepare(pool, chain)

        load_weights(nc, ctx, stage, [(W_sb[n][...], w[n]) for n in names_w] + [(row_of_f[:, :, :], G.row_of)], prepare)
        with nc.Block() as block:
            @block.vector
            def _(dve):
                dve.tensor_copy(row_of[:, :, :], row_of_f[:, :, :])

        A.w_out = lambda k: W_sb["w_out"][:, k, :]
        A.q_max = lambda s, g, h, qt: q_b[:, g, h, qt * P:(qt + 1) * P]
        A.k_max = lambda s, g, h, c0, n: k_b[:, g, c0:c0 + n]
        A.wait_max = lambda pe, quad: pe.wait_ge(S["max_ready"], quad + 1)

        def scores(pe, out, s, g, h, k0, n):
            pe.matmul(out, k_f[:, g, k0:k0 + n], q_f[:, g, h, :], start=True, stop=False)
            return pe.matmul(out, row_of[:, h, 0:n], A.negmax_row[:, g % 2, :], start=False, stop=True)

        def wait_out(pe, quad):
            if quad >= 1:
                pe.wait_ge(S["heads_out"], quad)

        def pv(pe, s, g, t, b):
            n = s.tiles[t][1]
            for h in range(4):
                out = A.bank[h % 2][0:V_COLS, h // 2 * TOK:(h // 2 + 1) * TOK]
                v, last = v_parts[0:n, t, 4 * g + h, :], t == s.T - 1
                opens = t == 0 and h // 2 == 0
                if own_keys:
                    pe.matmul(out, ones_col[0:n, :], A.high(A.probs, b, n)[:, A.place(h)], start=opens, stop=False,
                              skip_group_check=True)
                    pe.matmul(out, ones_col[0:n, :], A.rest[0:n, b, A.place(h)], start=False, stop=False,
                              skip_group_check=True)
                    high, rest, opens = A.high(A.kept, b, n), A.kept_rest, False
                else:
                    high, rest = A.high(A.probs, b, n), A.rest
                pe.matmul(out, v, high[:, A.place(h)], start=opens, stop=False, skip_group_check=True)
                ins = pe.matmul(out, v, rest[0:n, b, A.place(h)], start=False, stop=last, skip_group_check=True)
            return ins

        def take_out(act, quad):
            for a in range(2):
                ins = act.activation(A.heads[:, 4 * quad + a:4 * quad + 4:2, :],
                                     A.bank[a][0:V_COLS, :].rearrange("p (h q) -> p h q", h=2), ACT.Copy)
            return ins

        A.scores, A.wait_out, A.pv, A.take_out = scores, wait_out, pv, take_out

        ring = []
        if not own_keys:
            ring += [("ctx", t, min(t + 4, s.T)) for t in range(0, s.T, 4)]
        ring += [("x", 0, 0)] + [("q", g, 0) for g in range(QUADS)]
        ring += [("k", g, c) for g in range(QUADS) for c in range(len(s.chunks))]
        after_x = ring.index(("x", 0, 0)) + 1
        ring_bank = [A.S4[:, a, c, :] for a in range(2) for c in range(2)]

        with nc.Block() as block:
            @block.sync
            def _(sp):
                with sp.Fori(0, BATCH) as b:
                    sp.dma_start(x_sb[:, :, :], x_in[b].rearrange("(t p) c -> p t c", p=P)).then_inc(S["x_in"], 16)
                    if own_keys:
                        sp.wait_ge(S["x1"], 1)
                        sp.dma_start(x1_out[b].rearrange("(t p) c -> p t c", p=P), x1[:, :, :]).then_inc(S["x1_out"], 16)
                        sp.wait_ge(S["x1_out"], 16)
                    else:
                        full = nk // P * P
                        sp.dma_start(ctx_sb[:, 0:nk // P, :],
                                     G.ctx[b, 0:full].rearrange("(t p) c -> p t c", p=P)).then_inc(S["ctx_in"], 16)
                        sp.dma_start(ctx_sb[0:nk - full, nk // P, :], G.ctx[b, full:nk]).then_inc(S["ctx_in"], 16)
                    sp.wait_ge(S["res"], 1)
                    sp.dma_start(x_out[b].rearrange("(t p) c -> p t c", p=P), xn[:, :, :]).then_inc(S["x_out"], 16)
                    sp.wait_ge(S["x_out"], 16)
                    S.next_iteration(sp)

            @block.tensor
            def _(pe):
                with pe.Fori(0, BATCH) as b:
                    if not own_keys:
                        pe.wait_ge(S["yn"], 1)
                    for i, (what, g, c) in enumerate(ring):
                        bank = ring_bank[i % 4]
                        if i >= 4:
                            pe.wait_ge(S["ring"], i - 3)
                        if i == after_x:
                            pe.wait_ge(S["ring"], after_x)
                        if what == "ctx":
                            for t in range(g, c):
                                k0, n = s.tiles[t]
                                ins = pe.transpose(bank[0:CC, (t - g) * P:(t - g) * P + n], ctx_sb[0:n, t, :],
                                                   A.ident[0:n, 0:n])
                        if what == "x":
                            pe.wait_ge(S["xn"], 1)
                            for t in range(QT):
                                ins = pe.transpose(bank[:, t * P:(t + 1) * P], xn[:, t, :], A.ident[:, :])
                        if what == "q":
                            ins = pe.matmul(bank[:, 0:TOK], W_sb["wq"][:, g * P:(g + 1) * P], xqT[:, :], start=True, stop=True)
                        if what == "k":
                            c0, n = s.chunks[c]
                            ins = pe.matmul(bank[:, 0:n], W_sb["wk"][:, g * P:(g + 1) * P], yT[:, c0:c0 + n],
                                            start=True, stop=True)
                        ins.then_inc(S["ring_ps"], 1)
                    for t, (k0, n) in enumerate(s.tiles):
                        if t >= 4:
                            pe.wait_ge(S["v_left"], t - 3)
                        pe.matmul(A.bank[t % 4][0:n, :], yT[:, k0:k0 + n], W_sb["wv"][:, :],
                                  start=True, stop=True).then_inc(S["v_ps"], 1)
                    pe.wait_ge(S["ring"], len(ring))
                    pe.wait_ge(S["qk_b"], 2)
                    pe.wait_ge(S["v_parts"], s.T)
                    core_pe(pe, S, A, s)
                    tail_pe(pe, S, A, HEADS // 2)
                    S.end_iteration(pe, "pe")

            @block.scalar
            def _(act):
                with act.Fori(0, BATCH) as b:
                    for i, (what, g, c) in enumerate(ring):
                        bank = ring_bank[i % 4]
                        act.wait_ge(S["ring_ps"], i + 1)
                        if what == "ctx":
                            k0 = g * P
                            n = s.tiles[c - 1][0] + s.tiles[c - 1][1] - k0
                            ins = act.activation(yT[:, k0:k0 + n], bank[0:CC, 0:n], ACT.Identity,
                                                 bias=W_sb["lny_b"][:, 0:1], scale=W_sb["lny_g"][:, 0:1])
                        if what == "x":
                            if own_keys:
                                act.activation(yT[:, :], bank[:, 0:TOK], ACT.Identity, bias=W_sb["lny_b"][:, 0:1],
                                               scale=W_sb["lny_g"][:, 0:1])
                            ins = act.activation(xqT[:, :], bank[:, 0:TOK], ACT.Identity, bias=W_sb["lnx_b"][:, 0:1],
                                                 scale=W_sb["lnx_g"][:, 0:1])
                        if what == "q":
                            for h in range(4):
                                r = slice(D32 * h, D32 * h + D32)
                                ins = act.activation(q_f[r, g, h, :], bank[r, 0:TOK], ACT.Copy)
                        if what == "k":
                            c0, n = s.chunks[c]
                            ins = act.activation(k_f[:, g, c0:c0 + n], bank[:, 0:n], ACT.Copy)
                        ins.then_inc(S["ring"], 1)
                    core_act(act, S, A, s)
                    S.end_iteration(act, "act")

            @block.vector
            def _(dve):
                with dve.Fori(0, BATCH) as b:
                    chain = Chain(dve, S["dve_own"])
                    L.begin(chain)
                    if not own_keys:
                        dve.wait_ge(S["ctx_in"], 32)
                        ctx_tiles = [ctx_sb[0:n, t, :] for t, (_, n) in enumerate(s.tiles)]
                        ln_stats(dve, S, L, ctx_tiles)
                        for t, tile in enumerate(ctx_tiles):
                            ins = ln_apply(dve, L, t, tile, tile)
                        ins.then_inc(S["yn"], 1)
                    dve.wait_ge(S["x_in"], 16)
                    tiles = lambda m: [m[:, t, :] for t in range(QT)]
                    if own_keys:
                        ln_stats(dve, S, L, tiles(x_sb))
                        for t in range(QT):
                            ins = ln_apply(dve, L, t, x_sb[:, t, :], x_sb[:, t, :])
                        chain(ins)
                        ln_stats(dve, S, L, tiles(x_sb))
                        for t in range(QT):
                            ins = ln_apply(dve, L, t, x1[:, t, :], x_sb[:, t, :])
                        chain(ins)
                        for t in range(QT):
                            ins = dve.tensor_tensor(x1[:, t, :], x1[:, t, :], W_sb["ln1_g"][:, :], ALU.mult)
                        chain(ins)
                        for t in range(QT):
                            ins = dve.tensor_tensor(x1[:, t, :], x1[:, t, :], W_sb["ln1_b"][:, :], ALU.add)
                        ins.then_inc(S["x1"], 1)
                        dve.wait_ge(S["x1"], 1)
                    ln_stats(dve, S, L, tiles(x1))
                    for t in range(QT):
                        ins = ln_apply(dve, L, t, xn[:, t, :], x1[:, t, :])
                    ins.then_inc(S["xn"], 1)
                    for t, (_, n) in enumerate(s.tiles):
                        dve.wait_ge(S["v_ps"], t + 1)
                        if t >= 2:
                            dve.wait_ge(S["v_parts"], t - 1)
                        first = v_parts[0:n, t, :, 0:D32]
                        v = A.bank[t % 4][0:n, :].rearrange("p (h d) -> p h d", d=D32)
                        chain(dve.tensor_copy(first, v))
                        dve.tensor_tensor(v_left[0:n, t % 2, :].rearrange("p (h d) -> p h d", d=D32), v, first,
                                          ALU.subtract).then_inc(S["v_left"], 1)
                    dve.wait_ge(S["ring"], len(ring))
                    dve.tensor_copy(q_b[:, :, :, :], q_f[:, :, :, :]).then_inc(S["qk_b"], 1)
                    dve.tensor_copy(k_b[:, :, :], k_f[:, :, :]).then_inc(S["qk_b"], 1)
                    core_dve(dve, S, A, s, chain)
                    for t in range(QT):
                        ins = dve.tensor_tensor(x_sb[:, t, :], x1[:, t, :], W_sb["b_out"][:, :], ALU.add)
                    chain(ins)
                    tail_dve(dve, S, A, HEADS // 2)
                    dve.tensor_tensor(xn[:, :, :].rearrange("p t c -> p (t c)"), A.bank[3][:, 0:TOK],
                                      x_sb[:, :, :].rearrange("p t c -> p (t c)"), ALU.add).then_inc(S["res"], 1)
                    S.end_iteration(dve, "dve")

            @block.gpsimd
            def _(pool):
                with pool.Fori(0, BATCH) as b:
                    if own_keys:
                        for k in range(3):
                            ln_rstd(pool, S, L, k, QT)
                    else:
                        ln_rstd(pool, S, L, 0, s.T)
                        ln_rstd(pool, S, L, 1, QT)
                    for t, (_, n) in enumerate(s.tiles):
                        pool.wait_ge(S["v_left"], t + 1)
                        left = v_left[0:n, t % 2, :].rearrange("p (h d) -> p h d", d=D32)
                        second = v_parts[0:n, t, :, D32:2 * D32]
                        pool.tensor_copy(second, left).then_inc(S["v_mid"], 1)
                        pool.wait_ge(S["v_mid"], t + 1)
                        pool.tensor_tensor(v_parts[0:n, t, :, 2 * D32:3 * D32], left, second,
                                           ALU.subtract).then_inc(S["v_parts"], 1)
                        pool.wait_ge(S["v_parts"], t + 1)
                    core_pool(pool, S, A, s)
                    S.end_iteration(pool, "pool")



def token_tiles(x):
    return x.rearrange("b t c -> (b t) c").rearrange("(s t p) c -> s p t c", t=FT, p=P)


class Banks:

    def __init__(self, G):
        self.all = [G.S4[:, a, c, :] for a in range(2) for c in range(2)] + [b[:, :] for b in G.bank]


def flat(t):
    return t.rearrange("p t c -> p (t c)")


def transpose_tiles(pe, bank, tiles, ident):
    for t, tile in enumerate(tiles):
        ins = pe.transpose(bank[0:tile.shape[1], t * P:(t + 1) * P], tile, ident[:, :])
    return ins


def mlp32(nc, G, stage, xo_in, skip_in, add_in, out, w, last_ln):
    KH = w["li2_w"].shape[1] // P
    with ExitStack() as ctx:
        sb = Mem(nc, ctx, stage)
        banks = Banks(G).all
        names_w = ["li2_w", "li2_b", "li3_w", "li3_b", "ln3_g", "ln3_b"] + ["ln2_g", "ln2_b"] * last_ln
        W_sb = {n: sb(n, list(w[n].shape)) for n in names_w}
        xo, skip, add, xn = (sb(n, [P, FT, C]) for n in ("xo", "skip", "add", "xn"))
        nT = sb("nT", [C, FTOK])
        hT = sb("hT", [P, KH, FTOK])
        L = LnMem(sb, FT)
        S = Sems(nc, ctx, stage, ["xo_in", "skip_in", "add_in", "xn", "xnT_ps", "nT", "h_ps", "h", "y_ps", "res",
                                  "x_out", "dve_own"] + LN_SEMS)
        load_weights(nc, ctx, stage, [(W_sb[n][...], w[n]) for n in names_w], L.prepare)

        with nc.Block() as block:
            @block.sync
            def _(sp):
                with sp.Fori(0, FSTEPS) as i:
                    sp.dma_start(xo[:, :, :], token_tiles(xo_in)[i]).then_inc(S["xo_in"], 16)
                    sp.dma_start(skip[:, :, :], token_tiles(skip_in)[i]).then_inc(S["skip_in"], 16)
                    if not last_ln:
                        sp.dma_start(add[:, :, :], token_tiles(add_in)[i]).then_inc(S["add_in"], 16)
                    sp.wait_ge(S["res"], 1)
                    sp.dma_start(token_tiles(out)[i], xn[:, :, :]).then_inc(S["x_out"], 16)
                    sp.wait_ge(S["x_out"], 16)
                    S.next_iteration(sp)

            @block.tensor
            def _(pe):
                with pe.Fori(0, FSTEPS) as i:
                    pe.wait_ge(S["xn"], 1)
                    transpose_tiles(pe, banks[4], [xn[:, t, :] for t in range(FT)], G.ident).then_inc(S["xnT_ps"], 1)
                    pe.wait_ge(S["nT"], 1)
                    for k in range(KH):
                        pe.matmul(banks[k], W_sb["li2_w"][:, k * P:(k + 1) * P], nT[:, :],
                                  start=True, stop=True).then_inc(S["h_ps"], 1)
                    pe.wait_ge(S["h"], KH)
                    for t in range(FT):
                        for k in range(KH):
                            ins = pe.matmul(banks[5][:, t * C:(t + 1) * C], hT[:, k, t * P:(t + 1) * P],
                                            W_sb["li3_w"][:, k, :], start=(k == 0), stop=(k == KH - 1))
                    ins.then_inc(S["y_ps"], 1)
                    S.end_iteration(pe, "pe")

            @block.scalar
            def _(act):
                with act.Fori(0, FSTEPS) as i:
                    act.wait_ge(S["xnT_ps"], 1)
                    act.activation(nT[:, :], banks[4], ACT.Identity, bias=W_sb["ln3_b"][:, 0:1],
                                   scale=W_sb["ln3_g"][:, 0:1]).then_inc(S["nT"], 1)
                    for k in range(KH):
                        act.wait_ge(S["h_ps"], k + 1)
                        act.activation(hT[:, k, :], banks[k], ACT.Gelu,
                                       bias=W_sb["li2_b"][:, k:k + 1]).then_inc(S["h"], 1)
                    S.end_iteration(act, "act")

            @block.vector
            def _(dve):
                with dve.Fori(0, FSTEPS) as i:
                    chain = Chain(dve, S["dve_own"])
                    L.begin(chain)
                    dve.wait_ge(S["xo_in"], 16)
                    ln_stats(dve, S, L, [xo[:, t, :] for t in range(FT)])
                    for t in range(FT):
                        ins = ln_apply(dve, L, t, xn[:, t, :], xo[:, t, :])
                    ins.then_inc(S["xn"], 1)
                    dve.wait_ge(S["skip_in"], 16)
                    chain(dve.tensor_tensor(flat(skip[:, :, :]), flat(skip[:, :, :]), flat(xo[:, :, :]), ALU.add))
                    for t in range(FT):
                        ins = dve.tensor_tensor(skip[:, t, :], skip[:, t, :], W_sb["li3_b"][:, :], ALU.add)
                    chain(ins)
                    if not last_ln:
                        dve.wait_ge(S["add_in"], 16)
                        chain(dve.tensor_tensor(flat(skip[:, :, :]), flat(skip[:, :, :]), flat(add[:, :, :]), ALU.add))
                    dve.wait_ge(S["y_ps"], 1)
                    if not last_ln:
                        dve.tensor_tensor(flat(xn[:, :, :]), flat(skip[:, :, :]), banks[5], ALU.add).then_inc(S["res"], 1)
                    else:
                        chain(dve.tensor_tensor(flat(skip[:, :, :]), flat(skip[:, :, :]), banks[5], ALU.add))
                        ln_stats(dve, S, L, [skip[:, t, :] for t in range(FT)])
                        for t in range(FT):
                            ins = ln_apply(dve, L, t, xn[:, t, :], skip[:, t, :])
                        chain(ins)
                        for t in range(FT):
                            ins = dve.tensor_tensor(xn[:, t, :], xn[:, t, :], W_sb["ln2_g"][:, :], ALU.mult)
                        chain(ins)
                        for t in range(FT):
                            ins = dve.tensor_tensor(xn[:, t, :], xn[:, t, :], W_sb["ln2_b"][:, :], ALU.add)
                        ins.then_inc(S["res"], 1)
                    S.end_iteration(dve, "dve")

            @block.gpsimd
            def _(pool):
                with pool.Fori(0, FSTEPS) as i:
                    for k in range(1 + last_ln):
                        ln_rstd(pool, S, L, k, FT)
                    S.end_iteration(pool, "pool")


def experts(nc, G, stage, x_in, out, w, kind):
    K_TOP = {"hash": 4, "top1": 1, "shared": 2}[kind]
    E = {"hash": 32, "top1": 8, "shared": 16}[kind]
    EG = E + (kind == "shared")
    NH = w["w_down"].shape[1]
    with ExitStack() as ctx:
        sb = Mem(nc, ctx, stage)
        banks = Banks(G).all
        names_w = {"hash": ["hasher", "keys", "scale"], "top1": ["gate", "ln_scale", "ln_bias", "b1", "b2"],
                   "shared": ["gate", "w_gate"]}[kind] + ["w_up", "w_down", "spread", "iota"]
        W_sb = {n: sb(n, list(w[n].shape)) for n in names_w}
        x, z = sb("x", [P, FT, C]), sb("z", [P, FT, C])
        res = sb("res", [P, FT, C])
        xh = sb("xh", [P, FT, C]) if kind == "top1" else None
        zT = sb("zT", [C, FTOK])
        xhT = sb("xhT", [C, FTOK]) if kind == "top1" else zT
        hashT = sb("hashT", [32, FTOK])
        logits = sb("logits", [P, FT, EG])
        best, best_f = sb("best", [P, FT, 8]), sb("best_f", [P, FT, 8])
        best_i = sb("best_i", [P, FT, 8], U32)
        weight = sb("weight", [P, FT, 8])
        total, inv = sb("total", [P, FT, 1]), sb("inv", [P, FT, 1])
        sig = sb("sig", [P, FT, 1])
        term = sb("term", [P, FT, E])
        gates = sb("gates", [P, FT, EG])
        gatesT = sb("gatesT", [EG, FTOK])
        act_out = sb("act_out", [P, NH, FTOK])
        hT = sb("hT", [P, NH, FTOK])
        L = LnMem(sb, FT)
        S = Sems(nc, ctx, stage, ["x_in", "z", "xh", "zT_ps", "zT", "hash_ps", "hash", "logits_ps", "logits", "best", "weight",
                                  "gates", "gT_ps", "gT", "up_ps", "act", "h", "y_ps", "res", "x_out",
                                  "dve_own"] + LN_SEMS)
        load_weights(nc, ctx, stage, [(W_sb[n][...], w[n]) for n in names_w], L.prepare)

        if kind == "top1":
            s_bias = ctx.enter_context(nc.semaphore(f"{stage}_bias"))
            HID = NH * P // E
            with nc.Block() as block:
                @block.tensor
                def _(pe):
                    for e in range(E):
                        r = e % (P // HID) * HID
                        ins = pe.matmul(banks[0][r:r + HID, e // (P // HID):e // (P // HID) + 1],
                                        W_sb["w_up"][:, e * HID:(e + 1) * HID], W_sb["ln_bias"][:, e:e + 1],
                                        start=True, stop=True)
                    ins.then_inc(s_bias, 1)

                @block.vector
                def _(dve):
                    dve.wait_ge(s_bias, 1)
                    dve.sem_clear(s_bias)
                    dve.tensor_tensor(W_sb["b1"][:, :], W_sb["b1"][:, :], banks[0][:, 0:NH], ALU.add)
                    for e in range(E):
                        w1 = W_sb["w_up"][:, e * HID:(e + 1) * HID]
                        dve.tensor_scalar(w1, w1, W_sb["ln_scale"][:, e:e + 1], None, ALU.mult)

        gate_w = W_sb["gate"] if kind != "hash" else None
        per_tile = 3 if kind == "shared" else 2

        def tile_banks(k):
            return [banks[2 + (k % 2) * per_tile + j] for j in range(per_tile)]

        def has_own_gate(k):
            return kind == "shared"

        with nc.Block() as block:
            @block.sync
            def _(sp):
                with sp.Fori(0, FSTEPS) as i:
                    sp.dma_start(x[:, :, :], token_tiles(x_in)[i]).then_inc(S["x_in"], 16)
                    sp.wait_ge(S["res"], 1)
                    sp.dma_start(token_tiles(out)[i], res[:, :, :]).then_inc(S["x_out"], 16)
                    sp.wait_ge(S["x_out"], 16)
                    S.next_iteration(sp)

            @block.tensor
            def _(pe):
                with pe.Fori(0, FSTEPS) as i:
                    pe.wait_ge(S["z"], 1)
                    transpose_tiles(pe, banks[0], [z[:, t, :] for t in range(FT)], G.ident).then_inc(S["zT_ps"], 1)
                    pe.wait_ge(S["zT"], 1)
                    keys, keyed = gate_w, zT
                    if kind == "hash":
                        pe.matmul(banks[0][0:32, :], W_sb["hasher"][:, :], zT[:, :], start=True, stop=True).then_inc(S["hash_ps"], 1)
                        pe.wait_ge(S["hash"], 1)
                        keys, keyed = W_sb["keys"], hashT
                    for t in range(FT):
                        ins = pe.matmul(banks[1][:, t * EG:(t + 1) * EG], keyed[:, t * P:(t + 1) * P], keys[:, :],
                                        start=True, stop=True)
                    ins.then_inc(S["logits_ps"], 1)
                    if kind == "top1":
                        pe.wait_ge(S["xh"], 1)
                        transpose_tiles(pe, banks[0], [xh[:, t, :] for t in range(FT)], G.ident).then_inc(S["zT_ps"], 1)
                        pe.wait_ge(S["zT"], 2)
                    pe.wait_ge(S["gates"], 1)
                    transpose_tiles(pe, banks[0], [gates[:, t, :] for t in range(FT)], G.ident).then_inc(S["gT_ps"], 1)
                    pe.wait_ge(S["gT"], 1)
                    for k in range(NH):
                        tb = tile_banks(k)
                        cols = slice(k * P, (k + 1) * P)
                        if k >= 2:
                            pe.wait_ge(S["act"], k - 1)
                            pe.wait_ge(S["h"], k - 1)
                        pe.matmul(tb[0], W_sb["w_gate" if kind == "shared" else "w_up"][:, cols], xhT[:, :],
                                  start=True, stop=True)
                        if kind == "shared":
                            pe.matmul(tb[2], W_sb["w_up"][:, cols], zT[:, :], start=True, stop=True)
                        pe.matmul(tb[1], W_sb["spread"][:, cols], gatesT[:, :], start=True, stop=True).then_inc(S["up_ps"], 1)
                    pe.wait_ge(S["h"], NH)
                    for t in range(FT):
                        o = banks[1][:, t * C:(t + 1) * C]
                        if kind == "top1":
                            pe.matmul(o, gatesT[:, t * P:(t + 1) * P], W_sb["b2"][:, :], start=True, stop=False)
                        for k in range(NH):
                            ins = pe.matmul(o, hT[:, k, t * P:(t + 1) * P], W_sb["w_down"][:, k, :],
                                            start=(k == 0 and kind != "top1"), stop=(k == NH - 1))
                    ins.then_inc(S["y_ps"], 1)
                    S.end_iteration(pe, "pe")

            @block.scalar
            def _(act):
                with act.Fori(0, FSTEPS) as i:
                    act.wait_ge(S["zT_ps"], 1)
                    act.activation(zT[:, :], banks[0], ACT.Copy).then_inc(S["zT"], 1)
                    if kind == "hash":
                        act.wait_ge(S["hash_ps"], 1)
                        act.activation(hashT[:, :], banks[0][0:32, :], ACT.Copy).then_inc(S["hash"], 1)
                    if kind == "top1":
                        act.wait_ge(S["zT_ps"], 2)
                        act.activation(xhT[:, :], banks[0], ACT.Copy).then_inc(S["zT"], 1)
                    if kind != "top1":
                        act.wait_ge(S["best"], 1)
                        ins = act.activation(weight[:, :, :], best[:, :, :], ACT.Exp)
                        if kind == "shared":
                            ins = act.activation(sig[:, :, :], logits[:, :, E:EG], ACT.Exp, scale=-1.0)
                        ins.then_inc(S["weight"], 1)
                    act.wait_ge(S["gT_ps"], 1)
                    act.activation(gatesT[:, :], banks[0][0:EG, :], ACT.Copy).then_inc(S["gT"], 1)
                    for k in range(NH):
                        act.wait_ge(S["up_ps"], k + 1)
                        if kind == "top1":
                            ins = act.activation(act_out[:, k, :], tile_banks(k)[0], ACT.Gelu, bias=W_sb["b1"][:, k:k + 1])
                        else:
                            ins = act.activation(act_out[:, k, :], tile_banks(k)[0], ACT.Silu)
                        ins.then_inc(S["act"], 1)
                    S.end_iteration(act, "act")

            @block.vector
            def _(dve):
                with dve.Fori(0, FSTEPS) as i:
                    chain = Chain(dve, S["dve_own"])
                    L.begin(chain)
                    dve.wait_ge(S["x_in"], 16)
                    ln_stats(dve, S, L, [x[:, t, :] for t in range(FT)])
                    for t in range(FT):
                        ins = ln_apply(dve, L, t, z[:, t, :], x[:, t, :])
                    ins.then_inc(S["z"], 1)
                    dve.wait_ge(S["z"], 1)
                    if kind == "top1":
                        ln_stats(dve, S, L, [z[:, t, :] for t in range(FT)])
                        for t in range(FT):
                            ins = ln_apply(dve, L, t, xh[:, t, :], z[:, t, :])
                        ins.then_inc(S["xh"], 1)
                    dve.wait_ge(S["logits_ps"], 1)
                    chain(dve.tensor_copy(flat(logits[:, :, :]), banks[1][:, 0:FT * EG]))
                    for t in range(FT):
                        ins = dve.max(best[:, t, :], logits[:, t, 0:E])
                    chain(ins)
                    for t in range(FT):
                        ins = dve.max_index(best_i[:, t, :], best[:, t, :], logits[:, t, 0:E])
                    chain(ins)
                    chain(dve.tensor_copy(best_f[:, :, :], best_i[:, :, :]))
                    if kind == "top1":
                        for t in range(FT):
                            ins = dve.tensor_scalar(gates[:, t, :], W_sb["iota"][:, :], best_f[:, t, 0:1], None, ALU.is_equal)
                        ins.then_inc(S["gates"], 1)
                    else:
                        chain(dve.tensor_copy(total[:, :, :], best[:, :, 0:1]))
                        for t in range(FT):
                            ins = dve.tensor_scalar(best[:, t, :], best[:, t, :], total[:, t, :], None, ALU.subtract)
                        ins.then_inc(S["best"], 1)
                        dve.wait_ge(S["weight"], 1)
                        chain(dve.tensor_reduce(total[:, :, :], weight[:, :, 0:K_TOP], AX.X, ALU.add))
                        chain(dve.reciprocal(inv[:, :, :], total[:, :, :]))
                        for t in range(FT):
                            ins = dve.tensor_scalar(weight[:, t, :], weight[:, t, :], inv[:, t, :], None, ALU.mult)
                        chain(ins)
                        for k in range(K_TOP):
                            for t in range(FT):
                                ins = dve.tensor_scalar(gates[:, t, 0:E] if k == 0 else term[:, t, :], W_sb["iota"][:, :],
                                                        best_f[:, t, k:k + 1], weight[:, t, k:k + 1], ALU.is_equal, ALU.mult)
                            chain(ins)
                            if k:
                                chain(dve.tensor_tensor(gates[:, :, 0:E], gates[:, :, 0:E], term[:, :, :], ALU.add))
                        if kind == "shared":
                            chain(dve.tensor_scalar(sig[:, :, :], sig[:, :, :], 1.0, None, ALU.add))
                            chain(dve.reciprocal(gates[:, :, E:EG], sig[:, :, :]))
                        dve.tensor_copy(total[:, :, :], inv[:, :, :]).then_inc(S["gates"], 1)
                    for k in range(NH):
                        dve.wait_ge(S["act"], k + 1)
                        tb = tile_banks(k)
                        if kind == "shared":
                            chain(dve.tensor_tensor(act_out[:, k, :], act_out[:, k, :], tb[2], ALU.mult))
                        dve.tensor_tensor(hT[:, k, :], act_out[:, k, :], tb[1], ALU.mult).then_inc(S["h"], 1)
                    if kind == "hash":
                        chain(dve.tensor_tensor(flat(x[:, :, :]), flat(x[:, :, :]), flat(z[:, :, :]), ALU.add))
                    dve.wait_ge(S["y_ps"], 1)
                    if kind == "hash":
                        ins = dve.scalar_tensor_tensor(out=flat(res[:, :, :]), in0=banks[1], scalar=W_sb["scale"][:, 0:1],
                                                       in1=flat(x[:, :, :]), op0=ALU.mult, op1=ALU.add)
                    else:
                        ins = dve.tensor_tensor(flat(res[:, :, :]), banks[1], flat(x[:, :, :]), ALU.add)
                    ins.then_inc(S["res"], 1)
                    S.end_iteration(dve, "dve")

            @block.gpsimd
            def _(pool):
                with pool.Fori(0, FSTEPS) as i:
                    for k in range(1 + (kind == "top1")):
                        ln_rstd(pool, S, L, k, FT)
                    S.end_iteration(pool, "pool")


ROUND = 1.5 * 2.0 ** 23


def bit_ffn(nc, G, stage, x_in, out, w):
    KH = w["w1"].shape[1] // P
    NB = FTOK // TOK
    with ExitStack() as ctx:
        sb = Mem(nc, ctx, stage)
        banks = Banks(G).all
        W_sb = {n: sb(n, list(w[n].shape)) for n in ("w1", "w2", "conv_w", "conv_b")}
        x, z, res = (sb(n, [P, FT, C]) for n in ("x", "z", "res"))
        top, unit, per = (sb(n, [P, FT, 1]) for n in ("top", "unit", "per"))
        zT = sb("zT", [C, FTOK])
        hp = sb("hp", [P, KH, NB, TOK + 2])
        cv = sb("cv", [P, KH, NB, TOK])
        sT = sb("sT", [P, KH, FTOK])
        s_tok = sb("s_tok", [P, FT, KH * P])
        ones = sb("ones", [P, P])
        wsum, wall, wstep, wper = (sb(n, [P, 2]) for n in ("wsum", "wall", "wstep", "wper"))
        L = LnMem(sb, FT)
        S = Sems(nc, ctx, stage, ["x_in", "z", "zT_ps", "zT", "h_ps", "hp", "cv", "sT", "st_ps", "s_tok", "sq", "sqT_ps",
                                  "sqT", "y_ps", "res", "x_out", "dve_own"] + LN_SEMS)

        def prepare(pool, chain):
            chain(pool.memset(hp[:, :, :, :], 0.0))
            chain(pool.memset(ones[:, :], 1.0))
            L.prepare(pool, chain)

        load_weights(nc, ctx, stage, [(W_sb[n][...], w[n]) for n in W_sb], prepare)

        s_sum, s_all = (ctx.enter_context(nc.semaphore(f"{stage}_{n}")) for n in ("wsum", "wall"))
        s_own = ctx.enter_context(nc.semaphore(f"{stage}_wown"))
        with nc.Block() as block:
            @block.tensor
            def _(pe):
                pe.wait_ge(s_sum, 1)
                pe.sem_clear(s_sum)
                pe.matmul(banks[0][:, 0:2], ones[:, :], wsum[:, :], start=True, stop=True).then_inc(s_all, 1)

            @block.vector
            def _(dve):
                chain = Chain(dve, s_own)
                both = [W_sb["w1"][:, :], W_sb["w2"][:, :, :].rearrange("p k c -> p (k c)")]
                for j, m in enumerate(both):
                    ins = dve.tensor_reduce(wsum[:, j:j + 1], m, AX.X, ALU.add, apply_absolute_value=True)
                ins.then_inc(s_sum, 1)
                dve.wait_ge(s_all, 1)
                dve.sem_clear(s_all)
                chain(dve.tensor_scalar(wper[:, :], banks[0][:, 0:2], 1.0 / (KH * P * C), 1e-5, ALU.mult, ALU.max))
                chain(dve.reciprocal(wstep[:, :], wper[:, :]))
                for j, m in enumerate(both):
                    chain(dve.tensor_scalar(m, m, wstep[:, j:j + 1], ROUND, ALU.mult, ALU.add))
                    chain(dve.tensor_scalar(m, m, ROUND, 1.0, ALU.subtract, ALU.min))
                    chain(dve.tensor_scalar(m, m, -1.0, wper[:, j:j + 1], ALU.max, ALU.mult))
                dve.sem_clear(s_own)

        def quantise(dve, chain, tiles):
            for t, m in enumerate(tiles):
                ins = dve.tensor_reduce(top[:, t, :], m, AX.X, ALU.max, apply_absolute_value=True)
            chain(ins)
            chain(dve.tensor_scalar(top[:, :, :], top[:, :, :], 1e-5, None, ALU.max))
            chain(dve.reciprocal(unit[:, :, :], top[:, :, :]))
            chain(dve.tensor_scalar(unit[:, :, :], unit[:, :, :], 127.0, None, ALU.mult))
            chain(dve.reciprocal(per[:, :, :], unit[:, :, :]))
            for t, m in enumerate(tiles):
                ins = dve.tensor_scalar(m, m, unit[:, t, :], ROUND, ALU.mult, ALU.add)
            chain(ins)
            for t, m in enumerate(tiles):
                ins = dve.tensor_scalar(m, m, ROUND, 127.0, ALU.subtract, ALU.min)
            chain(ins)
            for t, m in enumerate(tiles):
                ins = dve.tensor_scalar(m, m, -128.0, per[:, t, :], ALU.max, ALU.mult)
            return ins

        with nc.Block() as block:
            @block.sync
            def _(sp):
                with sp.Fori(0, FSTEPS) as i:
                    sp.dma_start(x[:, :, :], token_tiles(x_in)[i]).then_inc(S["x_in"], 16)
                    sp.wait_ge(S["res"], 1)
                    sp.dma_start(token_tiles(out)[i], res[:, :, :]).then_inc(S["x_out"], 16)
                    sp.wait_ge(S["x_out"], 16)
                    S.next_iteration(sp)

            @block.tensor
            def _(pe):
                with pe.Fori(0, FSTEPS) as i:
                    pe.wait_ge(S["z"], 1)
                    transpose_tiles(pe, banks[4], [z[:, t, :] for t in range(FT)], G.ident).then_inc(S["zT_ps"], 1)
                    pe.wait_ge(S["zT"], 1)
                    for k in range(KH):
                        pe.matmul(banks[k], W_sb["w1"][:, k * P:(k + 1) * P], zT[:, :], start=True, stop=True).then_inc(S["h_ps"], 1)
                    pe.wait_ge(S["hp"], KH)
                    pe.wait_ge(S["sT"], KH)
                    for t in range(FT):
                        for k in range(KH):
                            ins = pe.transpose(banks[t][:, k * P:(k + 1) * P], sT[:, k, t * P:(t + 1) * P], G.ident[:, :])
                        ins.then_inc(S["st_ps"], 1)
                    pe.wait_ge(S["sq"], 1)
                    for k in range(KH):
                        for t in range(FT):
                            ins = pe.transpose(banks[4 + k][:, t * P:(t + 1) * P], s_tok[:, t, k * P:(k + 1) * P], G.ident[:, :])
                        ins.then_inc(S["sqT_ps"], 1)
                    pe.wait_ge(S["sqT"], KH)
                    for t in range(FT):
                        for k in range(KH):
                            ins = pe.matmul(banks[0][:, t * C:(t + 1) * C], sT[:, k, t * P:(t + 1) * P], W_sb["w2"][:, k, :],
                                            start=(k == 0), stop=(k == KH - 1))
                    ins.then_inc(S["y_ps"], 1)
                    S.end_iteration(pe, "pe")

            @block.scalar
            def _(act):
                with act.Fori(0, FSTEPS) as i:
                    act.wait_ge(S["zT_ps"], 1)
                    act.activation(zT[:, :], banks[4], ACT.Copy).then_inc(S["zT"], 1)
                    for k in range(KH):
                        act.wait_ge(S["h_ps"], k + 1)
                        act.activation(hp[:, k, :, 1:TOK + 1], banks[k].rearrange("p (b t) -> p b t", b=NB),
                                       ACT.Copy).then_inc(S["hp"], 1)
                    for k in range(KH):
                        act.wait_ge(S["cv"], k + 1)
                        act.activation(sT[:, k, :], cv[:, k, :, :].rearrange("p b t -> p (b t)"), ACT.Silu,
                                       bias=W_sb["conv_b"][:, k:k + 1]).then_inc(S["sT"], 1)
                    for t in range(FT):
                        act.wait_ge(S["st_ps"], t + 1)
                        act.activation(s_tok[:, t, :], banks[t], ACT.Copy).then_inc(S["s_tok"], 1)
                    for k in range(KH):
                        act.wait_ge(S["sqT_ps"], k + 1)
                        act.activation(sT[:, k, :], banks[4 + k], ACT.Copy).then_inc(S["sqT"], 1)
                    S.end_iteration(act, "act")

            @block.vector
            def _(dve):
                with dve.Fori(0, FSTEPS) as i:
                    chain = Chain(dve, S["dve_own"])
                    L.begin(chain)
                    dve.wait_ge(S["x_in"], 16)
                    ln_stats(dve, S, L, [x[:, t, :] for t in range(FT)])
                    for t in range(FT):
                        ins = ln_apply(dve, L, t, z[:, t, :], x[:, t, :])
                    chain(ins)
                    quantise(dve, chain, [z[:, t, :] for t in range(FT)]).then_inc(S["z"], 1)
                    for k in range(KH):
                        dve.wait_ge(S["hp"], k + 1)
                        chain(dve.tensor_scalar(cv[:, k, :, :], hp[:, k, :, 0:TOK], W_sb["conv_w"][:, k, 0:1], None, ALU.mult))
                        for j in (1, 2):
                            ins = dve.scalar_tensor_tensor(out=cv[:, k, :, :], in0=hp[:, k, :, j:j + TOK],
                                                           scalar=W_sb["conv_w"][:, k, j:j + 1], in1=cv[:, k, :, :],
                                                           op0=ALU.mult, op1=ALU.add)
                            if j == 1:
                                chain(ins)
                        ins.then_inc(S["cv"], 1)
                    dve.wait_ge(S["s_tok"], FT)
                    quantise(dve, chain, [s_tok[:, t, :] for t in range(FT)]).then_inc(S["sq"], 1)
                    dve.wait_ge(S["y_ps"], 1)
                    dve.tensor_tensor(flat(res[:, :, :]), banks[0], flat(x[:, :, :]), ALU.add).then_inc(S["res"], 1)
                    S.end_iteration(dve, "dve")

            @block.gpsimd
            def _(pool):
                with pool.Fori(0, FSTEPS) as i:
                    ln_rstd(pool, S, L, 0, FT)
                    S.end_iteration(pool, "pool")


def stages(nc, G, d, sub, out):
    def scratch(name):
        return nc.dram_tensor(f"{name}_dram", [BATCH, TOK, C], F32, kind="Internal").ap()

    x = [d["x"]] + [scratch(f"x_after_{i}") for i in range(7)] + [out]
    own_x1, own_xo, mid_x, cross_xo = (scratch(n) for n in ("own_x1", "own_xo", "mid_x", "cross_xo"))
    attention8(nc, G, "a0", x[0], x[1], sub("a0_"), True)
    experts(nc, G, "f0", x[1], x[2], sub("f0_"), "hash")
    attention8(nc, G, "a1", x[2], x[3], sub("a1_"), False)
    bit_ffn(nc, G, "f1", x[3], x[4], sub("f1_"))
    attention32(nc, G, "own", x[4], own_x1, own_xo, sub("own_"), True)
    mlp32(nc, G, "own_mlp", own_xo, own_x1, None, mid_x, sub("own_"), True)
    attention32(nc, G, "cross", mid_x, None, cross_xo, sub("cross_"), False)
    mlp32(nc, G, "cross_mlp", cross_xo, mid_x, x[4], x[5], sub("cross_"), False)
    experts(nc, G, "f2", x[5], x[6], sub("f2_"), "top1")
    attention8(nc, G, "a3", x[6], x[7], sub("a3_"), False)
    experts(nc, G, "f3", x[7], x[8], sub("f3_"), "shared")



class Globals:
    pass


def program(nc, d, out):
    with ExitStack() as ctx:
        G = Globals()
        G.S4 = ctx.enter_context(nc.psum_tensor("scores_ps", [P, 2, 2, 512], F32))
        G.bank = [ctx.enter_context(nc.psum_tensor(f"bank{i}", [P, 512], F32)) for i in range(4)]
        sb = Mem(nc, ctx, "shared")
        G.ident = sb("ident", [P, P])
        G.spread32 = sb("spread32", [97, 97])
        G.past = sb("past", [P, QT, TOK])
        load_weights(nc, ctx, "shared", [(G.ident[:, :], d["ident"]),
                                         (G.spread32[:, :], d["spread32"]), (G.past[:, :, :], d["past"])])
        G.ctxT, G.ctx = d["ctxT"], d["ctx_512"]
        G.row_of = d["row_of"]
        sub = lambda pre: {k[len(pre):]: v for k, v in d.items() if k.startswith(pre)}
        stages(nc, G, d, sub, out)



def layout(i):
    import numpy as np

    f = np.float32
    a = {"x": i["x"], "ctx_512": i["ctx_512"], "ctxT": i["ctx_512"].transpose(0, 2, 1)}
    a["ident"] = np.eye(P, dtype=f)
    r = np.arange(P)
    a["spread32"] = np.repeat((np.arange(97) == 96).astype(f)[:, None], 97, axis=1)
    q = (np.arange(QT)[None, :, None] * P + r[:, None, None])
    a["past"] = np.where(np.arange(TOK)[None, None, :] <= q, f(0), f(-1e30)).astype(f)

    def rep(v, n=1):
        return np.broadcast_to(np.tile(v, n), (P, n * v.size))

    def col(v):
        return v.reshape(-1, 1) if v.size <= P else v.reshape(-1, P).T

    def bcol(v):
        return np.broadcast_to(v.reshape(-1, 1), (v.size, P))

    z = np.zeros(C, f)
    n = "L0_xattn_"
    a.update({"a0_wq_s": i[n + "Wq"], "a0_wk_s": i[n + "Wk"], "a0_wv_s": i[n + "Wv"], "a0_bq_s": col(i[n + "bq"]),
              "a0_bk_s": col(i[n + "bk"]), "a0_bv_s": bcol(i[n + "bv"]),
              "a0_wq_c": i[n + "Wcq"], "a0_wk_c": i[n + "Wck"], "a0_wv_c": i[n + "Wcv"], "a0_bq_c": col(i[n + "bcq"]),
              "a0_bk_c": col(i[n + "bck"]), "a0_bv_c": bcol(i[n + "bcv"]),
              "a0_w_plain": i[n + "Wp"], "a0_b_out": rep(i[n + "bp"])})
    n = "L1_xattn_"
    a.update({"a1_wq_c": i[n + "Wq"].T, "a1_wk_c": i[n + "Wkv"][0:C].T, "a1_wv_c": i[n + "Wkv"][C:].T,
              "a1_bq_c": col(z), "a1_bk_c": col(z), "a1_bv_c": bcol(z),
              "a1_w_plain": i[n + "Wo"].T, "a1_b_out": rep(z)})
    n = "L3_xattn_"
    a.update({"a3_wq_c": i[n + "Wq"], "a3_wk_c": i[n + "Wk"], "a3_wv_c": i[n + "Wv"], "a3_bq_c": col(i[n + "bq"]),
              "a3_bk_c": col(i[n + "bk"]), "a3_bv_c": bcol(i[n + "bv"]),
              "a3_w_plain": i[n + "Wo"], "a3_b_out": rep(i[n + "bo"])})
    for stage, pre in (("own_", "L2_xattn_a1_"), ("cross_", "L2_xattn_a2_")):
        for m in "qkv":
            a[stage + "w" + m] = i[pre + "w" + m].transpose(1, 0, 2).reshape(i[pre + "w" + m].shape[1], -1)
        o = np.zeros((97, HEADS, C), f)
        for part in range(3):
            o[32 * part:32 * part + 32] = i[pre + "li1_w"].reshape(HEADS, 32, C).transpose(1, 0, 2)
        a.update({stage + "w_out": o, stage + "b_out": rep(i[pre + "li1_b"]),
                  stage + "li2_w": i[pre + "li2_w"], stage + "li2_b": col(i[pre + "li2_b"]),
                  stage + "li3_w": i[pre + "li3_w"].reshape(-1, P, C).transpose(1, 0, 2),
                  stage + "li3_b": rep(i[pre + "li3_b"])})
        for v in ("lnx", "lny", "ln3"):
            a[f"{stage}{v}_g"], a[f"{stage}{v}_b"] = col(i[f"{pre}{v}_g"]), col(i[f"{pre}{v}_b"])
    for v in ("ln1", "ln2"):
        a[f"own_{v}_g"], a[f"own_{v}_b"] = rep(i[f"L2_xattn_{v}_g"]), rep(i[f"L2_xattn_{v}_b"])
    a["row_of"] = np.broadcast_to(np.eye(P, dtype=f)[:, 0:4, None], (P, 4, P))

    def spread(experts, hidden):
        return np.repeat(np.eye(experts, dtype=f), hidden, axis=1)

    def iota(n):
        return np.broadcast_to(np.arange(n, dtype=f), (P, n))

    def down(v):
        return v.reshape(-1, P, C).transpose(1, 0, 2)

    n = "L0_ffn_"
    a.update({"f0_hasher": i[n + "hasher_w"].T, "f0_keys": i[n + "keys"].T,
              "f0_scale": np.broadcast_to(i[n + "scale"], (P, 1)),
              "f0_w_up": i[n + "values_down"].transpose(1, 0, 2).reshape(C, -1),
              "f0_w_down": down(i[n + "values_up"].reshape(-1, C)), "f0_spread": spread(32, 32), "f0_iota": iota(32)})
    n = "L1_ffn_"
    a.update({"f1_w1": i[n + "w1"].T, "f1_w2": down(i[n + "w2"].T),
              "f1_conv_w": i[n + "conv_w"].reshape(-1, P, 3).transpose(1, 0, 2), "f1_conv_b": col(i[n + "conv_b"])})
    n = "L2_ffn_"
    a.update({"f2_gate": i[n + "Wg"].T, "f2_ln_scale": i[n + "ln_scale"].T, "f2_ln_bias": i[n + "ln_bias"].T,
              "f2_b1": col(i[n + "b1"].reshape(-1)), "f2_b2": i[n + "b2"],
              "f2_w_up": i[n + "W1"].transpose(1, 0, 2).reshape(C, -1), "f2_w_down": down(i[n + "W2"].reshape(-1, C)),
              "f2_spread": spread(8, 32), "f2_iota": iota(8)})
    n = "L3_ffn_"
    share = np.zeros((17, 256), f)
    share[16] = 1
    a.update({"f3_gate": np.concatenate([i[n + "Wg"], i[n + "Wsg"]]).T,
              "f3_w_gate": np.concatenate([i[n + "We_gate"].reshape(-1, C), i[n + "Ws_gate"]]).T,
              "f3_w_up": np.concatenate([i[n + "We_up"].reshape(-1, C), i[n + "Ws_up"]]).T,
              "f3_w_down": down(np.concatenate([i[n + "We_down"].transpose(0, 2, 1).reshape(-1, C), i[n + "Ws_down"].T])),
              "f3_spread": np.concatenate([np.pad(spread(16, 64), ((0, 1), (0, 0))), share], axis=1),
              "f3_iota": iota(16)})
    return {k: np.ascontiguousarray(v) for k, v in a.items()}


def kernel(**inputs):
    import numpy as np
    import concourse.bacc as bacc
    from concourse.bass_utils import run_bass_kernel_spmd

    nc = bacc.Bacc("TRN2", target_bir_lowering=False, num_devices=1)
    arrays = layout({k: np.asarray(v) for k, v in inputs.items()})
    d = {k: nc.dram_tensor(f"in_{k}", v.shape, mybir.dt.from_np(v.dtype), kind="ExternalInput").ap()
         for k, v in arrays.items()}
    out = nc.dram_tensor("out_0", (BATCH, TOK, C), F32, kind="ExternalOutput").ap()
    program(nc, d, out)
    r = run_bass_kernel_spmd(nc, [{f"in_{k}": v for k, v in arrays.items()}], core_ids=[0])
    return r.results[0]["out_0"]
```

```python
from contextlib import ExitStack

import concourse.bass as bass
from concourse import mybir

F32 = mybir.dt.float32
BF16 = mybir.dt.bfloat16
U32 = mybir.dt.uint32
ALU = mybir.AluOpType
ACT = mybir.ActivationFunctionType
AX = mybir.AxisListType

P = 128
BATCH, TOK, C, CC, NKEY = 16, 256, 128, 64, 1601
HEADS = 16
QUADS = HEADS // 4
QT = TOK // P
FTOK = 512
FT = FTOK // P
FSTEPS = BATCH * TOK // FTOK
EPS = 1e-5
K_PART = (0, 0, 0, 1, 1, 2)
Q_PART = (0, 1, 2, 0, 1, 0)
SLOTS = len(K_PART)
MAXROW = P - 1
V8 = 9
P_BUFS = 5
LAG = 2
LAG8 = 3


def key_tiles(nk):
    return [(t * P, min(P, nk - t * P)) for t in range((nk + P - 1) // P)]


def key_chunks(nk):
    n = (nk + 511) // 512
    cuts = [nk * i // n for i in range(n + 1)]
    return [(cuts[i], cuts[i + 1] - cuts[i]) for i in range(n)]


class Sems:

    def __init__(self, nc, ctx, stage, names):
        self.work = {n: ctx.enter_context(nc.semaphore(f"{stage}_{n}")) for n in names + ["iter_done"]}
        self.go = {e: ctx.enter_context(nc.semaphore(f"{stage}_go_{e}")) for e in ("pe", "act", "dve", "pool")}

    def __getitem__(self, name):
        return self.work[name]

    def end_iteration(self, eng, who):
        eng.drain().then_inc(self["iter_done"], 1)
        eng.wait_ge(self.go[who], 1)
        eng.sem_clear(self.go[who])

    def next_iteration(self, sp):
        sp.wait_ge(self["iter_done"], 4)
        nums = sorted(s.num for s in self.work.values())
        if nums[-1] - nums[0] + 1 == len(nums):
            sp.sem_clear(range(nums[0], nums[-1] + 1))
        else:
            for s in self.work.values():
                sp.sem_clear(s)
        for s in self.go.values():
            sp.sem_inc(s, 1)


class Chain:

    def __init__(self, eng, sem):
        self.eng, self.sem, self.n = eng, sem, 0

    def __call__(self, ins):
        ins.then_inc(self.sem, 1)
        self.n += 1
        self.eng.wait_ge(self.sem, self.n)


class Mem:

    def __init__(self, nc, ctx, stage):
        self.nc, self.ctx, self.stage = nc, ctx, stage

    def __call__(self, name, shape, dt=F32):
        return self.ctx.enter_context(self.nc.sbuf_tensor(f"{self.stage}_{name}", shape, dt))


def load_weights(nc, ctx, stage, pairs, prepare=None):
    s_w = ctx.enter_context(nc.semaphore(f"{stage}_weights"))
    s_c = ctx.enter_context(nc.semaphore(f"{stage}_constants"))
    with nc.Block() as block:
        @block.sync
        def _(sp):
            for dst, src in pairs:
                sp.dma_start(dst, src).then_inc(s_w, 16)
            sp.wait_ge(s_w, 16 * len(pairs))
            sp.sem_clear(s_w)

        @block.gpsimd
        def _(pool):
            if prepare:
                prepare(pool, Chain(pool, s_c))
                pool.sem_clear(s_c)



def ln_stats(dve, S, L, tiles, rows=None):
    for t, x in enumerate(tiles):
        ins = dve.bn_stats(L.st[0:x.shape[0], t, :], x)
    L.chain(ins)
    for t, x in enumerate(tiles):
        ins = dve.bn_aggr(L.mv[0:x.shape[0], t, :], L.st[0:x.shape[0], t, :])
    ins.then_inc(S["ln_var"], 1)
    L.count += 1
    dve.wait_ge(S["ln_rstd"], L.count)


def ln_apply(dve, L, t, out, x):
    n = x.shape[0]
    return dve.tensor_scalar(out, x, L.mv[0:n, t, 0:1], L.rs[0:n, t, 0:1], ALU.subtract, ALU.mult)


def ln_rstd(pool, S, L, k, nt):
    pool.wait_ge(S["ln_var"], k + 1)
    pool.tensor_scalar(L.ve[:, 0:nt, :], L.mv[:, 0:nt, 1:2], EPS, None, ALU.add).then_inc(S["ln_eps"], 1)
    pool.wait_ge(S["ln_eps"], k + 1)
    pool.tensor_tensor(L.rs[:, 0:nt, :], L.ve[:, 0:nt, :], L.mh[:, 0:nt, :], ALU.pow).then_inc(S["ln_rstd"], 1)


LN_SEMS = ["ln_var", "ln_eps", "ln_rstd"]


class LnMem:
    def __init__(self, sb, n):
        self.n = n
        self.st = sb("ln_st", [P, n, 6])
        self.mv = sb("ln_mv", [P, n, 2])
        self.ve = sb("ln_ve", [P, n, 1])
        self.rs = sb("ln_rs", [P, n, 1])
        self.mh = sb("ln_mh", [P, n, 1])

    def prepare(self, pool, chain):
        chain(pool.memset(self.mh[:, :, :], -0.5))
        chain(pool.memset(self.mv[:, :, :], 0.0))

    def begin(self, chain):
        self.chain, self.count = chain, 0



class Source:

    def __init__(self, nk, mask, idx0, unit0, quad0):
        self.nk, self.mask = nk, mask
        self.tiles, self.chunks = key_tiles(nk), key_chunks(nk)
        self.T = len(self.tiles)
        self.NU = QT * 4 * len(self.chunks)
        self.idx0, self.unit0, self.quad0 = idx0, unit0, quad0

    def unit(self, k):
        nc_ = len(self.chunks)
        return k // (4 * nc_), k // nc_ % 4, k % nc_

    def schedule(self):
        last_unit, turn = (self.T - 4, self.T - 2) if self.T > 4 else (0, self.T - 1)
        steps = [(g, t) for g in range(QUADS) for t in range(self.T)]
        plan = [("unit", 0, k) for k in range(self.NU)] + [("turn", 0, 0)]
        for n, (g, t) in enumerate(steps):
            plan.append(("scores", g, t))
            if g + 1 < QUADS and t <= last_unit:
                plan += [("unit", g + 1, k) for k in range(self.NU * t // (last_unit + 1),
                                                           self.NU * (t + 1) // (last_unit + 1))]
            if g + 1 < QUADS and t == turn:
                plan.append(("turn", g + 1, 0))
            if n >= LAG:
                plan.append(("pv",) + steps[n - LAG])
        plan += [("pv",) + s for s in steps[-LAG:]]
        return plan


CORE_SEMS = ["max_scores", "max_taken", "max_rows", "max_turned", "max_ready", "scores", "probs", "masked", "rest",
             "pv", "heads_out", "sums_wide", "sums_inv", "heads_ok", "proj"]


def make_sources(specs):
    out, i, u, q = [], 0, 0, 0
    for nk, mask in specs:
        s = Source(nk, mask, i, u, q)
        out.append(s)
        i, u, q = i + QUADS * s.T, u + QUADS * s.NU, q + QUADS
    return out


def core_pe(pe, S, A, s):
    def unit(g, k):
        u = s.unit0 + g * s.NU + k
        qt, h, c = s.unit(k)
        c0, n = s.chunks[c]
        if k == 0 and s.quad0 + g >= 1:
            pe.wait_ge(S["max_ready"], s.quad0 + g)
        if u >= 2:
            pe.wait_ge(S["max_taken"], u - 1)
        pe.matmul(A.bank[2 + u % 2][:, 0:n], A.q_max(s, g, h, qt), A.k_max(s, g, h, c0, n),
                  start=True, stop=True).then_inc(S["max_scores"], 1)

    def turn(g):
        pe.wait_ge(S["max_rows"], s.quad0 + g + 1)
        for qt in range(QT):
            ins = pe.transpose(A.bank[2][0:4, qt * P:(qt + 1) * P], A.negmax[:, qt, :], A.ident[:, :])
        ins.then_inc(S["max_turned"], 1)

    def scores(g, t):
        i = s.idx0 + g * s.T + t
        if i >= 2:
            pe.wait_ge(S["probs"], i - 1)
        if t == 0:
            A.wait_max(pe, s.quad0 + g)
        for h in range(4):
            k0, n = s.tiles[t]
            ins = A.scores(pe, A.S4[0:n, i % 2, h % 2, h // 2 * TOK:(h // 2 + 1) * TOK], s, g, h, k0, n)
        ins.then_inc(S["scores"], 1)

    def pv(g, t):
        i = s.idx0 + g * s.T + t
        pe.wait_ge(S["rest"], i + 1)
        if t == 0:
            A.wait_out(pe, s.quad0 + g)
        A.pv(pe, s, g, t, i % P_BUFS).then_inc(S["pv"], 1)

    for what, g, j in s.schedule():
        {"unit": unit, "turn": lambda g, _: turn(g), "scores": scores, "pv": pv}[what](g, j)


def core_act(act, S, A, s):
    for what, g, t in s.schedule():
        i = s.idx0 + g * s.T + t
        if what == "scores":
            act.wait_ge(S["scores"], i + 1)
            if i >= P_BUFS:
                act.wait_ge(S["pv"], i - P_BUFS + 1)
            n = s.tiles[t][1]
            act.activation(A.probs[0:n, i % P_BUFS, :].rearrange("p (a q) -> p a q", a=2), A.S4[0:n, i % 2, :, :],
                           ACT.Exp, scale=A.scale).then_inc(S["probs"], 1)
        if what == "pv" and t == s.T - 1:
            act.wait_ge(S["pv"], i + 1)
            A.take_out(act, s.quad0 + g).then_inc(S["heads_out"], 1)


def core_pool(pool, S, A, s):
    for g in range(QUADS):
        for t in range(s.T):
            i = s.idx0 + g * s.T + t
            k0, n = s.tiles[t]
            b = i % P_BUFS
            if i:
                pool.wait_ge(S["rest"], i)
            pool.wait_ge(S["probs"], i + 1)
            pr = A.probs[0:n, b, :]
            if s.mask == "causal":
                pool.affine_select(out=pr, in_=pr, pattern=[[0, 4], [1, TOK]], compare_op=ALU.is_ge, fill=0.0,
                                   base=-k0, channel_multiplier=-1).then_inc(S["masked"], 1)
                pool.wait_ge(S["masked"], i + 1)
            if s.mask == "after":
                pool.affine_select(out=A.kept[0:n, b, :], in_=pr, pattern=[[0, 4], [-1, TOK]], compare_op=ALU.is_gt,
                                   fill=0.0, base=k0, channel_multiplier=1).then_inc(S["masked"], 1)
                pool.wait_ge(S["masked"], i + 1)
                pool.tensor_tensor(A.kept_rest[0:n, b, :], A.kept[0:n, b, :], A.high(A.kept, b, n), ALU.subtract)
            pool.tensor_tensor(A.rest[0:n, b, :], pr, A.high(A.probs, b, n), ALU.subtract).then_inc(S["rest"], 1)


def core_dve(dve, S, A, s, chain):
    for what, g, k in s.schedule():
        if what == "unit":
            u = s.unit0 + g * s.NU + k
            qt, h, c = s.unit(k)
            n = s.chunks[c][1]
            dve.wait_ge(S["max_scores"], u + 1)
            if s.mask == "causal":
                if u:
                    dve.wait_ge(S["max_taken"], u)
                dve.tensor_tensor_reduce(A.junk[:, 0:n], A.bank[2 + u % 2][:, 0:n], A.past[:, qt, :], 1.0, -3.0e38,
                                         ALU.add, ALU.max, A.unit_max[:, qt, h, c:c + 1]).then_inc(S["max_taken"], 1)
            else:
                dve.tensor_reduce(A.unit_max[:, qt, h, c:c + 1], A.bank[2 + u % 2][:, 0:n], AX.X,
                                  ALU.max).then_inc(S["max_taken"], 1)
            if k == s.NU - 1:
                dve.wait_ge(S["max_taken"], u + 1)
                dve.tensor_reduce(A.negmax[:, :, :], A.unit_max[:, :, :, 0:len(s.chunks)], AX.X, ALU.max,
                                  negate=True).then_inc(S["max_rows"], 1)
        if what == "turn":
            dve.wait_ge(S["max_turned"], s.quad0 + g + 1)
            dve.tensor_copy(A.negmax_row[0:4, (s.quad0 + g) % 2, :],
                            A.bank[2][0:4, 0:TOK]).then_inc(S["max_ready"], 1)


def tail_pe(pe, S, A, n):
    for k in range(n):
        if k == 0:
            pe.wait_ge(S["heads_out"], A.quads)
        if k >= 4:
            pe.wait_ge(S["sums_inv"], k - 3)
        pe.matmul(A.S4[0:A.rows, k % 4 // 2, k % 2, :], A.spread[:, :], A.heads[:, 2 * k:2 * k + 2, :],
                  start=True, stop=True).then_inc(S["sums_wide"], 1)
    pe.wait_ge(S["heads_ok"], n)
    for qt in range(QT):
        for k in range(2 * n):
            ins = pe.matmul(A.bank[3][:, qt * C:(qt + 1) * C], A.heads[:, k, qt * P:(qt + 1) * P], A.w_out(k),
                            start=(k == 0), stop=(k == 2 * n - 1))
    ins.then_inc(S["proj"], 1)


def tail_dve(dve, S, A, n):
    for k in range(n):
        dve.wait_ge(S["sums_wide"], k + 1)
        inv = A.inv[:, k % 2, :]
        dve.reciprocal(inv, A.S4[0:A.rows, k % 4 // 2, k % 2, :]).then_inc(S["sums_inv"], 1)
        dve.wait_ge(S["sums_inv"], k + 1)
        v = A.heads[:, 2 * k:2 * k + 2, :].rearrange("p g q -> p (g q)")
        dve.tensor_tensor(v, v, inv, ALU.mult).then_inc(S["heads_ok"], 1)
    dve.wait_ge(S["proj"], 1)


class Core:

    def __init__(self, G, sb, scale, bufs=P_BUFS):
        self.S4, self.bank, self.ident = G.S4, G.bank, G.ident
        self.scale = scale
        self.probs = sb("probs", [P, bufs, 4 * TOK])
        self.rest = sb("rest", [P, bufs, 4 * TOK], BF16)
        self.unit_max = sb("unit_max", [P, QT, 4, 4])
        self.negmax = sb("negmax", [P, QT, 4])
        self.negmax_row = sb("negmax_row", [4, 2, TOK], BF16)

    def high(self, t, b, n):
        return t[0:n, b, :].bitcast(BF16)[:, 1::2]

    @staticmethod
    def place(h):
        return slice(h % 2 * 512 + h // 2 * TOK, h % 2 * 512 + (h // 2 + 1) * TOK)



POOL_COLS = 704
POOL_HEADS = 2
PIECES = 4


class Ev:

    def __init__(self, kind, s=None, g=0, t=0, i=0, k=0, nxt=False, job=None, src=0, j=0, c=0, part=0, quad=0, r=0):
        self.kind, self.s, self.g, self.t, self.i, self.k, self.nxt = kind, s, g, t, i, k, nxt
        self.job, self.src, self.j, self.c, self.part, self.quad, self.r = job, src, j, c, part, quad, r


def schedule8(sources, side, with_core, with_next):
    cross, own = sources[0], sources[1:]
    steps = [(s, g, t) for s in sources for g in range(QUADS) for t in range(s.T)] if with_core else []
    turns, plan = {}, []

    windows, at = [], 0
    for g in range(1, QUADS):
        windows.append((cross, g, False, at, cross.T * g - 2))
        at = cross.T * g - 2
    for s in own:
        for g in range(QUADS):
            windows.append((s, g, False, at, at + 2 + g // (QUADS - 1)))
            at += 2 + g // (QUADS - 1)
    if not steps:
        windows, at = [], max(n for n, _, _ in side) + 1
    if with_next:
        windows.append((cross, 0, True, at, max(at + 1, len(steps) - 2)))

    def step(n, scores=None):
        for s, g, nxt, start, end in windows:
            if n == end:
                turns[s, g, nxt] = len(turns)
                plan.append(Ev("side", s=s, g=g, nxt=nxt, job="turn"))
        units = [Ev("unit", s=s, g=g, k=k, nxt=nxt) for s, g, nxt, start, end in windows for k in range(s.NU)
                 if start + k * (end - start) // s.NU == n]
        plan.extend(units[0:2] + ([scores] if scores else []) + units[2:])
        for when, kind, k in side:
            if when == n and (with_core if kind in ENDING8 else with_next):
                plan.append(Ev("side" if kind not in OTHER8 else kind, job=kind, **k))

    for n, (s, g, t) in enumerate(steps):
        step(n, Ev("scores", s=s, g=g, t=t, i=n))
        if n >= 1:
            plan.append(Ev("rest", i=n - 1))
        if n >= LAG8:
            ps, pg, pt = steps[n - LAG8]
            plan.append(Ev("pv", s=ps, g=pg, t=pt, i=n - LAG8))
    if steps:
        plan.append(Ev("rest", i=len(steps) - 1))
        for i in range(len(steps) - LAG8, len(steps)):
            plan.append(Ev("pv", s=steps[i][0], g=steps[i][1], t=steps[i][2], i=i))
    for n in range(len(steps), max(len(steps) + 8, at + 2)):
        step(n)

    u = k = q = 0
    for e in plan:
        if e.kind == "unit":
            e.u, e.last = u, e.k == e.s.NU - 1
            u += 1
        if e.kind == "side":
            e.n = k
            k += 1
            if e.job == "turn":
                e.q = q
                q += 1
        if e.kind == "scores":
            e.turn = turns.get((e.s, e.g, False)) if e.t == 0 else None
    return plan, q


OTHER8 = ("ln_stats", "ln_rstd", "ln_apply", "part0", "left", "part1", "part2", "write", "stack", "v_first", "v_left",
          "v_second", "v_third", "divide")
ENDING8 = ("divide", "heads_turned", "proj")


def attention8(nc, G, stage, x_in, x_out, w, with_self):
    sources = make_sources([(NKEY, None)] + [(TOK, "causal")] * with_self)
    ns = len(sources)
    cross = sources[0]
    q_col = [i * TOK for i in range(ns)]
    k_col = [ns * TOK + sum(s.nk for s in sources[:i]) for i in range(ns)]
    W = ns * TOK + sum(s.nk for s in sources)
    n_steps = QUADS * sum(s.T for s in sources)
    n_quads = QUADS * ns
    parts_dram = nc.dram_tensor(f"{stage}_parts_dram", [3, P, W], BF16, kind="Internal").ap()

    def last_step(quad):
        return sum(s.T for s in sources for g in range(QUADS) if sources.index(s) * QUADS + g <= quad)

    side = [(1 + c, "k_cross", {"c": c}) for c in range(len(cross.chunks))]
    side += [(5 + j, "v_cross", {"j": j}) for j in range((cross.T + 3) // 4)]
    side += [(3, "ln_stats", {}), (5, "ln_rstd", {}), (8, "ln_apply", {}), (10, "x_turned", {}), (12, "q", {})]
    if with_self:
        side += [(13, "k_own", {}), (14, "v_own", {})]
    for j in range(PIECES):
        side += [(15 + j, "part0", {"j": j}), (16 + j, "left", {"j": j}), (17 + j, "part1", {"j": j}), (18 + j, "part2", {"j": j})]
    side += [(16 + PIECES + k, "write", {"part": k}) for k in range(3)]
    side += [(2 * cross.T, "stack", {})]
    for i in range(ns):
        side += [(28 + 4 * i + j, kind, {"src": i}) for j, kind in enumerate(("v_first", "v_left", "v_second", "v_third"))]
    side += [(min(last_step(quad) + LAG8 + 2, n_steps + 1), "divide", {"quad": quad}) for quad in range(n_quads)]
    side += [(n_steps + 2, "heads_turned", {}), (n_steps + 3, "proj", {})]

    with ExitStack() as ctx:
        sb = Mem(nc, ctx, stage)
        A = Core(G, sb, 8 ** -0.5)
        x_sb = [sb(f"x{p}", [P, QT, C]) for p in range(2)]
        xn = sb("xn", [P, QT, C])
        xnT = sb("xnT", [C, TOK])
        ctxT = sb("ctxT", [CC, NKEY])
        qk = sb("qk", [P, W])
        parts = sb("parts", [P, 3, W], BF16)
        k_stack = [sb(f"k_stack{p}", [P, HEADS // 2, W - ns * TOK], BF16) for p in range(2)]
        q_stack = [sb(f"q_stack{p}", [P, HEADS, ns * TOK], BF16) for p in range(2)]
        v_f = [sb(f"v_f{i}", [P, s.T, P]) for i, s in enumerate(sources)]
        v_parts = [[sb(f"v_parts{i}{p}", [P, s.T, HEADS, 3, V8], BF16) for i, s in enumerate(sources)] for p in range(2)]
        junk = sb("junk", [P, 2, TOK]) if with_self else None
        raw = sb("raw", [P, n_quads, 4 * QT, 3 * V8])
        heads = sb("heads", [P, 4 * QT, V8])
        inv = sb("inv1", [P, 4 * QT, 1])
        attn = sb("attn", [P, QT, C])
        more = sb("more", [P, 4 * QT, 8])
        attnT = sb("attnT", [C, TOK])
        L = LnMem(sb, QT)
        names_w = ["wq_c", "wk_c", "wv_c", "bq_c", "bk_c", "b_out", "w_plain", "bv_c"]
        if with_self:
            names_w += ["wq_s", "wk_s", "wv_s", "bq_s", "bk_s", "bv_s"]
        W_sb = {n: sb(n, list(w[n].shape)) for n in names_w}
        wq, wk, wv, bq, bk, bv = ([W_sb[f"{n}_{x}"] for x in "cs"[0:ns]] for n in ("wq", "wk", "wv", "bq", "bk", "bv"))
        out_bank, side_bank, max_bank = G.bank[0], G.bank[1], G.bank[2:4]

        S = Sems(nc, ctx, stage, ["x_in", "ctx_in", "ln_done", "side_ps", "side_done", "part0", "left", "part1", "part2",
                                  "parts_out", "stacked", "max_in0", "max_in1", "v_first", "v_left", "v_second", "v_third",
                                  "rest_dve", "divided", "res", "x_out", "dve_own"] + LN_SEMS + CORE_SEMS)

        def prepare(pool, chain):
            for ks, qs in zip(k_stack, q_stack):
                chain(pool.memset(qs[:, :, :], 0.0))
                chain(pool.memset(ks[32:64, :, :], 0.0))
                chain(pool.memset(ks[96:P, :, :], 1.0))
            for vps in v_parts:
                for vp in vps:
                    chain(pool.memset(vp[:, :, :, 0, 8:9], 1.0))
                    chain(pool.memset(vp[:, :, :, 1:3, 8:9], 0.0))
            for vf in v_f:
                chain(pool.memset(vf[:, :, :], 0.0))
            L.prepare(pool, chain)

        load_weights(nc, ctx, stage, [(W_sb[n][...], w[n]) for n in names_w], prepare)

        s_bias = ctx.enter_context(nc.semaphore(f"{stage}_bias"))
        with nc.Block() as block:
            @block.tensor
            def _(pe):
                for i in range(ns):
                    ins = pe.matmul(side_bank[:, 0:C], bv[i][:, :], W_sb["w_plain"][:, :], start=(i == 0), stop=(i == ns - 1))
                ins.then_inc(s_bias, 1)

            @block.vector
            def _(dve):
                dve.wait_ge(s_bias, 1)
                dve.sem_clear(s_bias)
                dve.tensor_tensor(W_sb["b_out"][:, :], W_sb["b_out"][:, :], side_bank[:, 0:C], ALU.add)

        def q_of(p, g, h, n, c0, m, depth):
            head = 4 * g + h
            return q_stack[p][0:depth, head:head + n, c0:c0 + m]

        def k_of(p, g, h, c0, n, depth):
            return k_stack[p][0:depth, (4 * g + h) // 2, c0 - ns * TOK:c0 - ns * TOK + n]

        def keys_of(s, qt, c):
            c0, n = s.chunks[c]
            return (c0, min(n, (qt + 1) * P)) if s.mask else (c0, n)

        def first_query(s, t):
            return t * P if s.mask else 0

        def last_tile(s, qt):
            return qt if s.mask else s.T - 1

        def by_head(m):
            return m.rearrange("p (h q) -> p h q", q=TOK)

        def rows_in(turn):
            return 16 * (turn // 2 + 1)

        def piece(j):
            return slice(W * j // PIECES, W * (j + 1) // PIECES)

        def quad_of(e):
            return sources.index(e.s) * QUADS + e.g

        def idx(e):
            return sources.index(e.s)


        def seg_sync(sp, plan, n_turns, p, cur, nxt):
            if nxt is not None:
                sp.dma_start(x_sb[1 - p][:, :, :], x_in[nxt].rearrange("(t p) c -> p t c", p=P)).then_inc(S["x_in"], 16)
                sp.dma_start(ctxT[:, :], G.ctxT[nxt]).then_inc(S["ctx_in"], 16)
            for e in plan:
                if e.kind == "write":
                    sp.wait_ge(S[f"part{e.part}"], PIECES)
                    sp.dma_start(parts_dram[e.part], parts[:, e.part, :]).then_inc(S["parts_out"], 16)
                if e.kind == "stack":
                    sp.wait_ge(S["parts_out"], 48)
                    for slot in range(SLOTS):
                        k_src, q_src = (parts_dram[part_of[slot]].rearrange("(h a d) n -> a d h n", a=2, d=8)
                                        for part_of in (K_PART, Q_PART))
                        for a in range(2):
                            r = slice(64 * a + 8 * slot, 64 * a + 8 * slot + 8)
                            sp.dma_start(k_stack[1 - p][r, :, :], k_src[a][:, :, ns * TOK:W]).then_inc(S["stacked"], 16)
                            sp.dma_start(q_stack[1 - p][r, a::2, :], q_src[a][:, :, 0:ns * TOK]).then_inc(S["stacked"], 16)
                if e.kind == "side" and e.job == "turn":
                    sp.wait_ge(S["side_done"], e.n + 1)
                    if e.nxt:
                        sp.wait_ge(S["stacked"], 16 * 4 * SLOTS)
                    c0 = q_col[idx(e)]
                    sp.dma_start(q_stack[1 - p if e.nxt else p][MAXROW:MAXROW + 1, 4 * e.g:4 * e.g + 4, c0:c0 + TOK],
                                 A.negmax_row[0:4, e.q % 2, :]).then_inc(S[f"max_in{e.q % 2}"], 16)
            for k in range(min(n_turns, 2)):
                sp.wait_ge(S[f"max_in{k}"], rows_in(n_turns - 1 - (n_turns - 1 - k) % 2))
            if cur is not None:
                sp.wait_ge(S["res"], 1)
                sp.dma_start(x_out[cur].rearrange("(t p) c -> p t c", p=P), xn[:, :, :]).then_inc(S["x_out"], 16)
                sp.wait_ge(S["x_out"], 16)
            S.next_iteration(sp)

        def seg_pe(pe, plan, p, cur, nxt):
            for e in plan:
                if e.kind == "unit":
                    q = 1 - p if e.nxt else p
                    qt, h, c = e.s.unit(e.k)
                    c0, n = keys_of(e.s, qt, c)
                    if e.k == 0 and e.nxt:
                        pe.wait_ge(S["stacked"], 16 * 4 * SLOTS)
                    if e.u >= 2:
                        pe.wait_ge(S["max_taken"], e.u - 1)
                    pe.matmul(max_bank[e.u % 2][:, 0:n], q_of(q, e.g, h, 1, q_col[idx(e)] + qt * P, P, MAXROW),
                              k_of(q, e.g, h, k_col[idx(e)] + c0, n, MAXROW),
                              start=True, stop=True).then_inc(S["max_scores"], 1)
                if e.kind == "scores":
                    k0, n = e.s.tiles[e.t]
                    if e.i >= 2:
                        pe.wait_ge(S["probs"], e.i - 1)
                    if e.turn is not None:
                        pe.wait_ge(S[f"max_in{e.turn % 2}"], rows_in(e.turn))
                    q0 = first_query(e.s, e.t)
                    for h in (0, 2):
                        out = A.S4[0:n, e.i % 2, h // 2, :].rearrange("p (h q) -> p h q", q=TOK)[:, :, q0:TOK]
                        ins = pe.matmul(out, k_of(p, e.g, h, k_col[idx(e)] + k0, n, MAXROW + 1),
                                        q_of(p, e.g, h, 2, q_col[idx(e)] + q0, TOK - q0, MAXROW + 1), start=True, stop=True)
                    ins.then_inc(S["scores"], 1)
                if e.kind == "pv":
                    n, b = e.s.tiles[e.t][1], e.i % P_BUFS
                    pe.wait_ge(S["rest"], e.i + 1)
                    pe.wait_ge(S["rest_dve"], e.i + 1)
                    if e.t == 0 and quad_of(e) >= 1:
                        pe.wait_ge(S["heads_out"], quad_of(e))
                    for j in range(4 * QT):
                        h, qt = j // QT, j % QT
                        if qt * P < first_query(e.s, e.t):
                            continue
                        out, v = out_bank[:, j * 3 * V8:(j + 1) * 3 * V8], v_parts[p][idx(e)][0:n, e.t, 4 * e.g + h, :, :]
                        at = slice(h * TOK + qt * P, h * TOK + qt * P + P)
                        pe.matmul(out, A.high(A.probs, b, n)[:, at], v, start=(e.t == 0 and j == 0), stop=False,
                                  skip_group_check=True)
                        ins = pe.matmul(out, A.rest[0:n, b, at], v, start=False, stop=(e.t == last_tile(e.s, qt)),
                                        skip_group_check=True)
                    ins.then_inc(S["pv"], 1)
                if e.kind == "side":
                    if e.n >= 1:
                        pe.wait_ge(S["side_done"], e.n)
                    if e.job == "turn":
                        pe.wait_ge(S["max_rows"], e.q + 1)
                        for qt in range(QT):
                            ins = pe.transpose(side_bank[0:4, qt * P:(qt + 1) * P], A.negmax[:, qt, :], A.ident[:, :])
                    if e.job == "k_cross":
                        pe.wait_ge(S["ctx_in"], 16)
                        c0, n = cross.chunks[e.c]
                        ins = pe.matmul(side_bank[:, 0:n], wk[0][:, :], ctxT[:, c0:c0 + n], start=True, stop=True)
                    if e.job == "v_cross":
                        for t in range(4 * e.j, min(4 * e.j + 4, cross.T)):
                            k0, n = cross.tiles[t]
                            ins = pe.matmul(side_bank[0:n, t % 4 * P:(t % 4 + 1) * P], ctxT[:, k0:k0 + n], wv[0][:, :],
                                            start=True, stop=True)
                    if e.job == "x_turned":
                        pe.wait_ge(S["ln_done"], 1)
                        for t in range(QT):
                            ins = pe.transpose(side_bank[:, t * P:(t + 1) * P], xn[:, t, :], A.ident[:, :])
                    if e.job == "q":
                        for i in range(ns):
                            ins = pe.matmul(side_bank[:, q_col[i]:q_col[i] + TOK], wq[i][:, :], xnT[:, :], start=True, stop=True)
                    if e.job == "k_own":
                        ins = pe.matmul(side_bank[:, 0:TOK], wk[1][:, :], xnT[:, :], start=True, stop=True)
                    if e.job == "v_own":
                        for t in range(QT):
                            ins = pe.matmul(side_bank[:, t * P:(t + 1) * P], xnT[:, t * P:(t + 1) * P], wv[1][:, :],
                                            start=True, stop=True)
                    if e.job == "heads_turned":
                        pe.wait_ge(S["divided"], n_quads)
                        for t in range(QT):
                            ins = pe.transpose(side_bank[:, t * P:(t + 1) * P], attn[:, t, :], A.ident[:, :])
                    if e.job == "proj":
                        for t in range(QT):
                            ins = pe.matmul(side_bank[:, t * C:(t + 1) * C], attnT[:, t * P:(t + 1) * P], W_sb["w_plain"][:, :],
                                            start=True, stop=True)
                    ins.then_inc(S["side_ps"], 1)
            S.end_iteration(pe, "pe")

        def seg_act(act, plan, p, cur, nxt):
            for e in plan:
                if e.kind == "scores":
                    n, b = e.s.tiles[e.t][1], e.i % P_BUFS
                    act.wait_ge(S["scores"], e.i + 1)
                    if e.i >= P_BUFS:
                        act.wait_ge(S["pv"], e.i - P_BUFS + 1)
                    q0 = first_query(e.s, e.t)
                    act.activation(by_head(A.probs[0:n, b, :])[:, :, q0:TOK],
                                   A.S4[0:n, e.i % 2, :, :].rearrange("p a (h q) -> p (a h) q", q=TOK)[:, :, q0:TOK],
                                   ACT.Exp, scale=A.scale).then_inc(S["probs"], 1)
                if e.kind == "pv" and e.t == e.s.T - 1:
                    act.wait_ge(S["pv"], e.i + 1)
                    act.activation(raw[:, quad_of(e), :, :].rearrange("p a k -> p (a k)"),
                                   out_bank[:, 0:4 * QT * 3 * V8], ACT.Copy).then_inc(S["heads_out"], 1)
                if e.kind == "side" and e.job not in ("turn", "proj"):
                    act.wait_ge(S["side_ps"], e.n + 1)
                    if e.job == "k_cross":
                        c0, n = cross.chunks[e.c]
                        ins = act.activation(qk[:, k_col[0] + c0:k_col[0] + c0 + n], side_bank[:, 0:n], ACT.Identity,
                                             bias=bk[0][:, 0:1])
                    if e.job == "v_cross":
                        t0, t1 = 4 * e.j, min(4 * e.j + 4, cross.T)
                        n = cross.tiles[t1 - 1][1]
                        ins = act.activation(v_f[0][0:n, t0:t1, :].rearrange("p t n -> p (t n)"),
                                             side_bank[0:n, 0:(t1 - t0) * P], ACT.Copy)
                    if e.job == "x_turned":
                        ins = act.activation(xnT[:, :], side_bank[:, 0:TOK], ACT.Copy)
                    if e.job == "heads_turned":
                        ins = act.activation(attnT[:, :], side_bank[:, 0:TOK], ACT.Copy)
                    if e.job == "q":
                        for i in range(ns):
                            ins = act.activation(qk[:, q_col[i]:q_col[i] + TOK], side_bank[:, q_col[i]:q_col[i] + TOK],
                                                 ACT.Identity, bias=bq[i][:, 0:1])
                    if e.job == "k_own":
                        ins = act.activation(qk[:, k_col[1]:k_col[1] + TOK], side_bank[:, 0:TOK], ACT.Identity, bias=bk[1][:, 0:1])
                    if e.job == "v_own":
                        ins = act.activation(v_f[1][:, :, :].rearrange("p t n -> p (t n)"), side_bank[:, 0:TOK], ACT.Copy)
                    ins.then_inc(S["side_done"], 1)
                    side_seen = e.n + 1
                if e.kind == "part0":
                    if e.j == 0:
                        act.wait_ge(S["side_done"], side_seen)
                    act.activation(parts[:, 0, piece(e.j)], qk[:, piece(e.j)], ACT.Copy).then_inc(S["part0"], 1)
                if e.kind == "part1":
                    act.wait_ge(S["left"], e.j + 1)
                    act.activation(parts[:, 1, piece(e.j)], qk[:, piece(e.j)], ACT.Copy).then_inc(S["part1"], 1)
                if e.kind in ("v_first", "v_second"):
                    part = 0 if e.kind == "v_first" else 1
                    if e.kind == "v_second":
                        act.wait_ge(S["v_left"], e.src + 1)
                    act.activation(v_parts[1 - p][e.src][:, :, :, part, 0:8].rearrange("p t h d -> p (t h) d"),
                                   v_f[e.src][:, :, :].rearrange("p t (h d) -> p (t h) d", d=8),
                                   ACT.Copy).then_inc(S[e.kind], 1)
            S.end_iteration(act, "act")

        def seg_dve(dve, plan, p, cur, nxt):
            chain = Chain(dve, S["dve_own"])
            L.begin(chain)
            for e in plan:
                if e.kind == "unit":
                    qt, h, c = e.s.unit(e.k)
                    n = keys_of(e.s, qt, c)[1]
                    dve.wait_ge(S["max_scores"], e.u + 1)
                    if e.s.mask == "causal":
                        if e.u >= 2:
                            dve.wait_ge(S["max_taken"], e.u - 1)
                        dve.tensor_tensor_reduce(junk[:, e.u % 2, 0:n], max_bank[e.u % 2][:, 0:n], G.past[:, qt, 0:n], 1.0, -3.0e38,
                                                 ALU.add, ALU.max, A.unit_max[:, qt, h, c:c + 1]).then_inc(S["max_taken"], 1)
                    else:
                        dve.tensor_reduce(A.unit_max[:, qt, h, c:c + 1], max_bank[e.u % 2][:, 0:n], AX.X,
                                          ALU.max).then_inc(S["max_taken"], 1)
                    if e.last:
                        dve.wait_ge(S["max_taken"], e.u + 1)
                        dve.tensor_reduce(A.negmax[:, :, :], A.unit_max[:, :, :, 0:len(e.s.chunks)], AX.X, ALU.max,
                                          negate=True).then_inc(S["max_rows"], 1)
                if e.kind == "side" and e.job == "turn":
                    dve.wait_ge(S["side_ps"], e.n + 1)
                    if e.q >= 2:
                        dve.wait_ge(S[f"max_in{e.q % 2}"], rows_in(e.q - 2))
                    dve.tensor_copy(A.negmax_row[0:4, e.q % 2, :], side_bank[0:4, 0:TOK]).then_inc(S["side_done"], 1)
                if e.kind == "rest":
                    s, g, t = steps_of[e.i]
                    n, b = s.tiles[t][1], e.i % P_BUFS
                    dve.wait_ge(S["probs"], e.i + 1)
                    if s.mask:
                        dve.wait_ge(S["masked"], e.i + 1 - cross.T * QUADS)
                        q = slice(first_query(s, t), TOK)
                        out, pr, hi = (by_head(m)[:, POOL_HEADS:4, q] for m in
                                       (A.rest[0:n, b, :], A.probs[0:n, b, :], A.high(A.probs, b, n)))
                    else:
                        out, pr, hi = (m[:, POOL_COLS:4 * TOK] for m in
                                       (A.rest[0:n, b, :], A.probs[0:n, b, :], A.high(A.probs, b, n)))
                    dve.tensor_tensor(out, pr, hi, ALU.subtract).then_inc(S["rest_dve"], 1)
                if e.kind == "ln_stats":
                    dve.wait_ge(S["x_in"], 16)
                    for t in range(QT):
                        ins = dve.bn_stats(L.st[:, t, :], x_sb[1 - p][:, t, :])
                    chain(ins)
                    for t in range(QT):
                        ins = dve.bn_aggr(L.mv[:, t, :], L.st[:, t, :])
                    ins.then_inc(S["ln_var"], 1)
                if e.kind == "ln_apply":
                    dve.wait_ge(S["ln_rstd"], 1)
                    for t in range(QT):
                        ins = ln_apply(dve, L, t, xn[:, t, :], x_sb[1 - p][:, t, :])
                    ins.then_inc(S["ln_done"], 1)
                if e.kind in ("v_left", "v_third"):
                    vf = v_f[e.src][:, :, :].rearrange("p t (h d) -> p (t h) d", d=8)
                    vp = v_parts[1 - p][e.src][:, :, :, :, 0:8].rearrange("p t h k d -> p (t h) k d")
                    if e.kind == "v_left":
                        dve.wait_ge(S["v_first"], e.src + 1)
                        dve.tensor_tensor(vf, vf, vp[:, :, 0, :], ALU.subtract).then_inc(S["v_left"], 1)
                    else:
                        dve.wait_ge(S["v_second"], e.src + 1)
                        dve.tensor_tensor(vp[:, :, 2, :], vf, vp[:, :, 1, :], ALU.subtract).then_inc(S["v_third"], 1)
                if e.kind == "divide":
                    i, g = e.quad // QUADS, e.quad % QUADS
                    dve.wait_ge(S["heads_out"], e.quad + 1)
                    chain(dve.tensor_reduce(heads[:, :, :], raw[:, e.quad, :, :].rearrange("p a (k d) -> p a d k", d=V8),
                                            AX.X, ALU.add))
                    chain(dve.reciprocal(inv[:, :, :], heads[:, :, 8:9]))
                    out = attn[:, :, 32 * g:32 * g + 32].rearrange("p t (h d) -> p h t d", d=8)
                    by = lambda m: m.rearrange("p (h t) d -> p h t d", t=QT)
                    to = out if i == 0 else by(more[:, :, :])
                    ins = dve.tensor_tensor(to, by(heads[:, :, 0:8]), by(inv[:, :, 0:1].to_broadcast([P, 4 * QT, 8])), ALU.mult)
                    if i:
                        chain(ins)
                        ins = dve.tensor_tensor(out, out, by(more[:, :, :]), ALU.add)
                    ins.then_inc(S["divided"], 1)
                    dve.wait_ge(S["divided"], e.quad + 1)
                if e.kind == "side" and e.job == "proj":
                    for t in range(QT):
                        ins = dve.tensor_tensor(x_sb[p][:, t, :], x_sb[p][:, t, :], W_sb["b_out"][:, :], ALU.add)
                    chain(ins)
                    dve.wait_ge(S["side_ps"], e.n + 1)
                    dve.tensor_tensor(xn[:, :, :].rearrange("p t c -> p (t c)"), side_bank[:, 0:TOK],
                                      x_sb[p][:, :, :].rearrange("p t c -> p (t c)"), ALU.add).then_inc(S["res"], 1)
            S.end_iteration(dve, "dve")

        def seg_pool(pool, plan, p, cur, nxt):
            for e in plan:
                if e.kind == "scores":
                    s, b, i = e.s, e.i % P_BUFS, e.i
                    k0, n = s.tiles[e.t]
                    pool.wait_ge(S["probs"], i + 1)
                    out, pr, hi = A.rest[0:n, b, :], A.probs[0:n, b, :], A.high(A.probs, b, n)
                    if s.mask:
                        q0 = first_query(s, e.t)
                        some = by_head(pr)[:, :, q0:q0 + P]
                        pool.affine_select(out=some, in_=some, pattern=[[0, 4], [1, P]], compare_op=ALU.is_ge, fill=0.0,
                                           base=q0 - k0, channel_multiplier=-1).then_inc(S["masked"], 1)
                        pool.wait_ge(S["masked"], i + 1 - cross.T * QUADS)
                        out, pr, hi = (by_head(m)[:, 0:POOL_HEADS, q0:TOK] for m in (out, pr, hi))
                    else:
                        out, pr, hi = (m[:, 0:POOL_COLS] for m in (out, pr, hi))
                    pool.tensor_tensor(out, pr, hi, ALU.subtract).then_inc(S["rest"], 1)
                    pool.wait_ge(S["rest"], i + 1)
                if e.kind == "ln_rstd":
                    ln_rstd(pool, S, L, 0, QT)
                    pool.wait_ge(S["ln_rstd"], 1)
                if e.kind == "left":
                    pool.wait_ge(S["part0"], e.j + 1)
                    c = piece(e.j)
                    pool.tensor_tensor(qk[:, c], qk[:, c], parts[:, 0, c], ALU.subtract).then_inc(S["left"], 1)
                    pool.wait_ge(S["left"], e.j + 1)
                if e.kind == "part2":
                    pool.wait_ge(S["part1"], e.j + 1)
                    c = piece(e.j)
                    pool.tensor_tensor(parts[:, 2, c], qk[:, c], parts[:, 1, c], ALU.subtract).then_inc(S["part2"], 1)
                    pool.wait_ge(S["part2"], e.j + 1)
            S.end_iteration(pool, "pool")

        steps_of = [(s, g, t) for s in sources for g in range(QUADS) for t in range(s.T)]
        first, first_turns = schedule8(sources, side, False, True)
        middle, middle_turns = schedule8(sources, side, True, True)
        last, last_turns = schedule8(sources, side, True, False)

        def batches(eng, seg, turns=False):
            def run(plan, n, p, cur, nxt):
                if turns:
                    seg(eng, plan, n, p, cur, nxt)
                else:
                    seg(eng, plan, p, cur, nxt)
            run(first, first_turns, 1, None, 0)
            with eng.Fori(0, BATCH // 2 - 1) as i:
                run(middle, middle_turns, 0, i * 2, i * 2 + 1)
                run(middle, middle_turns, 1, i * 2 + 1, i * 2 + 2)
            run(middle, middle_turns, 0, BATCH - 2, BATCH - 1)
            run(last, last_turns, 1, BATCH - 1, None)

        with nc.Block() as block:
            @block.sync
            def _(sp):
                batches(sp, seg_sync, True)

            @block.tensor
            def _(pe):
                batches(pe, seg_pe)

            @block.scalar
            def _(act):
                batches(act, seg_act)

            @block.vector
            def _(dve):
                batches(dve, seg_dve)

            @block.gpsimd
            def _(pool):
                batches(pool, seg_pool)



D32 = 32
V_COLS = 3 * D32 + 1


def attention32(nc, G, stage, x_in, x1_out, x_out, w, own_keys):
    nk, cy = (TOK, C) if own_keys else (NKEY, CC)
    s, = make_sources([(nk, "after" if own_keys else None)])
    with ExitStack() as ctx:
        sb = Mem(nc, ctx, stage)
        A = Core(G, sb, D32 ** -0.5)
        A.rows = V_COLS
        A.heads, A.inv = sb("heads", [V_COLS, HEADS, TOK]), sb("inv", [V_COLS, 2, 2 * TOK])
        A.quads, A.spread = QUADS, G.spread32
        x_sb = sb("x", [P, QT, C])
        x1 = sb("x1", [P, QT, C]) if own_keys else x_sb
        xn = sb("xn", [P, QT, C])
        xqT = sb("xqT", [C, TOK])
        yT = sb("yT", [cy, nk])
        q_f, q_b = sb("q_f", [P, QUADS, 4, TOK]), sb("q_b", [P, QUADS, 4, TOK], BF16)
        k_f, k_b = sb("k_f", [P, QUADS, nk]), sb("k_b", [P, QUADS, nk], BF16)
        v_left = sb("v_left", [P, 2, HEADS * D32])
        v_parts = sb("v_parts", [P, s.T, HEADS, V_COLS], BF16)
        row_of = sb("row_of", [P, 4, P], BF16)
        names_w = ["wq", "wk", "wv", "w_out", "b_out", "lnx_g", "lnx_b", "lny_g", "lny_b"] + ["ln1_g", "ln1_b"] * own_keys
        W_sb = {n: sb(n, list(w[n].shape)) for n in names_w}
        row_of_f = sb("row_of_f", [P, 4, P])
        A.negmax_row = sb("negmax_rows", [P, 2, TOK], BF16)
        if own_keys:
            A.kept = sb("kept", [P, P_BUFS, 4 * TOK])
            A.kept_rest = sb("kept_rest", [P, P_BUFS, 4 * TOK], BF16)
            ones_col = sb("ones_col", [P, V_COLS], BF16)
            L = LnMem(sb, QT)
        else:
            ctx_sb = sb("ctx", [P, s.T, CC])
            L = LnMem(sb, s.T)

        S = Sems(nc, ctx, stage, ["x_in", "ctx_in", "x1", "x1_out", "xn", "yn", "ring_ps", "ring", "v_ps", "v_left",
                                  "v_mid", "v_parts", "qk_b", "res", "x_out", "dve_own"] + LN_SEMS + CORE_SEMS)

        def prepare(pool, chain):
            chain(pool.memset(v_parts[:, :, :, 3 * D32:V_COLS], 0.0 if own_keys else 1.0))
            if own_keys:
                chain(pool.memset(ones_col[:, 0:3 * D32], 0.0))
                chain(pool.memset(ones_col[:, 3 * D32:V_COLS], 1.0))
            else:
                chain(pool.memset(ctx_sb[:, :, :], 0.0))
            chain(pool.memset(A.negmax_row[:, :, :], 0.0))
            chain(pool.memset(q_f[:, :, :, :], 0.0))
            L.prepare(pool, chain)

        load_weights(nc, ctx, stage, [(W_sb[n][...], w[n]) for n in names_w] + [(row_of_f[:, :, :], G.row_of)], prepare)
        with nc.Block() as block:
            @block.vector
            def _(dve):
                dve.tensor_copy(row_of[:, :, :], row_of_f[:, :, :])

        A.w_out = lambda k: W_sb["w_out"][:, k, :]
        A.q_max = lambda s, g, h, qt: q_b[:, g, h, qt * P:(qt + 1) * P]
        A.k_max = lambda s, g, h, c0, n: k_b[:, g, c0:c0 + n]
        A.wait_max = lambda pe, quad: pe.wait_ge(S["max_ready"], quad + 1)

        def scores(pe, out, s, g, h, k0, n):
            pe.matmul(out, k_f[:, g, k0:k0 + n], q_f[:, g, h, :], start=True, stop=False)
            return pe.matmul(out, row_of[:, h, 0:n], A.negmax_row[:, g % 2, :], start=False, stop=True)

        def wait_out(pe, quad):
            if quad >= 1:
                pe.wait_ge(S["heads_out"], quad)

        def pv(pe, s, g, t, b):
            n = s.tiles[t][1]
            for h in range(4):
                out = A.bank[h % 2][0:V_COLS, h // 2 * TOK:(h // 2 + 1) * TOK]
                v, last = v_parts[0:n, t, 4 * g + h, :], t == s.T - 1
                opens = t == 0 and h // 2 == 0
                if own_keys:
                    pe.matmul(out, ones_col[0:n, :], A.high(A.probs, b, n)[:, A.place(h)], start=opens, stop=False,
                              skip_group_check=True)
                    pe.matmul(out, ones_col[0:n, :], A.rest[0:n, b, A.place(h)], start=False, stop=False,
                              skip_group_check=True)
                    high, rest, opens = A.high(A.kept, b, n), A.kept_rest, False
                else:
                    high, rest = A.high(A.probs, b, n), A.rest
                pe.matmul(out, v, high[:, A.place(h)], start=opens, stop=False, skip_group_check=True)
                ins = pe.matmul(out, v, rest[0:n, b, A.place(h)], start=False, stop=last, skip_group_check=True)
            return ins

        def take_out(act, quad):
            for a in range(2):
                ins = act.activation(A.heads[:, 4 * quad + a:4 * quad + 4:2, :],
                                     A.bank[a][0:V_COLS, :].rearrange("p (h q) -> p h q", h=2), ACT.Copy)
            return ins

        A.scores, A.wait_out, A.pv, A.take_out = scores, wait_out, pv, take_out

        ring = []
        if not own_keys:
            ring += [("ctx", t, min(t + 4, s.T)) for t in range(0, s.T, 4)]
        ring += [("x", 0, 0)] + [("q", g, 0) for g in range(QUADS)]
        ring += [("k", g, c) for g in range(QUADS) for c in range(len(s.chunks))]
        after_x = ring.index(("x", 0, 0)) + 1
        ring_bank = [A.S4[:, a, c, :] for a in range(2) for c in range(2)]

        with nc.Block() as block:
            @block.sync
            def _(sp):
                with sp.Fori(0, BATCH) as b:
                    sp.dma_start(x_sb[:, :, :], x_in[b].rearrange("(t p) c -> p t c", p=P)).then_inc(S["x_in"], 16)
                    if own_keys:
                        sp.wait_ge(S["x1"], 1)
                        sp.dma_start(x1_out[b].rearrange("(t p) c -> p t c", p=P), x1[:, :, :]).then_inc(S["x1_out"], 16)
                        sp.wait_ge(S["x1_out"], 16)
                    else:
                        full = nk // P * P
                        sp.dma_start(ctx_sb[:, 0:nk // P, :],
                                     G.ctx[b, 0:full].rearrange("(t p) c -> p t c", p=P)).then_inc(S["ctx_in"], 16)
                        sp.dma_start(ctx_sb[0:nk - full, nk // P, :], G.ctx[b, full:nk]).then_inc(S["ctx_in"], 16)
                    sp.wait_ge(S["res"], 1)
                    sp.dma_start(x_out[b].rearrange("(t p) c -> p t c", p=P), xn[:, :, :]).then_inc(S["x_out"], 16)
                    sp.wait_ge(S["x_out"], 16)
                    S.next_iteration(sp)

            @block.tensor
            def _(pe):
                with pe.Fori(0, BATCH) as b:
                    if not own_keys:
                        pe.wait_ge(S["yn"], 1)
                    for i, (what, g, c) in enumerate(ring):
                        bank = ring_bank[i % 4]
                        if i >= 4:
                            pe.wait_ge(S["ring"], i - 3)
                        if i == after_x:
                            pe.wait_ge(S["ring"], after_x)
                        if what == "ctx":
                            for t in range(g, c):
                                k0, n = s.tiles[t]
                                ins = pe.transpose(bank[0:CC, (t - g) * P:(t - g) * P + n], ctx_sb[0:n, t, :],
                                                   A.ident[0:n, 0:n])
                        if what == "x":
                            pe.wait_ge(S["xn"], 1)
                            for t in range(QT):
                                ins = pe.transpose(bank[:, t * P:(t + 1) * P], xn[:, t, :], A.ident[:, :])
                        if what == "q":
                            ins = pe.matmul(bank[:, 0:TOK], W_sb["wq"][:, g * P:(g + 1) * P], xqT[:, :], start=True, stop=True)
                        if what == "k":
                            c0, n = s.chunks[c]
                            ins = pe.matmul(bank[:, 0:n], W_sb["wk"][:, g * P:(g + 1) * P], yT[:, c0:c0 + n],
                                            start=True, stop=True)
                        ins.then_inc(S["ring_ps"], 1)
                    for t, (k0, n) in enumerate(s.tiles):
                        if t >= 4:
                            pe.wait_ge(S["v_left"], t - 3)
                        pe.matmul(A.bank[t % 4][0:n, :], yT[:, k0:k0 + n], W_sb["wv"][:, :],
                                  start=True, stop=True).then_inc(S["v_ps"], 1)
                    pe.wait_ge(S["ring"], len(ring))
                    pe.wait_ge(S["qk_b"], 2)
                    pe.wait_ge(S["v_parts"], s.T)
                    core_pe(pe, S, A, s)
                    tail_pe(pe, S, A, HEADS // 2)
                    S.end_iteration(pe, "pe")

            @block.scalar
            def _(act):
                with act.Fori(0, BATCH) as b:
                    for i, (what, g, c) in enumerate(ring):
                        bank = ring_bank[i % 4]
                        act.wait_ge(S["ring_ps"], i + 1)
                        if what == "ctx":
                            k0 = g * P
                            n = s.tiles[c - 1][0] + s.tiles[c - 1][1] - k0
                            ins = act.activation(yT[:, k0:k0 + n], bank[0:CC, 0:n], ACT.Identity,
                                                 bias=W_sb["lny_b"][:, 0:1], scale=W_sb["lny_g"][:, 0:1])
                        if what == "x":
                            if own_keys:
                                act.activation(yT[:, :], bank[:, 0:TOK], ACT.Identity, bias=W_sb["lny_b"][:, 0:1],
                                               scale=W_sb["lny_g"][:, 0:1])
                            ins = act.activation(xqT[:, :], bank[:, 0:TOK], ACT.Identity, bias=W_sb["lnx_b"][:, 0:1],
                                                 scale=W_sb["lnx_g"][:, 0:1])
                        if what == "q":
                            for h in range(4):
                                r = slice(D32 * h, D32 * h + D32)
                                ins = act.activation(q_f[r, g, h, :], bank[r, 0:TOK], ACT.Copy)
                        if what == "k":
                            c0, n = s.chunks[c]
                            ins = act.activation(k_f[:, g, c0:c0 + n], bank[:, 0:n], ACT.Copy)
                        ins.then_inc(S["ring"], 1)
                    core_act(act, S, A, s)
                    S.end_iteration(act, "act")

            @block.vector
            def _(dve):
                with dve.Fori(0, BATCH) as b:
                    chain = Chain(dve, S["dve_own"])
                    L.begin(chain)
                    if not own_keys:
                        dve.wait_ge(S["ctx_in"], 32)
                        ctx_tiles = [ctx_sb[0:n, t, :] for t, (_, n) in enumerate(s.tiles)]
                        ln_stats(dve, S, L, ctx_tiles)
                        for t, tile in enumerate(ctx_tiles):
                            ins = ln_apply(dve, L, t, tile, tile)
                        ins.then_inc(S["yn"], 1)
                    dve.wait_ge(S["x_in"], 16)
                    tiles = lambda m: [m[:, t, :] for t in range(QT)]
                    if own_keys:
                        ln_stats(dve, S, L, tiles(x_sb))
                        for t in range(QT):
                            ins = ln_apply(dve, L, t, x_sb[:, t, :], x_sb[:, t, :])
                        chain(ins)
                        ln_stats(dve, S, L, tiles(x_sb))
                        for t in range(QT):
                            ins = ln_apply(dve, L, t, x1[:, t, :], x_sb[:, t, :])
                        chain(ins)
                        for t in range(QT):
                            ins = dve.tensor_tensor(x1[:, t, :], x1[:, t, :], W_sb["ln1_g"][:, :], ALU.mult)
                        chain(ins)
                        for t in range(QT):
                            ins = dve.tensor_tensor(x1[:, t, :], x1[:, t, :], W_sb["ln1_b"][:, :], ALU.add)
                        ins.then_inc(S["x1"], 1)
                        dve.wait_ge(S["x1"], 1)
                    ln_stats(dve, S, L, tiles(x1))
                    for t in range(QT):
                        ins = ln_apply(dve, L, t, xn[:, t, :], x1[:, t, :])
                    ins.then_inc(S["xn"], 1)
                    for t, (_, n) in enumerate(s.tiles):
                        dve.wait_ge(S["v_ps"], t + 1)
                        if t >= 2:
                            dve.wait_ge(S["v_parts"], t - 1)
                        first = v_parts[0:n, t, :, 0:D32]
                        v = A.bank[t % 4][0:n, :].rearrange("p (h d) -> p h d", d=D32)
                        chain(dve.tensor_copy(first, v))
                        dve.tensor_tensor(v_left[0:n, t % 2, :].rearrange("p (h d) -> p h d", d=D32), v, first,
                                          ALU.subtract).then_inc(S["v_left"], 1)
                    dve.wait_ge(S["ring"], len(ring))
                    dve.tensor_copy(q_b[:, :, :, :], q_f[:, :, :, :]).then_inc(S["qk_b"], 1)
                    dve.tensor_copy(k_b[:, :, :], k_f[:, :, :]).then_inc(S["qk_b"], 1)
                    core_dve(dve, S, A, s, chain)
                    for t in range(QT):
                        ins = dve.tensor_tensor(x_sb[:, t, :], x1[:, t, :], W_sb["b_out"][:, :], ALU.add)
                    chain(ins)
                    tail_dve(dve, S, A, HEADS // 2)
                    dve.tensor_tensor(xn[:, :, :].rearrange("p t c -> p (t c)"), A.bank[3][:, 0:TOK],
                                      x_sb[:, :, :].rearrange("p t c -> p (t c)"), ALU.add).then_inc(S["res"], 1)
                    S.end_iteration(dve, "dve")

            @block.gpsimd
            def _(pool):
                with pool.Fori(0, BATCH) as b:
                    if own_keys:
                        for k in range(3):
                            ln_rstd(pool, S, L, k, QT)
                    else:
                        ln_rstd(pool, S, L, 0, s.T)
                        ln_rstd(pool, S, L, 1, QT)
                    for t, (_, n) in enumerate(s.tiles):
                        pool.wait_ge(S["v_left"], t + 1)
                        left = v_left[0:n, t % 2, :].rearrange("p (h d) -> p h d", d=D32)
                        second = v_parts[0:n, t, :, D32:2 * D32]
                        pool.tensor_copy(second, left).then_inc(S["v_mid"], 1)
                        pool.wait_ge(S["v_mid"], t + 1)
                        pool.tensor_tensor(v_parts[0:n, t, :, 2 * D32:3 * D32], left, second,
                                           ALU.subtract).then_inc(S["v_parts"], 1)
                        pool.wait_ge(S["v_parts"], t + 1)
                    core_pool(pool, S, A, s)
                    S.end_iteration(pool, "pool")



K_PASS = ((0, 0, 0), (1, 1, 2))
Q_PASS = ((0, 1, 2), (0, 1, 0))
ROWS32 = 3 * D32
V32 = D32 + 1
POOL_COLS32 = 640
P_BUFS32, LAG32 = 6, 4
LN_PIECES = 5
RING32 = ("unit", "turn", "q", "k", "v", "ctx", "x_turned", "heads", "proj")


def schedule32(s, with_core, with_next):
    T, n_chunks = s.T, len(s.chunks)
    steps = [(g, t) for g in range(QUADS) for t in range(T)] if with_core else []
    end = len(steps)
    at = {}

    def put(n, kind, **k):
        at.setdefault(n, []).append(Ev(kind, s=s, **k))

    prep = []
    if with_core:
        prep = [(1, 0, 4, T - 2), (2, T - 5, T - 2, 2 * T - 2), (3, 2 * T - 5, 2 * T - 2, 3 * T - 2)]
    if with_next:
        first = 3 * T - 2 if with_core else 17
        prep.append((4, first, first + 4, 4 * T - 2 if with_core else first + 5))
        for j in range(LN_PIECES):
            put(first - 17 + j, "ln_stats", j=j)
            put(first - 9 + j, "ln_apply", j=j)
        put(first - 11, "ln_rstd")
        for j in range((T + 3) // 4):
            put(first - 3 + j // 2, "ctx", j=j)
        put(first - 1, "x_turned")
    for r, (quad, start, w0, w1) in enumerate(prep):
        v = start + (4, 8, 8, 6)[quad - 1]
        put(w1, "turn", quad=quad, r=r)
        put(start, "q", quad=quad, r=r)
        for c in range(n_chunks):
            put(start + c, "k", quad=quad, r=r, c=c)
        for k in range(s.NU):
            put(w0 + k * (w1 - w0) // s.NU, "unit", quad=quad, r=r, k=k)
        put(start + 1, "q_max", quad=quad, r=r)
        put(start + 4, "write", quad=quad, r=r, part=0)
        for j in range(PIECES):
            put(start + 4 + j, "part1", quad=quad, r=r, j=j)
            put(start + 5 + j, "part2", quad=quad, r=r, j=j)
        put(start + 7, "write", quad=quad, r=r, part=1)
        put(start + 8, "write", quad=quad, r=r, part=2)
        put(start + 8, "stack", quad=quad, r=r)
        for j in range((T + 3) // 4):
            put(v + j, "v", quad=quad, r=r, j=j)
        for j in range(PIECES):
            put(v + 4 + j, "v_second", quad=quad, r=r, j=j)
            put(v + 5 + j, "v_third", quad=quad, r=r, j=j)
    for quad in range(QUADS if with_core else 0):
        done = T * (quad + 1) - 1 + LAG32 + 1
        at.setdefault(min(done, end), []).insert(0, Ev("take", s=s, quad=quad))
        put(min(done, end) + 1, "heads", quad=quad)
    if with_core:
        put(end + 2, "proj")

    plan = []
    for n in range(max(list(at) + [end]) + 1):
        now = at.get(n, [])
        if n < end:
            now.insert(2, Ev("scores", s=s, g=steps[n][0], t=steps[n][1], i=n))
        if n == end and with_core:
            plan.append(Ev("rest", s=s, t=steps[-1][1], i=end - 1))
            for i in range(end - LAG32, end):
                plan.append(Ev("pv", s=s, g=steps[i][0], t=steps[i][1], i=i))
        plan += now
        if 1 <= n < end:
            plan.append(Ev("rest", s=s, t=steps[n - 1][1], i=n - 1))
        if LAG32 <= n < end:
            i = n - LAG32
            plan.append(Ev("pv", s=s, g=steps[i][0], t=steps[i][1], i=i))
    u = k = f = 0
    for e in plan:
        if e.kind in RING32:
            e.n = k
            k += 1
        if e.kind in ("q", "k", "v"):
            e.f = f
            f += 1
        if e.kind == "unit":
            e.u = u
            u += 1
    return plan, len(prep)


def cross32(nc, G, stage, x_in, x_out, w):
    s, = make_sources([(NKEY, None)])
    T = s.T
    W = TOK + NKEY
    NG = 4 * QT
    tiles_y = T + QT
    ln_piece = [range(tiles_y * j // LN_PIECES, tiles_y * (j + 1) // LN_PIECES) for j in range(LN_PIECES)]
    parts_dram = nc.dram_tensor(f"{stage}_parts_dram", [3, P, W], BF16, kind="Internal").ap()
    STACKED = 16 * 2 * 2 * 3
    with ExitStack() as ctx:
        sb = Mem(nc, ctx, stage)
        A = Core(G, sb, D32 ** -0.5, P_BUFS32)
        x_sb, x_res = sb("x", [P, QT, C]), sb("x_res", [P, QT, C])
        res = sb("res", [P, QT, C])
        ctx_sb = sb("ctx", [P, T, CC])
        yT, xqT = sb("yT", [CC, NKEY]), sb("xqT", [C, TOK])
        first = [sb(f"first{p}", [P, W], BF16) for p in range(2)]
        q_max = [sb(f"q_max{p}", [P, 4, TOK], BF16) for p in range(2)]
        k_stack = [[sb(f"k_stack{p}{m}", [P, 4, NKEY], BF16) for m in range(2)] for p in range(2)]
        q_stack = [[sb(f"q_stack{p}{m}", [P, 4, TOK], BF16) for m in range(2)] for p in range(2)]
        v_parts = [sb(f"v_parts{p}", [P, T, 4, 3, V32], BF16) for p in range(2)]
        others = sb("others", [P, 2, W], BF16)
        left = sb("left", [P, W])
        v_left = sb("v_left", [P, T, 4 * D32])
        sums = sb("sums", [P, NG, V32])
        inv = sb("inv", [P, NG, 1])
        attn = sb("attn", [P, QT, 4 * D32])
        attnT = sb("attnT", [P, QUADS, TOK])
        L = LnMem(sb, tiles_y)
        names_w = ["wq", "wk", "wv", "w_out", "b_out", "lnx_g", "lnx_b", "lny_g", "lny_b"]
        W_sb = {n: sb(n, list(w[n].shape)) for n in names_w}
        out_bank, ring_bank = G.bank[0:2], G.bank[2:4]

        S = Sems(nc, ctx, stage, ["x_in", "ctx_in", "x_res_in", "ln_done", "ln_stats", "ring_ps", "ring_done0", "ring_done1", "first",
                                  "q_max", "max_rows", "turned", "max_in0", "max_in1", "part1", "part2", "parts_out", "stacked",
                                  "v_second", "v_third", "scores", "probs", "rest", "rest_dve", "pv", "taken", "heads_ok",
                                  "heads_in", "res", "x_out", "dve_own"] + LN_SEMS)

        def prepare(pool, chain):
            for p in range(2):
                for m in range(2):
                    chain(pool.memset(k_stack[p][m][96:P, :, :], 1.0))
                    chain(pool.memset(q_stack[p][m][96:P, :, :], 0.0))
                chain(pool.memset(q_max[p][:, :, :], 0.0))
                chain(pool.memset(v_parts[p][:, :, :, 0, D32:V32], 1.0))
                chain(pool.memset(v_parts[p][:, :, :, 1:3, D32:V32], 0.0))
            chain(pool.memset(v_left[:, :, :], 0.0))
            chain(pool.memset(ctx_sb[:, :, :], 0.0))
            L.prepare(pool, chain)

        load_weights(nc, ctx, stage, [(W_sb[n][...], w[n]) for n in names_w], prepare)

        def ring_free(eng, e):
            if e.n >= 2:
                eng.wait_ge(S[f"ring_done{e.n % 2}"], e.n // 2)

        def ring_done(e):
            return S[f"ring_done{e.n % 2}"]

        def rows_in(turn):
            return 16 * (turn // 2 + 1)

        def piece(j):
            return slice(W * j // PIECES, W * (j + 1) // PIECES)

        def v_tiles(j):
            t0, t1 = 4 * j, min(4 * j + 4, T)
            return t0, t1, s.tiles[t1 - 1][1]

        def columns(e):
            c0, n = (0, TOK) if e.kind == "q" else (TOK + s.chunks[e.c][0], s.chunks[e.c][1])
            return slice(c0, c0 + n), n

        def ln_tile(t):
            return ctx_sb[0:s.tiles[t][1], t, :] if t < T else x_sb[:, t - T, :]

        def group(j):
            return out_bank[j // 4][:, j % 4 * 3 * V32:(j % 4 + 1) * 3 * V32]

        def seg_sync(sp, plan, n_prep, cur, nxt):
            if cur is not None:
                sp.dma_start(x_res[:, :, :], x_in[cur].rearrange("(t p) c -> p t c", p=P)).then_inc(S["x_res_in"], 16)
            if nxt is not None:
                full = NKEY // P * P
                sp.dma_start(x_sb[:, :, :], x_in[nxt].rearrange("(t p) c -> p t c", p=P)).then_inc(S["x_in"], 16)
                sp.dma_start(ctx_sb[:, 0:NKEY // P, :],
                             G.ctx[nxt, 0:full].rearrange("(t p) c -> p t c", p=P)).then_inc(S["ctx_in"], 16)
                sp.dma_start(ctx_sb[0:NKEY - full, NKEY // P, :], G.ctx[nxt, full:NKEY]).then_inc(S["ctx_in"], 16)
            for e in plan:
                p = e.quad % 2
                if e.kind == "write":
                    if e.part == 0 and e.r:
                        sp.wait_ge(S["stacked"], STACKED * e.r)
                    if e.part == 0:
                        sp.wait_ge(S["first"], first_of[e.r])
                    if e.part == 1:
                        sp.wait_ge(S["part1"], PIECES * (e.r + 1))
                    if e.part == 2:
                        sp.wait_ge(S["part2"], PIECES * (e.r + 1))
                    sp.dma_start(parts_dram[e.part], first[p][:, :] if e.part == 0 else others[:, e.part - 1, :]
                                 ).then_inc(S["parts_out"], 16)
                if e.kind == "stack":
                    sp.wait_ge(S["parts_out"], 48 * (e.r + 1))
                    if e.quad >= 2 and cur is not None:
                        sp.wait_ge(S["scores"], T * (e.quad - 1))
                    for m in range(2):
                        for slot in range(3):
                            r = slice(D32 * slot, D32 * slot + D32)
                            k_src, q_src = (parts_dram[part[m][slot]].rearrange("(h d) n -> d h n", d=D32)
                                            for part in (K_PASS, Q_PASS))
                            sp.dma_start(k_stack[p][m][r, :, :], k_src[:, :, TOK:W]).then_inc(S["stacked"], 16)
                            sp.dma_start(q_stack[p][m][r, :, :], q_src[:, :, 0:TOK]).then_inc(S["stacked"], 16)
                if e.kind == "turn":
                    sp.wait_ge(S["turned"], e.r + 1)
                    sp.dma_start(q_stack[p][1][ROWS32:ROWS32 + 1, :, :],
                                 A.negmax_row[0:4, e.r % 2, :]).then_inc(S[f"max_in{e.r % 2}"], 16)
            sp.wait_ge(S["stacked"], STACKED * n_prep)
            for k in range(min(n_prep, 2)):
                sp.wait_ge(S[f"max_in{k}"], rows_in(n_prep - 1 - (n_prep - 1 - k) % 2))
            if cur is not None:
                sp.wait_ge(S["res"], 1)
                sp.dma_start(x_out[cur].rearrange("(t p) c -> p t c", p=P), res[:, :, :]).then_inc(S["x_out"], 16)
                sp.wait_ge(S["x_out"], 16)
            S.next_iteration(sp)

        def seg_pe(pe, plan, cur):
            for e in plan:
                p = e.quad % 2
                if e.kind in RING32:
                    ring_free(pe, e)
                    bank = ring_bank[e.n % 2]
                if e.kind == "unit":
                    qt, h, c = s.unit(e.k)
                    c0, n = s.chunks[c]
                    if e.k == 0:
                        pe.wait_ge(S["first"], first_of[e.r])
                        pe.wait_ge(S["q_max"], e.r + 1)
                    ins = pe.matmul(bank[:, 0:n], q_max[p][:, h, qt * P:(qt + 1) * P],
                                    first[p][:, TOK + c0:TOK + c0 + n], start=True, stop=True)
                if e.kind == "turn":
                    pe.wait_ge(S["max_rows"], e.r + 1)
                    for qt in range(QT):
                        ins = pe.transpose(bank[0:4, qt * P:(qt + 1) * P], A.negmax[:, qt, :], A.ident[:, :])
                if e.kind == "ctx":
                    if e.j == 0:
                        pe.wait_ge(S["ln_done"], LN_PIECES)
                    t0, t1, _ = v_tiles(e.j)
                    for t in range(t0, t1):
                        n = s.tiles[t][1]
                        ins = pe.transpose(bank[0:CC, (t - t0) * P:(t - t0) * P + n], ctx_sb[0:n, t, :], A.ident[0:n, 0:n])
                if e.kind == "x_turned":
                    for t in range(QT):
                        ins = pe.transpose(bank[:, t * P:(t + 1) * P], x_sb[:, t, :], A.ident[:, :])
                if e.kind in ("q", "k", "v"):
                    if e.quad == 4 and e.kind == "q":
                        for k in range(2):
                            pe.wait_ge(S[f"ring_done{k}"], (e.n + 1 - k) // 2)
                    cols = slice(e.quad % QUADS * P, (e.quad % QUADS + 1) * P)
                    if e.kind == "q":
                        ins = pe.matmul(bank[:, 0:TOK], W_sb["wq"][:, cols], xqT[:, :], start=True, stop=True)
                    if e.kind == "k":
                        c0, n = s.chunks[e.c]
                        ins = pe.matmul(bank[:, 0:n], W_sb["wk"][:, cols], yT[:, c0:c0 + n], start=True, stop=True)
                    if e.kind == "v":
                        t0, t1, _ = v_tiles(e.j)
                        for t in range(t0, t1):
                            k0, n = s.tiles[t]
                            ins = pe.matmul(bank[0:n, (t - t0) * P:(t - t0 + 1) * P], yT[:, k0:k0 + n], W_sb["wv"][:, cols],
                                            start=True, stop=True)
                if e.kind == "heads":
                    pe.wait_ge(S["heads_ok"], e.quad + 1)
                    for t in range(QT):
                        ins = pe.transpose(bank[:, t * P:(t + 1) * P], attn[:, t, :], A.ident[:, :])
                if e.kind == "proj":
                    pe.wait_ge(S["heads_in"], QUADS)
                    for t in range(QT):
                        for k in range(QUADS):
                            ins = pe.matmul(bank[:, t * C:(t + 1) * C], attnT[:, k, t * P:(t + 1) * P], W_sb["w_out"][:, k, :],
                                            start=(k == 0), stop=(k == QUADS - 1))
                if e.kind in RING32:
                    ins.then_inc(S["ring_ps"], 1)
                if e.kind == "scores":
                    k0, n = s.tiles[e.t]
                    p = e.g % 2
                    if e.i >= 2:
                        pe.wait_ge(S["probs"], e.i - 1)
                    if e.t == 0 and e.g:
                        pe.wait_ge(S["stacked"], STACKED * e.g)
                        pe.wait_ge(S[f"max_in{(e.g - 1) % 2}"], rows_in(e.g - 1))
                    for h in range(4):
                        out = A.S4[0:n, e.i % 2, h // 2, h % 2 * TOK:(h % 2 + 1) * TOK]
                        for m in range(2):
                            ins = pe.matmul(out, k_stack[p][m][:, h, k0:k0 + n], q_stack[p][m][:, h, :],
                                            start=(m == 0), stop=(m == 1))
                    ins.then_inc(S["scores"], 1)
                if e.kind == "pv":
                    n, b, p = s.tiles[e.t][1], e.i % P_BUFS32, e.g % 2
                    pe.wait_ge(S["rest"], e.i + 1)
                    pe.wait_ge(S["rest_dve"], e.i + 1)
                    if e.t == 0 and e.g:
                        pe.wait_ge(S["v_third"], PIECES * e.g)
                        pe.wait_ge(S["taken"], e.g)
                    for j in range(NG):
                        h, qt = j // QT, j % QT
                        at, v = slice(h * TOK + qt * P, h * TOK + qt * P + P), v_parts[p][0:n, e.t, h, :, :]
                        pe.matmul(group(j), A.high(A.probs, b, n)[:, at], v, start=(e.t == 0 and j % 4 == 0), stop=False,
                                  skip_group_check=True)
                        ins = pe.matmul(group(j), A.rest[0:n, b, at], v, start=False, stop=(e.t == T - 1), skip_group_check=True)
                    ins.then_inc(S["pv"], 1)
            S.end_iteration(pe, "pe")

        def seg_act(act, plan, cur):
            for e in plan:
                p = e.quad % 2
                if e.kind in ("q", "k", "v", "ctx", "x_turned", "heads"):
                    act.wait_ge(S["ring_ps"], e.n + 1)
                    bank = ring_bank[e.n % 2]
                if e.kind == "ctx":
                    t0, t1, n = v_tiles(e.j)
                    k0, m = t0 * P, (t1 - t0 - 1) * P + n
                    act.activation(yT[:, k0:k0 + m], bank[0:CC, 0:m], ACT.Identity, bias=W_sb["lny_b"][:, 0:1],
                                   scale=W_sb["lny_g"][:, 0:1]).then_inc(ring_done(e), 1)
                if e.kind == "x_turned":
                    act.activation(xqT[:, :], bank[:, 0:TOK], ACT.Identity, bias=W_sb["lnx_b"][:, 0:1],
                                   scale=W_sb["lnx_g"][:, 0:1]).then_inc(ring_done(e), 1)
                if e.kind == "heads":
                    act.activation(attnT[:, e.quad, :], bank[:, 0:TOK], ACT.Copy).then_inc(S["heads_in"], 1)
                    act.wait_ge(S["heads_in"], e.quad + 1)
                    act.sem_inc(ring_done(e), 1)
                if e.kind in ("q", "k"):
                    if e.kind == "q" and e.r >= 2:
                        act.wait_ge(S["max_rows"], e.r - 1)
                        act.wait_ge(S["parts_out"], 48 * (e.r - 1))
                    cols, n = columns(e)
                    act.activation(first[p][:, cols], bank[:, 0:n], ACT.Copy).then_inc(S["first"], 1)
                if e.kind == "part1":
                    if e.j == 0:
                        for k in range(2):
                            act.wait_ge(S[f"ring_done{k}"], left_of[e.r][k])
                        if e.r:
                            act.wait_ge(S["parts_out"], 48 * e.r)
                    act.activation(others[:, 0, piece(e.j)], left[:, piece(e.j)], ACT.Copy).then_inc(S["part1"], 1)
                if e.kind == "v":
                    if e.j == 0 and e.quad >= 2 and cur is not None:
                        act.wait_ge(S["pv"], T * (e.quad - 1))
                    t0, t1, n = v_tiles(e.j)
                    act.activation(v_parts[p][0:n, t0:t1, :, 0, 0:D32],
                                   bank[0:n, 0:(t1 - t0) * P].rearrange("p (t h d) -> p t h d", h=4, d=D32),
                                   ACT.Copy).then_inc(S["first"], 1)
                if e.kind == "v_second":
                    if e.j == 0:
                        for k in range(2):
                            act.wait_ge(S[f"ring_done{k}"], v_left_of[e.r][k])
                    t = slice(T * e.j // PIECES, T * (e.j + 1) // PIECES)
                    act.activation(v_parts[p][:, t, :, 1, 0:D32].rearrange("p t h d -> p (t h) d"),
                                   v_left[:, t, :].rearrange("p t (h d) -> p (t h) d", d=D32),
                                   ACT.Copy).then_inc(S["v_second"], 1)
                if e.kind == "scores":
                    n, b = s.tiles[e.t][1], e.i % P_BUFS32
                    act.wait_ge(S["scores"], e.i + 1)
                    if e.i >= P_BUFS32:
                        act.wait_ge(S["pv"], e.i - P_BUFS32 + 1)
                    act.activation(A.probs[0:n, b, :].rearrange("p (a q) -> p a q", a=2), A.S4[0:n, e.i % 2, :, :],
                                   ACT.Exp, scale=A.scale).then_inc(S["probs"], 1)
            S.end_iteration(act, "act")

        def seg_dve(dve, plan, cur):
            chain = Chain(dve, S["dve_own"])
            for e in plan:
                p = e.quad % 2
                if e.kind in ("unit", "turn", "q", "k", "v", "proj"):
                    dve.wait_ge(S["ring_ps"], e.n + 1)
                    bank = ring_bank[e.n % 2]
                if e.kind == "unit":
                    qt, h, c = s.unit(e.k)
                    dve.tensor_reduce(A.unit_max[:, qt, h, c:c + 1], bank[:, 0:s.chunks[c][1]], AX.X,
                                      ALU.max).then_inc(ring_done(e), 1)
                    if e.k == s.NU - 1:
                        for k in range(2):
                            dve.wait_ge(S[f"ring_done{k}"], (e.n + 2 - k) // 2)
                        dve.tensor_reduce(A.negmax[:, :, :], A.unit_max[:, :, :, 0:len(s.chunks)], AX.X, ALU.max,
                                          negate=True).then_inc(S["max_rows"], 1)
                if e.kind == "turn":
                    if e.r >= 2:
                        dve.wait_ge(S[f"max_in{e.r % 2}"], rows_in(e.r - 2))
                    dve.tensor_copy(A.negmax_row[0:4, e.r % 2, :], bank[0:4, 0:TOK]).then_inc(S["turned"], 1)
                    dve.wait_ge(S["turned"], e.r + 1)
                    dve.sem_inc(ring_done(e), 1)
                if e.kind in ("q", "k"):
                    if e.kind == "q" and e.r:
                        dve.wait_ge(S["part2"], PIECES * e.r)
                    cols, n = columns(e)
                    dve.wait_ge(S["first"], e.f + 1)
                    dve.tensor_tensor(left[:, cols], bank[:, 0:n], first[p][:, cols], ALU.subtract).then_inc(ring_done(e), 1)
                if e.kind == "q_max":
                    dve.wait_ge(S["first"], q_of[e.r])
                    for h in range(4):
                        r = slice(D32 * h, D32 * h + D32)
                        ins = dve.tensor_copy(q_max[p][r, h, :], first[p][r, 0:TOK])
                    ins.then_inc(S["q_max"], 1)
                if e.kind == "v":
                    if e.j == 0 and e.r:
                        dve.wait_ge(S["v_third"], PIECES * e.r)
                    t0, t1, n = v_tiles(e.j)
                    dve.wait_ge(S["first"], e.f + 1)
                    dve.tensor_tensor(v_left[0:n, t0:t1, :].rearrange("p t (h d) -> p t h d", d=D32),
                                      bank[0:n, 0:(t1 - t0) * P].rearrange("p (t h d) -> p t h d", h=4, d=D32),
                                      v_parts[p][0:n, t0:t1, :, 0, 0:D32], ALU.subtract).then_inc(ring_done(e), 1)
                if e.kind == "take":
                    dve.wait_ge(S["pv"], T * (e.quad + 1))
                    for a in range(2):
                        ins = dve.tensor_reduce(sums[:, 4 * a:4 * a + 4, :],
                                                out_bank[a][:, 0:4 * 3 * V32].rearrange("p (j k d) -> p j d k", k=3, d=V32),
                                                AX.X, ALU.add)
                    ins.then_inc(S["taken"], 1)
                    dve.wait_ge(S["taken"], e.quad + 1)
                    chain(dve.reciprocal(inv[:, :, :], sums[:, :, D32:V32]))
                    if e.quad:
                        dve.wait_ge(S["heads_in"], e.quad)
                    by = lambda m: m.rearrange("p (h t) d -> p h t d", t=QT)
                    dve.tensor_tensor(attn[:, :, :].rearrange("p t (h d) -> p h t d", d=D32), by(sums[:, :, 0:D32]),
                                      by(inv[:, :, 0:1].to_broadcast([P, NG, D32])), ALU.mult).then_inc(S["heads_ok"], 1)
                if e.kind == "proj":
                    dve.wait_ge(S["x_res_in"], 16)
                    for t in range(QT):
                        ins = dve.tensor_tensor(x_res[:, t, :], x_res[:, t, :], W_sb["b_out"][:, :], ALU.add)
                    chain(ins)
                    dve.tensor_tensor(res[:, :, :].rearrange("p t c -> p (t c)"), bank[:, 0:TOK],
                                      x_res[:, :, :].rearrange("p t c -> p (t c)"), ALU.add).then_inc(S["res"], 1)
                if e.kind == "rest":
                    n, b, cols = s.tiles[e.t][1], e.i % P_BUFS32, slice(POOL_COLS32, 4 * TOK)
                    dve.wait_ge(S["probs"], e.i + 1)
                    dve.tensor_tensor(A.rest[0:n, b, cols], A.probs[0:n, b, cols], A.high(A.probs, b, n)[:, cols],
                                      ALU.subtract).then_inc(S["rest_dve"], 1)
                if e.kind == "ln_stats":
                    if e.j == 0:
                        dve.wait_ge(S["x_in"], 16)
                        dve.wait_ge(S["ctx_in"], 32)
                    for t in ln_piece[e.j]:
                        x = ln_tile(t)
                        ins = dve.bn_stats(L.st[0:x.shape[0], t, :], x)
                    chain(ins)
                    for t in ln_piece[e.j]:
                        n = ln_tile(t).shape[0]
                        ins = dve.bn_aggr(L.mv[0:n, t, :], L.st[0:n, t, :])
                    ins.then_inc(S["ln_stats"] if e.j < LN_PIECES - 1 else S["ln_var"], 1)
                if e.kind == "ln_apply":
                    if e.j == 0:
                        dve.wait_ge(S["ln_rstd"], 1)
                    for t in ln_piece[e.j]:
                        ins = ln_apply(dve, L, t, ln_tile(t), ln_tile(t))
                    ins.then_inc(S["ln_done"], 1)
            S.end_iteration(dve, "dve")

        def seg_pool(pool, plan, cur):
            for e in plan:
                p = e.quad % 2
                if e.kind == "scores":
                    n, b, cols = s.tiles[e.t][1], e.i % P_BUFS32, slice(0, POOL_COLS32)
                    pool.wait_ge(S["probs"], e.i + 1)
                    pool.tensor_tensor(A.rest[0:n, b, cols], A.probs[0:n, b, cols], A.high(A.probs, b, n)[:, cols],
                                       ALU.subtract).then_inc(S["rest"], 1)
                    pool.wait_ge(S["rest"], e.i + 1)
                if e.kind == "ln_rstd":
                    pool.wait_ge(S["ln_stats"], LN_PIECES - 1)
                    ln_rstd(pool, S, L, 0, tiles_y)
                    pool.wait_ge(S["ln_rstd"], 1)
                if e.kind == "part2":
                    pool.wait_ge(S["part1"], PIECES * e.r + e.j + 1)
                    if e.j == 0:
                        if e.r:
                            pool.wait_ge(S["parts_out"], 48 * e.r)
                    c = piece(e.j)
                    pool.tensor_tensor(others[:, 1, c], left[:, c], others[:, 0, c], ALU.subtract).then_inc(S["part2"], 1)
                    pool.wait_ge(S["part2"], PIECES * e.r + e.j + 1)
                if e.kind == "v_third":
                    pool.wait_ge(S["v_second"], PIECES * e.r + e.j + 1)
                    t = slice(T * e.j // PIECES, T * (e.j + 1) // PIECES)
                    pool.tensor_tensor(v_parts[p][:, t, :, 2, 0:D32].rearrange("p t h d -> p (t h) d"),
                                       v_left[:, t, :].rearrange("p t (h d) -> p (t h) d", d=D32),
                                       v_parts[p][:, t, :, 1, 0:D32].rearrange("p t h d -> p (t h) d"),
                                       ALU.subtract).then_inc(S["v_third"], 1)
                    pool.wait_ge(S["v_third"], PIECES * e.r + e.j + 1)
            S.end_iteration(pool, "pool")

        first_of, q_of, left_of, v_left_of = {}, {}, {}, {}

        def counts(plan):
            for e in plan:
                if e.kind == "q":
                    q_of[e.r] = e.f + 1
                if e.kind in ("q", "k"):
                    first_of[e.r] = e.f + 1
                    left_of[e.r] = ((e.n + 2) // 2, (e.n + 1) // 2)
                if e.kind == "v":
                    v_left_of[e.r] = ((e.n + 2) // 2, (e.n + 1) // 2)

        first_plan, middle_plan, last_plan = (schedule32(s, *a) for a in ((False, True), (True, True), (True, False)))

        def batches(eng, seg, sync=False):
            def run(plan, cur, nxt):
                counts(plan[0])
                if sync:
                    seg(eng, plan[0], plan[1], cur, nxt)
                else:
                    seg(eng, plan[0], cur)
            run(first_plan, None, 0)
            with eng.Fori(0, BATCH - 1) as i:
                run(middle_plan, i, i + 1)
            run(last_plan, BATCH - 1, None)

        with nc.Block() as block:
            @block.sync
            def _(sp):
                batches(sp, seg_sync, True)

            @block.tensor
            def _(pe):
                batches(pe, seg_pe)

            @block.scalar
            def _(act):
                batches(act, seg_act)

            @block.vector
            def _(dve):
                batches(dve, seg_dve)

            @block.gpsimd
            def _(pool):
                batches(pool, seg_pool)



def token_tiles(x):
    return x.rearrange("b t c -> (b t) c").rearrange("(s t p) c -> s p t c", t=FT, p=P)


class Banks:

    def __init__(self, G):
        self.all = [G.S4[:, a, c, :] for a in range(2) for c in range(2)] + [b[:, :] for b in G.bank]


def flat(t):
    return t.rearrange("p t c -> p (t c)")


def transpose_tiles(pe, bank, tiles, ident):
    for t, tile in enumerate(tiles):
        ins = pe.transpose(bank[0:tile.shape[1], t * P:(t + 1) * P], tile, ident[:, :])
    return ins


def mlp32(nc, G, stage, xo_in, skip_in, add_in, out, w, last_ln):
    KH = w["li2_w"].shape[1] // P
    with ExitStack() as ctx:
        sb = Mem(nc, ctx, stage)
        banks = Banks(G).all
        names_w = ["li2_w", "li2_b", "li3_w", "li3_b", "ln3_g", "ln3_b"] + ["ln2_g", "ln2_b"] * last_ln
        W_sb = {n: sb(n, list(w[n].shape)) for n in names_w}
        xo, skip, add, xn = (sb(n, [P, FT, C]) for n in ("xo", "skip", "add", "xn"))
        nT = sb("nT", [C, FTOK])
        hT = sb("hT", [P, KH, FTOK])
        L = LnMem(sb, FT)
        S = Sems(nc, ctx, stage, ["xo_in", "skip_in", "add_in", "xn", "xnT_ps", "nT", "h_ps", "h", "y_ps", "res",
                                  "x_out", "dve_own"] + LN_SEMS)
        load_weights(nc, ctx, stage, [(W_sb[n][...], w[n]) for n in names_w], L.prepare)

        with nc.Block() as block:
            @block.sync
            def _(sp):
                with sp.Fori(0, FSTEPS) as i:
                    sp.dma_start(xo[:, :, :], token_tiles(xo_in)[i]).then_inc(S["xo_in"], 16)
                    sp.dma_start(skip[:, :, :], token_tiles(skip_in)[i]).then_inc(S["skip_in"], 16)
                    if not last_ln:
                        sp.dma_start(add[:, :, :], token_tiles(add_in)[i]).then_inc(S["add_in"], 16)
                    sp.wait_ge(S["res"], 1)
                    sp.dma_start(token_tiles(out)[i], xn[:, :, :]).then_inc(S["x_out"], 16)
                    sp.wait_ge(S["x_out"], 16)
                    S.next_iteration(sp)

            @block.tensor
            def _(pe):
                with pe.Fori(0, FSTEPS) as i:
                    pe.wait_ge(S["xn"], 1)
                    transpose_tiles(pe, banks[4], [xn[:, t, :] for t in range(FT)], G.ident).then_inc(S["xnT_ps"], 1)
                    pe.wait_ge(S["nT"], 1)
                    for k in range(KH):
                        pe.matmul(banks[k], W_sb["li2_w"][:, k * P:(k + 1) * P], nT[:, :],
                                  start=True, stop=True).then_inc(S["h_ps"], 1)
                    pe.wait_ge(S["h"], KH)
                    for t in range(FT):
                        for k in range(KH):
                            ins = pe.matmul(banks[5][:, t * C:(t + 1) * C], hT[:, k, t * P:(t + 1) * P],
                                            W_sb["li3_w"][:, k, :], start=(k == 0), stop=(k == KH - 1))
                    ins.then_inc(S["y_ps"], 1)
                    S.end_iteration(pe, "pe")

            @block.scalar
            def _(act):
                with act.Fori(0, FSTEPS) as i:
                    act.wait_ge(S["xnT_ps"], 1)
                    act.activation(nT[:, :], banks[4], ACT.Identity, bias=W_sb["ln3_b"][:, 0:1],
                                   scale=W_sb["ln3_g"][:, 0:1]).then_inc(S["nT"], 1)
                    for k in range(KH):
                        act.wait_ge(S["h_ps"], k + 1)
                        act.activation(hT[:, k, :], banks[k], ACT.Gelu,
                                       bias=W_sb["li2_b"][:, k:k + 1]).then_inc(S["h"], 1)
                    S.end_iteration(act, "act")

            @block.vector
            def _(dve):
                with dve.Fori(0, FSTEPS) as i:
                    chain = Chain(dve, S["dve_own"])
                    L.begin(chain)
                    dve.wait_ge(S["xo_in"], 16)
                    ln_stats(dve, S, L, [xo[:, t, :] for t in range(FT)])
                    for t in range(FT):
                        ins = ln_apply(dve, L, t, xn[:, t, :], xo[:, t, :])
                    ins.then_inc(S["xn"], 1)
                    dve.wait_ge(S["skip_in"], 16)
                    chain(dve.tensor_tensor(flat(skip[:, :, :]), flat(skip[:, :, :]), flat(xo[:, :, :]), ALU.add))
                    for t in range(FT):
                        ins = dve.tensor_tensor(skip[:, t, :], skip[:, t, :], W_sb["li3_b"][:, :], ALU.add)
                    chain(ins)
                    if not last_ln:
                        dve.wait_ge(S["add_in"], 16)
                        chain(dve.tensor_tensor(flat(skip[:, :, :]), flat(skip[:, :, :]), flat(add[:, :, :]), ALU.add))
                    dve.wait_ge(S["y_ps"], 1)
                    if not last_ln:
                        dve.tensor_tensor(flat(xn[:, :, :]), flat(skip[:, :, :]), banks[5], ALU.add).then_inc(S["res"], 1)
                    else:
                        chain(dve.tensor_tensor(flat(skip[:, :, :]), flat(skip[:, :, :]), banks[5], ALU.add))
                        ln_stats(dve, S, L, [skip[:, t, :] for t in range(FT)])
                        for t in range(FT):
                            ins = ln_apply(dve, L, t, xn[:, t, :], skip[:, t, :])
                        chain(ins)
                        for t in range(FT):
                            ins = dve.tensor_tensor(xn[:, t, :], xn[:, t, :], W_sb["ln2_g"][:, :], ALU.mult)
                        chain(ins)
                        for t in range(FT):
                            ins = dve.tensor_tensor(xn[:, t, :], xn[:, t, :], W_sb["ln2_b"][:, :], ALU.add)
                        ins.then_inc(S["res"], 1)
                    S.end_iteration(dve, "dve")

            @block.gpsimd
            def _(pool):
                with pool.Fori(0, FSTEPS) as i:
                    for k in range(1 + last_ln):
                        ln_rstd(pool, S, L, k, FT)
                    S.end_iteration(pool, "pool")


def experts(nc, G, stage, x_in, out, w, kind):
    K_TOP = {"hash": 4, "top1": 1, "shared": 2}[kind]
    E = {"hash": 32, "top1": 8, "shared": 16}[kind]
    EG = E + (kind == "shared")
    NH = w["w_down"].shape[1]
    with ExitStack() as ctx:
        sb = Mem(nc, ctx, stage)
        banks = Banks(G).all
        names_w = {"hash": ["hasher", "keys", "scale"], "top1": ["gate", "ln_scale", "ln_bias", "b1", "b2"],
                   "shared": ["gate", "w_gate"]}[kind] + ["w_up", "w_down", "spread", "iota"]
        W_sb = {n: sb(n, list(w[n].shape)) for n in names_w}
        x, z = sb("x", [P, FT, C]), sb("z", [P, FT, C])
        res = sb("res", [P, FT, C])
        xh = sb("xh", [P, FT, C]) if kind == "top1" else None
        zT = sb("zT", [C, FTOK])
        xhT = sb("xhT", [C, FTOK]) if kind == "top1" else zT
        hashT = sb("hashT", [32, FTOK])
        logits = sb("logits", [P, FT, EG])
        best, best_f = sb("best", [P, FT, 8]), sb("best_f", [P, FT, 8])
        best_i = sb("best_i", [P, FT, 8], U32)
        weight = sb("weight", [P, FT, 8])
        total, inv = sb("total", [P, FT, 1]), sb("inv", [P, FT, 1])
        sig = sb("sig", [P, FT, 1])
        term = sb("term", [P, FT, E])
        gates = sb("gates", [P, FT, EG])
        gatesT = sb("gatesT", [EG, FTOK])
        act_out = sb("act_out", [P, NH, FTOK])
        hT = sb("hT", [P, NH, FTOK])
        L = LnMem(sb, FT)
        S = Sems(nc, ctx, stage, ["x_in", "z", "xh", "zT_ps", "zT", "hash_ps", "hash", "logits_ps", "logits", "best", "weight",
                                  "gates", "gT_ps", "gT", "up_ps", "act", "h", "y_ps", "res", "x_out",
                                  "dve_own"] + LN_SEMS)
        load_weights(nc, ctx, stage, [(W_sb[n][...], w[n]) for n in names_w], L.prepare)

        if kind == "top1":
            s_bias = ctx.enter_context(nc.semaphore(f"{stage}_bias"))
            HID = NH * P // E
            with nc.Block() as block:
                @block.tensor
                def _(pe):
                    for e in range(E):
                        r = e % (P // HID) * HID
                        ins = pe.matmul(banks[0][r:r + HID, e // (P // HID):e // (P // HID) + 1],
                                        W_sb["w_up"][:, e * HID:(e + 1) * HID], W_sb["ln_bias"][:, e:e + 1],
                                        start=True, stop=True)
                    ins.then_inc(s_bias, 1)

                @block.vector
                def _(dve):
                    dve.wait_ge(s_bias, 1)
                    dve.sem_clear(s_bias)
                    dve.tensor_tensor(W_sb["b1"][:, :], W_sb["b1"][:, :], banks[0][:, 0:NH], ALU.add)
                    for e in range(E):
                        w1 = W_sb["w_up"][:, e * HID:(e + 1) * HID]
                        dve.tensor_scalar(w1, w1, W_sb["ln_scale"][:, e:e + 1], None, ALU.mult)

        gate_w = W_sb["gate"] if kind != "hash" else None
        per_tile = 3 if kind == "shared" else 2

        def tile_banks(k):
            return [banks[2 + (k % 2) * per_tile + j] for j in range(per_tile)]

        def has_own_gate(k):
            return kind == "shared"

        with nc.Block() as block:
            @block.sync
            def _(sp):
                with sp.Fori(0, FSTEPS) as i:
                    sp.dma_start(x[:, :, :], token_tiles(x_in)[i]).then_inc(S["x_in"], 16)
                    sp.wait_ge(S["res"], 1)
                    sp.dma_start(token_tiles(out)[i], res[:, :, :]).then_inc(S["x_out"], 16)
                    sp.wait_ge(S["x_out"], 16)
                    S.next_iteration(sp)

            @block.tensor
            def _(pe):
                with pe.Fori(0, FSTEPS) as i:
                    pe.wait_ge(S["z"], 1)
                    transpose_tiles(pe, banks[0], [z[:, t, :] for t in range(FT)], G.ident).then_inc(S["zT_ps"], 1)
                    pe.wait_ge(S["zT"], 1)
                    keys, keyed = gate_w, zT
                    if kind == "hash":
                        pe.matmul(banks[0][0:32, :], W_sb["hasher"][:, :], zT[:, :], start=True, stop=True).then_inc(S["hash_ps"], 1)
                        pe.wait_ge(S["hash"], 1)
                        keys, keyed = W_sb["keys"], hashT
                    for t in range(FT):
                        ins = pe.matmul(banks[1][:, t * EG:(t + 1) * EG], keyed[:, t * P:(t + 1) * P], keys[:, :],
                                        start=True, stop=True)
                    ins.then_inc(S["logits_ps"], 1)
                    if kind == "top1":
                        pe.wait_ge(S["xh"], 1)
                        transpose_tiles(pe, banks[0], [xh[:, t, :] for t in range(FT)], G.ident).then_inc(S["zT_ps"], 1)
                        pe.wait_ge(S["zT"], 2)
                    pe.wait_ge(S["gates"], 1)
                    transpose_tiles(pe, banks[0], [gates[:, t, :] for t in range(FT)], G.ident).then_inc(S["gT_ps"], 1)
                    pe.wait_ge(S["gT"], 1)
                    for k in range(NH):
                        tb = tile_banks(k)
                        cols = slice(k * P, (k + 1) * P)
                        if k >= 2:
                            pe.wait_ge(S["act"], k - 1)
                            pe.wait_ge(S["h"], k - 1)
                        pe.matmul(tb[0], W_sb["w_gate" if kind == "shared" else "w_up"][:, cols], xhT[:, :],
                                  start=True, stop=True)
                        if kind == "shared":
                            pe.matmul(tb[2], W_sb["w_up"][:, cols], zT[:, :], start=True, stop=True)
                        pe.matmul(tb[1], W_sb["spread"][:, cols], gatesT[:, :], start=True, stop=True).then_inc(S["up_ps"], 1)
                    pe.wait_ge(S["h"], NH)
                    for t in range(FT):
                        o = banks[1][:, t * C:(t + 1) * C]
                        if kind == "top1":
                            pe.matmul(o, gatesT[:, t * P:(t + 1) * P], W_sb["b2"][:, :], start=True, stop=False)
                        for k in range(NH):
                            ins = pe.matmul(o, hT[:, k, t * P:(t + 1) * P], W_sb["w_down"][:, k, :],
                                            start=(k == 0 and kind != "top1"), stop=(k == NH - 1))
                    ins.then_inc(S["y_ps"], 1)
                    S.end_iteration(pe, "pe")

            @block.scalar
            def _(act):
                with act.Fori(0, FSTEPS) as i:
                    act.wait_ge(S["zT_ps"], 1)
                    act.activation(zT[:, :], banks[0], ACT.Copy).then_inc(S["zT"], 1)
                    if kind == "hash":
                        act.wait_ge(S["hash_ps"], 1)
                        act.activation(hashT[:, :], banks[0][0:32, :], ACT.Copy).then_inc(S["hash"], 1)
                    if kind == "top1":
                        act.wait_ge(S["zT_ps"], 2)
                        act.activation(xhT[:, :], banks[0], ACT.Copy).then_inc(S["zT"], 1)
                    if kind != "top1":
                        act.wait_ge(S["best"], 1)
                        ins = act.activation(weight[:, :, :], best[:, :, :], ACT.Exp)
                        if kind == "shared":
                            ins = act.activation(sig[:, :, :], logits[:, :, E:EG], ACT.Exp, scale=-1.0)
                        ins.then_inc(S["weight"], 1)
                    act.wait_ge(S["gT_ps"], 1)
                    act.activation(gatesT[:, :], banks[0][0:EG, :], ACT.Copy).then_inc(S["gT"], 1)
                    for k in range(NH):
                        act.wait_ge(S["up_ps"], k + 1)
                        if kind == "top1":
                            ins = act.activation(act_out[:, k, :], tile_banks(k)[0], ACT.Gelu, bias=W_sb["b1"][:, k:k + 1])
                        else:
                            ins = act.activation(act_out[:, k, :], tile_banks(k)[0], ACT.Silu)
                        ins.then_inc(S["act"], 1)
                    S.end_iteration(act, "act")

            @block.vector
            def _(dve):
                with dve.Fori(0, FSTEPS) as i:
                    chain = Chain(dve, S["dve_own"])
                    L.begin(chain)
                    dve.wait_ge(S["x_in"], 16)
                    ln_stats(dve, S, L, [x[:, t, :] for t in range(FT)])
                    for t in range(FT):
                        ins = ln_apply(dve, L, t, z[:, t, :], x[:, t, :])
                    ins.then_inc(S["z"], 1)
                    dve.wait_ge(S["z"], 1)
                    if kind == "top1":
                        ln_stats(dve, S, L, [z[:, t, :] for t in range(FT)])
                        for t in range(FT):
                            ins = ln_apply(dve, L, t, xh[:, t, :], z[:, t, :])
                        ins.then_inc(S["xh"], 1)
                    dve.wait_ge(S["logits_ps"], 1)
                    chain(dve.tensor_copy(flat(logits[:, :, :]), banks[1][:, 0:FT * EG]))
                    for t in range(FT):
                        ins = dve.max(best[:, t, :], logits[:, t, 0:E])
                    chain(ins)
                    for t in range(FT):
                        ins = dve.max_index(best_i[:, t, :], best[:, t, :], logits[:, t, 0:E])
                    chain(ins)
                    chain(dve.tensor_copy(best_f[:, :, :], best_i[:, :, :]))
                    if kind == "top1":
                        for t in range(FT):
                            ins = dve.tensor_scalar(gates[:, t, :], W_sb["iota"][:, :], best_f[:, t, 0:1], None, ALU.is_equal)
                        ins.then_inc(S["gates"], 1)
                    else:
                        chain(dve.tensor_copy(total[:, :, :], best[:, :, 0:1]))
                        for t in range(FT):
                            ins = dve.tensor_scalar(best[:, t, :], best[:, t, :], total[:, t, :], None, ALU.subtract)
                        ins.then_inc(S["best"], 1)
                        dve.wait_ge(S["weight"], 1)
                        chain(dve.tensor_reduce(total[:, :, :], weight[:, :, 0:K_TOP], AX.X, ALU.add))
                        chain(dve.reciprocal(inv[:, :, :], total[:, :, :]))
                        for t in range(FT):
                            ins = dve.tensor_scalar(weight[:, t, :], weight[:, t, :], inv[:, t, :], None, ALU.mult)
                        chain(ins)
                        for k in range(K_TOP):
                            for t in range(FT):
                                ins = dve.tensor_scalar(gates[:, t, 0:E] if k == 0 else term[:, t, :], W_sb["iota"][:, :],
                                                        best_f[:, t, k:k + 1], weight[:, t, k:k + 1], ALU.is_equal, ALU.mult)
                            chain(ins)
                            if k:
                                chain(dve.tensor_tensor(gates[:, :, 0:E], gates[:, :, 0:E], term[:, :, :], ALU.add))
                        if kind == "shared":
                            chain(dve.tensor_scalar(sig[:, :, :], sig[:, :, :], 1.0, None, ALU.add))
                            chain(dve.reciprocal(gates[:, :, E:EG], sig[:, :, :]))
                        dve.tensor_copy(total[:, :, :], inv[:, :, :]).then_inc(S["gates"], 1)
                    for k in range(NH):
                        dve.wait_ge(S["act"], k + 1)
                        tb = tile_banks(k)
                        if kind == "shared":
                            chain(dve.tensor_tensor(act_out[:, k, :], act_out[:, k, :], tb[2], ALU.mult))
                        dve.tensor_tensor(hT[:, k, :], act_out[:, k, :], tb[1], ALU.mult).then_inc(S["h"], 1)
                    if kind == "hash":
                        chain(dve.tensor_tensor(flat(x[:, :, :]), flat(x[:, :, :]), flat(z[:, :, :]), ALU.add))
                    dve.wait_ge(S["y_ps"], 1)
                    if kind == "hash":
                        ins = dve.scalar_tensor_tensor(out=flat(res[:, :, :]), in0=banks[1], scalar=W_sb["scale"][:, 0:1],
                                                       in1=flat(x[:, :, :]), op0=ALU.mult, op1=ALU.add)
                    else:
                        ins = dve.tensor_tensor(flat(res[:, :, :]), banks[1], flat(x[:, :, :]), ALU.add)
                    ins.then_inc(S["res"], 1)
                    S.end_iteration(dve, "dve")

            @block.gpsimd
            def _(pool):
                with pool.Fori(0, FSTEPS) as i:
                    for k in range(1 + (kind == "top1")):
                        ln_rstd(pool, S, L, k, FT)
                    S.end_iteration(pool, "pool")


ROUND = 1.5 * 2.0 ** 23


def bit_ffn(nc, G, stage, x_in, out, w):
    KH = w["w1"].shape[1] // P
    NB = FTOK // TOK
    with ExitStack() as ctx:
        sb = Mem(nc, ctx, stage)
        banks = Banks(G).all
        W_sb = {n: sb(n, list(w[n].shape)) for n in ("w1", "w2", "conv_w", "conv_b")}
        x, z, res = (sb(n, [P, FT, C]) for n in ("x", "z", "res"))
        top, unit, per = (sb(n, [P, FT, 1]) for n in ("top", "unit", "per"))
        zT = sb("zT", [C, FTOK])
        hp = sb("hp", [P, KH, NB, TOK + 2])
        cv = sb("cv", [P, KH, NB, TOK])
        sT = sb("sT", [P, KH, FTOK])
        s_tok = sb("s_tok", [P, FT, KH * P])
        ones = sb("ones", [P, P])
        wsum, wall, wstep, wper = (sb(n, [P, 2]) for n in ("wsum", "wall", "wstep", "wper"))
        L = LnMem(sb, FT)
        S = Sems(nc, ctx, stage, ["x_in", "z", "zT_ps", "zT", "h_ps", "hp", "cv", "sT", "st_ps", "s_tok", "sq", "sqT_ps",
                                  "sqT", "y_ps", "res", "x_out", "dve_own"] + LN_SEMS)

        def prepare(pool, chain):
            chain(pool.memset(hp[:, :, :, :], 0.0))
            chain(pool.memset(ones[:, :], 1.0))
            L.prepare(pool, chain)

        load_weights(nc, ctx, stage, [(W_sb[n][...], w[n]) for n in W_sb], prepare)

        s_sum, s_all = (ctx.enter_context(nc.semaphore(f"{stage}_{n}")) for n in ("wsum", "wall"))
        s_own = ctx.enter_context(nc.semaphore(f"{stage}_wown"))
        with nc.Block() as block:
            @block.tensor
            def _(pe):
                pe.wait_ge(s_sum, 1)
                pe.sem_clear(s_sum)
                pe.matmul(banks[0][:, 0:2], ones[:, :], wsum[:, :], start=True, stop=True).then_inc(s_all, 1)

            @block.vector
            def _(dve):
                chain = Chain(dve, s_own)
                both = [W_sb["w1"][:, :], W_sb["w2"][:, :, :].rearrange("p k c -> p (k c)")]
                for j, m in enumerate(both):
                    ins = dve.tensor_reduce(wsum[:, j:j + 1], m, AX.X, ALU.add, apply_absolute_value=True)
                ins.then_inc(s_sum, 1)
                dve.wait_ge(s_all, 1)
                dve.sem_clear(s_all)
                chain(dve.tensor_scalar(wper[:, :], banks[0][:, 0:2], 1.0 / (KH * P * C), 1e-5, ALU.mult, ALU.max))
                chain(dve.reciprocal(wstep[:, :], wper[:, :]))
                for j, m in enumerate(both):
                    chain(dve.tensor_scalar(m, m, wstep[:, j:j + 1], ROUND, ALU.mult, ALU.add))
                    chain(dve.tensor_scalar(m, m, ROUND, 1.0, ALU.subtract, ALU.min))
                    chain(dve.tensor_scalar(m, m, -1.0, wper[:, j:j + 1], ALU.max, ALU.mult))
                dve.sem_clear(s_own)

        def quantise(dve, chain, tiles):
            for t, m in enumerate(tiles):
                ins = dve.tensor_reduce(top[:, t, :], m, AX.X, ALU.max, apply_absolute_value=True)
            chain(ins)
            chain(dve.tensor_scalar(top[:, :, :], top[:, :, :], 1e-5, None, ALU.max))
            chain(dve.reciprocal(unit[:, :, :], top[:, :, :]))
            chain(dve.tensor_scalar(unit[:, :, :], unit[:, :, :], 127.0, None, ALU.mult))
            chain(dve.reciprocal(per[:, :, :], unit[:, :, :]))
            for t, m in enumerate(tiles):
                ins = dve.tensor_scalar(m, m, unit[:, t, :], ROUND, ALU.mult, ALU.add)
            chain(ins)
            for t, m in enumerate(tiles):
                ins = dve.tensor_scalar(m, m, ROUND, 127.0, ALU.subtract, ALU.min)
            chain(ins)
            for t, m in enumerate(tiles):
                ins = dve.tensor_scalar(m, m, -128.0, per[:, t, :], ALU.max, ALU.mult)
            return ins

        with nc.Block() as block:
            @block.sync
            def _(sp):
                with sp.Fori(0, FSTEPS) as i:
                    sp.dma_start(x[:, :, :], token_tiles(x_in)[i]).then_inc(S["x_in"], 16)
                    sp.wait_ge(S["res"], 1)
                    sp.dma_start(token_tiles(out)[i], res[:, :, :]).then_inc(S["x_out"], 16)
                    sp.wait_ge(S["x_out"], 16)
                    S.next_iteration(sp)

            @block.tensor
            def _(pe):
                with pe.Fori(0, FSTEPS) as i:
                    pe.wait_ge(S["z"], 1)
                    transpose_tiles(pe, banks[4], [z[:, t, :] for t in range(FT)], G.ident).then_inc(S["zT_ps"], 1)
                    pe.wait_ge(S["zT"], 1)
                    for k in range(KH):
                        pe.matmul(banks[k], W_sb["w1"][:, k * P:(k + 1) * P], zT[:, :], start=True, stop=True).then_inc(S["h_ps"], 1)
                    pe.wait_ge(S["hp"], KH)
                    pe.wait_ge(S["sT"], KH)
                    for t in range(FT):
                        for k in range(KH):
                            ins = pe.transpose(banks[t][:, k * P:(k + 1) * P], sT[:, k, t * P:(t + 1) * P], G.ident[:, :])
                        ins.then_inc(S["st_ps"], 1)
                    pe.wait_ge(S["sq"], 1)
                    for k in range(KH):
                        for t in range(FT):
                            ins = pe.transpose(banks[4 + k][:, t * P:(t + 1) * P], s_tok[:, t, k * P:(k + 1) * P], G.ident[:, :])
                        ins.then_inc(S["sqT_ps"], 1)
                    pe.wait_ge(S["sqT"], KH)
                    for t in range(FT):
                        for k in range(KH):
                            ins = pe.matmul(banks[0][:, t * C:(t + 1) * C], sT[:, k, t * P:(t + 1) * P], W_sb["w2"][:, k, :],
                                            start=(k == 0), stop=(k == KH - 1))
                    ins.then_inc(S["y_ps"], 1)
                    S.end_iteration(pe, "pe")

            @block.scalar
            def _(act):
                with act.Fori(0, FSTEPS) as i:
                    act.wait_ge(S["zT_ps"], 1)
                    act.activation(zT[:, :], banks[4], ACT.Copy).then_inc(S["zT"], 1)
                    for k in range(KH):
                        act.wait_ge(S["h_ps"], k + 1)
                        act.activation(hp[:, k, :, 1:TOK + 1], banks[k].rearrange("p (b t) -> p b t", b=NB),
                                       ACT.Copy).then_inc(S["hp"], 1)
                    for k in range(KH):
                        act.wait_ge(S["cv"], k + 1)
                        act.activation(sT[:, k, :], cv[:, k, :, :].rearrange("p b t -> p (b t)"), ACT.Silu,
                                       bias=W_sb["conv_b"][:, k:k + 1]).then_inc(S["sT"], 1)
                    for t in range(FT):
                        act.wait_ge(S["st_ps"], t + 1)
                        act.activation(s_tok[:, t, :], banks[t], ACT.Copy).then_inc(S["s_tok"], 1)
                    for k in range(KH):
                        act.wait_ge(S["sqT_ps"], k + 1)
                        act.activation(sT[:, k, :], banks[4 + k], ACT.Copy).then_inc(S["sqT"], 1)
                    S.end_iteration(act, "act")

            @block.vector
            def _(dve):
                with dve.Fori(0, FSTEPS) as i:
                    chain = Chain(dve, S["dve_own"])
                    L.begin(chain)
                    dve.wait_ge(S["x_in"], 16)
                    ln_stats(dve, S, L, [x[:, t, :] for t in range(FT)])
                    for t in range(FT):
                        ins = ln_apply(dve, L, t, z[:, t, :], x[:, t, :])
                    chain(ins)
                    quantise(dve, chain, [z[:, t, :] for t in range(FT)]).then_inc(S["z"], 1)
                    for k in range(KH):
                        dve.wait_ge(S["hp"], k + 1)
                        chain(dve.tensor_scalar(cv[:, k, :, :], hp[:, k, :, 0:TOK], W_sb["conv_w"][:, k, 0:1], None, ALU.mult))
                        for j in (1, 2):
                            ins = dve.scalar_tensor_tensor(out=cv[:, k, :, :], in0=hp[:, k, :, j:j + TOK],
                                                           scalar=W_sb["conv_w"][:, k, j:j + 1], in1=cv[:, k, :, :],
                                                           op0=ALU.mult, op1=ALU.add)
                            if j == 1:
                                chain(ins)
                        ins.then_inc(S["cv"], 1)
                    dve.wait_ge(S["s_tok"], FT)
                    quantise(dve, chain, [s_tok[:, t, :] for t in range(FT)]).then_inc(S["sq"], 1)
                    dve.wait_ge(S["y_ps"], 1)
                    dve.tensor_tensor(flat(res[:, :, :]), banks[0], flat(x[:, :, :]), ALU.add).then_inc(S["res"], 1)
                    S.end_iteration(dve, "dve")

            @block.gpsimd
            def _(pool):
                with pool.Fori(0, FSTEPS) as i:
                    ln_rstd(pool, S, L, 0, FT)
                    S.end_iteration(pool, "pool")


def stages(nc, G, d, sub, out):
    def scratch(name):
        return nc.dram_tensor(f"{name}_dram", [BATCH, TOK, C], F32, kind="Internal").ap()

    x = [d["x"]] + [scratch(f"x_after_{i}") for i in range(7)] + [out]
    own_x1, own_xo, mid_x, cross_xo = (scratch(n) for n in ("own_x1", "own_xo", "mid_x", "cross_xo"))
    attention8(nc, G, "a0", x[0], x[1], sub("a0_"), True)
    experts(nc, G, "f0", x[1], x[2], sub("f0_"), "hash")
    attention8(nc, G, "a1", x[2], x[3], sub("a1_"), False)
    bit_ffn(nc, G, "f1", x[3], x[4], sub("f1_"))
    attention32(nc, G, "own", x[4], own_x1, own_xo, sub("own_"), True)
    mlp32(nc, G, "own_mlp", own_xo, own_x1, None, mid_x, sub("own_"), True)
    cross32(nc, G, "cross", mid_x, cross_xo, sub("cross_"))
    mlp32(nc, G, "cross_mlp", cross_xo, mid_x, x[4], x[5], sub("cross_"), False)
    experts(nc, G, "f2", x[5], x[6], sub("f2_"), "top1")
    attention8(nc, G, "a3", x[6], x[7], sub("a3_"), False)
    experts(nc, G, "f3", x[7], x[8], sub("f3_"), "shared")



class Globals:
    pass


def program(nc, d, out):
    with ExitStack() as ctx:
        G = Globals()
        G.S4 = ctx.enter_context(nc.psum_tensor("scores_ps", [P, 2, 2, 512], F32))
        G.bank = [ctx.enter_context(nc.psum_tensor(f"bank{i}", [P, 512], F32)) for i in range(4)]
        sb = Mem(nc, ctx, "shared")
        G.ident = sb("ident", [P, P])
        G.spread32 = sb("spread32", [97, 97])
        G.past = sb("past", [P, QT, TOK])
        load_weights(nc, ctx, "shared", [(G.ident[:, :], d["ident"]),
                                         (G.spread32[:, :], d["spread32"]), (G.past[:, :, :], d["past"])])
        G.ctxT, G.ctx = d["ctxT"], d["ctx_512"]
        G.row_of = d["row_of"]
        sub = lambda pre: {k[len(pre):]: v for k, v in d.items() if k.startswith(pre)}
        stages(nc, G, d, sub, out)



def layout(i):
    import numpy as np

    f = np.float32
    a = {"x": i["x"], "ctx_512": i["ctx_512"], "ctxT": i["ctx_512"].transpose(0, 2, 1)}
    a["ident"] = np.eye(P, dtype=f)
    r = np.arange(P)
    a["spread32"] = np.repeat((np.arange(97) == 96).astype(f)[:, None], 97, axis=1)
    q = (np.arange(QT)[None, :, None] * P + r[:, None, None])
    a["past"] = np.where(np.arange(TOK)[None, None, :] <= q, f(0), f(-1e30)).astype(f)

    def rep(v, n=1):
        return np.broadcast_to(np.tile(v, n), (P, n * v.size))

    def col(v):
        return v.reshape(-1, 1) if v.size <= P else v.reshape(-1, P).T

    def bcol(v):
        return np.broadcast_to(v.reshape(-1, 1), (v.size, P))

    z = np.zeros(C, f)
    n = "L0_xattn_"
    a.update({"a0_wq_s": i[n + "Wq"], "a0_wk_s": i[n + "Wk"], "a0_wv_s": i[n + "Wv"], "a0_bq_s": col(i[n + "bq"]),
              "a0_bk_s": col(i[n + "bk"]), "a0_bv_s": bcol(i[n + "bv"]),
              "a0_wq_c": i[n + "Wcq"], "a0_wk_c": i[n + "Wck"], "a0_wv_c": i[n + "Wcv"], "a0_bq_c": col(i[n + "bcq"]),
              "a0_bk_c": col(i[n + "bck"]), "a0_bv_c": bcol(i[n + "bcv"]),
              "a0_w_plain": i[n + "Wp"], "a0_b_out": rep(i[n + "bp"])})
    n = "L1_xattn_"
    a.update({"a1_wq_c": i[n + "Wq"].T, "a1_wk_c": i[n + "Wkv"][0:C].T, "a1_wv_c": i[n + "Wkv"][C:].T,
              "a1_bq_c": col(z), "a1_bk_c": col(z), "a1_bv_c": bcol(z),
              "a1_w_plain": i[n + "Wo"].T, "a1_b_out": rep(z)})
    n = "L3_xattn_"
    a.update({"a3_wq_c": i[n + "Wq"], "a3_wk_c": i[n + "Wk"], "a3_wv_c": i[n + "Wv"], "a3_bq_c": col(i[n + "bq"]),
              "a3_bk_c": col(i[n + "bk"]), "a3_bv_c": bcol(i[n + "bv"]),
              "a3_w_plain": i[n + "Wo"], "a3_b_out": rep(i[n + "bo"])})
    for stage, pre in (("own_", "L2_xattn_a1_"), ("cross_", "L2_xattn_a2_")):
        for m in "qkv":
            a[stage + "w" + m] = i[pre + "w" + m].transpose(1, 0, 2).reshape(i[pre + "w" + m].shape[1], -1)
        o = np.zeros((97, HEADS, C), f)
        for part in range(3):
            o[32 * part:32 * part + 32] = i[pre + "li1_w"].reshape(HEADS, 32, C).transpose(1, 0, 2)
        a.update({stage + "w_out": o if stage == "own_" else i[pre + "li1_w"].reshape(-1, P, C).transpose(1, 0, 2), stage + "b_out": rep(i[pre + "li1_b"]),
                  stage + "li2_w": i[pre + "li2_w"], stage + "li2_b": col(i[pre + "li2_b"]),
                  stage + "li3_w": i[pre + "li3_w"].reshape(-1, P, C).transpose(1, 0, 2),
                  stage + "li3_b": rep(i[pre + "li3_b"])})
        for v in ("lnx", "lny", "ln3"):
            a[f"{stage}{v}_g"], a[f"{stage}{v}_b"] = col(i[f"{pre}{v}_g"]), col(i[f"{pre}{v}_b"])
    for v in ("ln1", "ln2"):
        a[f"own_{v}_g"], a[f"own_{v}_b"] = rep(i[f"L2_xattn_{v}_g"]), rep(i[f"L2_xattn_{v}_b"])
    a["row_of"] = np.broadcast_to(np.eye(P, dtype=f)[:, 0:4, None], (P, 4, P))

    def spread(experts, hidden):
        return np.repeat(np.eye(experts, dtype=f), hidden, axis=1)

    def iota(n):
        return np.broadcast_to(np.arange(n, dtype=f), (P, n))

    def down(v):
        return v.reshape(-1, P, C).transpose(1, 0, 2)

    n = "L0_ffn_"
    a.update({"f0_hasher": i[n + "hasher_w"].T, "f0_keys": i[n + "keys"].T,
              "f0_scale": np.broadcast_to(i[n + "scale"], (P, 1)),
              "f0_w_up": i[n + "values_down"].transpose(1, 0, 2).reshape(C, -1),
              "f0_w_down": down(i[n + "values_up"].reshape(-1, C)), "f0_spread": spread(32, 32), "f0_iota": iota(32)})
    n = "L1_ffn_"
    a.update({"f1_w1": i[n + "w1"].T, "f1_w2": down(i[n + "w2"].T),
              "f1_conv_w": i[n + "conv_w"].reshape(-1, P, 3).transpose(1, 0, 2), "f1_conv_b": col(i[n + "conv_b"])})
    n = "L2_ffn_"
    a.update({"f2_gate": i[n + "Wg"].T, "f2_ln_scale": i[n + "ln_scale"].T, "f2_ln_bias": i[n + "ln_bias"].T,
              "f2_b1": col(i[n + "b1"].reshape(-1)), "f2_b2": i[n + "b2"],
              "f2_w_up": i[n + "W1"].transpose(1, 0, 2).reshape(C, -1), "f2_w_down": down(i[n + "W2"].reshape(-1, C)),
              "f2_spread": spread(8, 32), "f2_iota": iota(8)})
    n = "L3_ffn_"
    share = np.zeros((17, 256), f)
    share[16] = 1
    a.update({"f3_gate": np.concatenate([i[n + "Wg"], i[n + "Wsg"]]).T,
              "f3_w_gate": np.concatenate([i[n + "We_gate"].reshape(-1, C), i[n + "Ws_gate"]]).T,
              "f3_w_up": np.concatenate([i[n + "We_up"].reshape(-1, C), i[n + "Ws_up"]]).T,
              "f3_w_down": down(np.concatenate([i[n + "We_down"].transpose(0, 2, 1).reshape(-1, C), i[n + "Ws_down"].T])),
              "f3_spread": np.concatenate([np.pad(spread(16, 64), ((0, 1), (0, 0))), share], axis=1),
              "f3_iota": iota(16)})
    return {k: np.ascontiguousarray(v) for k, v in a.items()}


def kernel(**inputs):
    import numpy as np
    import concourse.bacc as bacc
    from concourse.bass_utils import run_bass_kernel_spmd

    nc = bacc.Bacc("TRN2", target_bir_lowering=False, num_devices=1)
    arrays = layout({k: np.asarray(v) for k, v in inputs.items()})
    d = {k: nc.dram_tensor(f"in_{k}", v.shape, mybir.dt.from_np(v.dtype), kind="ExternalInput").ap()
         for k, v in arrays.items()}
    out = nc.dram_tensor("out_0", (BATCH, TOK, C), F32, kind="ExternalOutput").ap()
    program(nc, d, out)
    r = run_bass_kernel_spmd(nc, [{f"in_{k}": v for k, v in arrays.items()}], core_ids=[0])
    return r.results[0]["out_0"]
```
